# Optimizing a Trainium2 kernel written in Bass

```python
import numpy as np
import jax
import jax.numpy as jnp

def _softmax(x, axis=-1):
    return jax.nn.softmax(x, axis=axis)

def _gelu(x):
    return jax.nn.gelu(x, approximate=True)

def _silu(x):
    return jax.nn.silu(x)

def _sigmoid(x):
    return jax.nn.sigmoid(x)

def _layernorm(x, axis=-1, eps=1e-05):
    m = jnp.mean(x, axis=axis, keepdims=True)
    v = jnp.var(x, axis=axis, keepdims=True)
    return (x - m) / jnp.sqrt(v + eps)

def _scatter_add(tgt, idx, src, axis=0):
    return tgt.at[idx].add(src)

def _segment_sum(src, seg, n):
    return jax.ops.segment_sum(src, seg, n)
kernel_name = 'mk_gnn_preln_d4_gnn_r8_08bdc2'

def setup_inputs(seed: int=0):
    np.random.seed(seed)
    _w = jnp.asarray

    def _rec_inputs():
        import jax
        import jax.numpy as jnp
        _gk = jax.random.key(seed)
        x = -0.000202 + 1 * jax.random.normal(jax.random.fold_in(_gk, 1), (12500, 128), jnp.float32)
        _s = jax.random.randint(jax.random.fold_in(_gk, 2), (100000,), 0, 12500, jnp.int32)
        _d = jax.random.randint(jax.random.fold_in(_gk, 3), (100000,), 0, 12500, jnp.int32)
        _loop = jnp.arange(12500, dtype=jnp.int32)
        src = jnp.concatenate([_s, _d, _loop])
        dst = jnp.concatenate([_d, _s, _loop])
        _o = jnp.argsort(dst, stable=True)
        src = src[_o]
        dst = dst[_o]
        edge_attr_16 = 0.000254156 + 0.999948 * jax.random.normal(jax.random.fold_in(_gk, 12), (212500, 16), jnp.float32)
        return (x, src, dst, edge_attr_16)
    x, src, dst, edge_attr_16 = _rec_inputs()

    def _L0_gnn_setup():
        import jax, jax.numpy as jnp
        import numpy as np
        N = 6250
        E = 200000
        F_IN = 128
        HID = 32
        HEADS = 4
        SLOPE = 0.2

        def _gat_layer(x, src, dst, W, a_src, a_dst, b, heads, out_dim):
            n = x.shape[0]
            h = (x @ W).reshape(n, heads, out_dim)
            al_s = jnp.einsum('nhd,hd->nh', h, a_src)
            al_d = jnp.einsum('nhd,hd->nh', h, a_dst)
            e = jax.nn.leaky_relu(al_s[src] + al_d[dst], SLOPE)
            m = jax.ops.segment_max(e, dst, num_segments=n)
            m = jnp.where(jnp.isfinite(m), m, 0.0)
            p = jnp.exp(e - m[dst])
            denom = jax.ops.segment_sum(p, dst, num_segments=n) + 1e-16
            w = p / denom[dst]
            msg = h[src] * w[:, :, None]
            out = jax.ops.segment_sum(msg, dst, num_segments=n)
            return out.reshape(n, heads * out_dim) + b
        key = jax.random.key(seed)
        ks = jax.random.split(key, 12)
        x = jax.random.normal(ks[0], (N, F_IN), dtype=jnp.float32)
        edge_index = jax.random.randint(ks[1], (2, E), 0, N, dtype=jnp.int64)
        s1 = 1.0 / np.sqrt(F_IN)
        s2 = 1.0 / np.sqrt(HEADS * HID)
        W1 = jax.random.normal(ks[2], (F_IN, HEADS * HID), dtype=jnp.float32) * s1
        a_src1 = jax.random.normal(ks[3], (HEADS, HID), dtype=jnp.float32) * s1
        a_dst1 = jax.random.normal(ks[4], (HEADS, HID), dtype=jnp.float32) * s1
        b1 = jnp.zeros((HEADS * HID,), dtype=jnp.float32)
        W2 = jax.random.normal(ks[5], (HEADS * HID, F_IN), dtype=jnp.float32) * s2
        a_src2 = jax.random.normal(ks[6], (1, F_IN), dtype=jnp.float32) * s2
        a_dst2 = jax.random.normal(ks[7], (1, F_IN), dtype=jnp.float32) * s2
        b2 = jnp.zeros((F_IN,), dtype=jnp.float32)
        return {'x': x, 'edge_index': edge_index, 'W1': W1, 'a_src1': a_src1, 'a_dst1': a_dst1, 'b1': b1, 'W2': W2, 'a_src2': a_src2, 'a_dst2': a_dst2, 'b2': b2}
    _L0_gnn_all = _L0_gnn_setup()
    _L0_gnn_in = {k: v for k, v in _L0_gnn_all.items() if k in ('W1', 'a_src1', 'a_dst1', 'b1', 'W2', 'a_src2', 'a_dst2', 'b2')}
    del _L0_gnn_all

    def _L1_gnn_setup():
        import jax, jax.numpy as jnp
        import numpy as np
        N = 6250
        E = 100000
        D = 128
        DE = 16
        key = jax.random.key(seed)
        ks = jax.random.split(key, 12)

        def lin(k, fan_in, fan_out):
            bound = 1.0 / np.sqrt(fan_in)
            kw, kb = jax.random.split(k)
            W = jax.random.uniform(kw, (fan_in, fan_out), jnp.float32, -bound, bound)
            b = jax.random.uniform(kb, (fan_out,), jnp.float32, -bound, bound)
            return (W, b)
        x = jax.random.normal(ks[0], (N, D), jnp.float32)
        edge_index = jax.random.randint(ks[1], (2, E), 0, N, jnp.int64)
        edge_attr = jax.random.normal(ks[2], (E, DE), jnp.float32)
        eW1, eb1 = lin(ks[3], 2 * D + DE, D)
        eW2, eb2 = lin(ks[4], D, D)
        nW1, nb1 = lin(ks[5], 2 * D, D)
        nW2, nb2 = lin(ks[6], D, D)
        return {'x': x, 'edge_index': edge_index, 'edge_attr': edge_attr, 'eW1': eW1, 'eb1': eb1, 'eW2': eW2, 'eb2': eb2, 'nW1': nW1, 'nb1': nb1, 'nW2': nW2, 'nb2': nb2}
    _L1_gnn_all = _L1_gnn_setup()
    _L1_gnn_in = {k: v for k, v in _L1_gnn_all.items() if k in ('eW1', 'eb1', 'eW2', 'eb2', 'nW1', 'nb1', 'nW2', 'nb2')}
    del _L1_gnn_all

    def _L2_gnn_setup():
        import jax, jax.numpy as jnp
        import numpy as np
        N, D, E = (6250, 128, 200000)
        BN_EPS = 1e-05
        key = jax.random.key(seed)
        ks = jax.random.split(key, 8)
        s = 1.0 / np.sqrt(D)
        return {'x': jax.random.normal(ks[0], (N, D), dtype=jnp.float32), 'edge_index': jax.random.randint(ks[1], (2, E), 0, N, dtype=jnp.int64), 'W1': jax.random.normal(ks[2], (D, D), dtype=jnp.float32) * s, 'b1': jnp.zeros((D,), jnp.float32), 'g1': jnp.ones((D,), jnp.float32), 'be1': jnp.zeros((D,), jnp.float32), 'W2': jax.random.normal(ks[3], (D, D), dtype=jnp.float32) * s, 'b2': jnp.zeros((D,), jnp.float32), 'g2': jnp.ones((D,), jnp.float32), 'be2': jnp.zeros((D,), jnp.float32), 'Wf': jax.random.normal(ks[4], (D, D), dtype=jnp.float32) * s, 'bf': jnp.zeros((D,), jnp.float32)}
    _L2_gnn_all = _L2_gnn_setup()
    _L2_gnn_in = {k: v for k, v in _L2_gnn_all.items() if k in ('W1', 'b1', 'g1', 'be1', 'W2', 'b2', 'g2', 'be2', 'Wf', 'bf')}
    del _L2_gnn_all

    def _L3_gnn_setup():
        import jax, jax.numpy as jnp
        import numpy as np
        N_NODES = 12500
        N_EDGES = 80000
        D_IN = 128
        D_OUT = 128
        EPS = 1e-05
        key = jax.random.key(seed)
        k_h, k_src, k_dst, k_ws, k_wn = jax.random.split(key, 5)
        h = jax.random.normal(k_h, (N_NODES, D_IN), dtype=jnp.float32)
        src = jax.random.randint(k_src, (N_EDGES,), 0, N_NODES, dtype=jnp.int32)
        dst = jax.random.randint(k_dst, (N_EDGES,), 0, N_NODES, dtype=jnp.int32)
        gamma = jnp.ones((D_IN,), dtype=jnp.float32)
        beta = jnp.zeros((D_IN,), dtype=jnp.float32)
        scale = 1.0 / np.sqrt(D_IN)
        W_self = jax.random.normal(k_ws, (D_IN, D_OUT), dtype=jnp.float32) * scale
        W_neigh = jax.random.normal(k_wn, (D_IN, D_OUT), dtype=jnp.float32) * scale
        b = jnp.zeros((D_OUT,), dtype=jnp.float32)
        return {'h': h, 'src': src, 'dst': dst, 'gamma': gamma, 'beta': beta, 'W_self': W_self, 'W_neigh': W_neigh, 'b': b}
    _L3_gnn_all = _L3_gnn_setup()
    _L3_gnn_in = {k: v for k, v in _L3_gnn_all.items() if k in ('gamma', 'beta', 'W_self', 'W_neigh', 'b')}
    del _L3_gnn_all
    return {'x': x, 'src': src, 'dst': dst, 'edge_attr_16': edge_attr_16, 'L0_gnn_W1': _L0_gnn_in['W1'], 'L0_gnn_a_src1': _L0_gnn_in['a_src1'], 'L0_gnn_a_dst1': _L0_gnn_in['a_dst1'], 'L0_gnn_b1': _L0_gnn_in['b1'], 'L0_gnn_W2': _L0_gnn_in['W2'], 'L0_gnn_a_src2': _L0_gnn_in['a_src2'], 'L0_gnn_a_dst2': _L0_gnn_in['a_dst2'], 'L0_gnn_b2': _L0_gnn_in['b2'], 'L1_gnn_eW1': _L1_gnn_in['eW1'], 'L1_gnn_eb1': _L1_gnn_in['eb1'], 'L1_gnn_eW2': _L1_gnn_in['eW2'], 'L1_gnn_eb2': _L1_gnn_in['eb2'], 'L1_gnn_nW1': _L1_gnn_in['nW1'], 'L1_gnn_nb1': _L1_gnn_in['nb1'], 'L1_gnn_nW2': _L1_gnn_in['nW2'], 'L1_gnn_nb2': _L1_gnn_in['nb2'], 'L2_gnn_W1': _L2_gnn_in['W1'], 'L2_gnn_b1': _L2_gnn_in['b1'], 'L2_gnn_g1': _L2_gnn_in['g1'], 'L2_gnn_be1': _L2_gnn_in['be1'], 'L2_gnn_W2': _L2_gnn_in['W2'], 'L2_gnn_b2': _L2_gnn_in['b2'], 'L2_gnn_g2': _L2_gnn_in['g2'], 'L2_gnn_be2': _L2_gnn_in['be2'], 'L2_gnn_Wf': _L2_gnn_in['Wf'], 'L2_gnn_bf': _L2_gnn_in['bf'], 'L3_gnn_gamma': _L3_gnn_in['gamma'], 'L3_gnn_beta': _L3_gnn_in['beta'], 'L3_gnn_W_self': _L3_gnn_in['W_self'], 'L3_gnn_W_neigh': _L3_gnn_in['W_neigh'], 'L3_gnn_b': _L3_gnn_in['b']}

def reference(x, src, dst, edge_attr_16, L0_gnn_W1, L0_gnn_a_src1, L0_gnn_a_dst1, L0_gnn_b1, L0_gnn_W2, L0_gnn_a_src2, L0_gnn_a_dst2, L0_gnn_b2, L1_gnn_eW1, L1_gnn_eb1, L1_gnn_eW2, L1_gnn_eb2, L1_gnn_nW1, L1_gnn_nb1, L1_gnn_nW2, L1_gnn_nb2, L2_gnn_W1, L2_gnn_b1, L2_gnn_g1, L2_gnn_be1, L2_gnn_W2, L2_gnn_b2, L2_gnn_g2, L2_gnn_be2, L2_gnn_Wf, L2_gnn_bf, L3_gnn_gamma, L3_gnn_beta, L3_gnn_W_self, L3_gnn_W_neigh, L3_gnn_b):
    import jax
    import jax.numpy as jnp

    def _L0_gnn_ref(x, edge_index, W1, a_src1, a_dst1, b1, W2, a_src2, a_dst2, b2):
        import jax, jax.numpy as jnp
        import numpy as np
        N = 6250
        E = 200000
        F_IN = 128
        HID = 32
        HEADS = 4
        SLOPE = 0.2

        def _gat_layer(x, src, dst, W, a_src, a_dst, b, heads, out_dim):
            n = x.shape[0]
            h = (x @ W).reshape(n, heads, out_dim)
            al_s = jnp.einsum('nhd,hd->nh', h, a_src)
            al_d = jnp.einsum('nhd,hd->nh', h, a_dst)
            e = jax.nn.leaky_relu(al_s[src] + al_d[dst], SLOPE)
            m = jax.ops.segment_max(e, dst, num_segments=n)
            m = jnp.where(jnp.isfinite(m), m, 0.0)
            p = jnp.exp(e - m[dst])
            denom = jax.ops.segment_sum(p, dst, num_segments=n) + 1e-16
            w = p / denom[dst]
            msg = h[src] * w[:, :, None]
            out = jax.ops.segment_sum(msg, dst, num_segments=n)
            return out.reshape(n, heads * out_dim) + b
        src = edge_index[0]
        dst = edge_index[1]
        h = _gat_layer(x, src, dst, W1, a_src1, a_dst1, b1, HEADS, HID)
        h = jax.nn.relu(h)
        out = _gat_layer(h, src, dst, W2, a_src2, a_dst2, b2, 1, F_IN)
        return jax.nn.log_softmax(out, axis=-1)

    def _L1_gnn_ref(x, edge_index, edge_attr, eW1, eb1, eW2, eb2, nW1, nb1, nW2, nb2):
        import jax, jax.numpy as jnp
        import numpy as np
        N = 6250
        E = 100000
        D = 128
        DE = 16
        row, col = (edge_index[0], edge_index[1])
        edge_input = jnp.concatenate([x[row], x[col], edge_attr], axis=-1)
        h = jax.nn.silu(edge_input @ eW1 + eb1)
        m_ij = jax.nn.silu(h @ eW2 + eb2)
        agg = jax.ops.segment_sum(m_ij, row, num_segments=x.shape[0])
        node_input = jnp.concatenate([x, agg], axis=-1)
        update = jax.nn.silu(node_input @ nW1 + nb1) @ nW2 + nb2
        return x + update

    def _L2_gnn_ref(x, edge_index, W1, b1, g1, be1, W2, b2, g2, be2, Wf, bf):
        import jax, jax.numpy as jnp
        import numpy as np
        N, D, E = (6250, 128, 200000)
        BN_EPS = 1e-05
        n = x.shape[0]
        loops = jnp.arange(n, dtype=edge_index.dtype)
        src = jnp.concatenate([edge_index[0], loops])
        dst = jnp.concatenate([edge_index[1], loops])
        deg = jax.ops.segment_sum(jnp.ones(src.shape[0], x.dtype), dst, num_segments=n)
        dinv = jnp.where(deg > 0, jax.lax.rsqrt(deg), 0.0)
        norm = dinv[src] * dinv[dst]

        def conv(h, W, b):
            h = h @ W
            agg = jax.ops.segment_sum(h[src] * norm[:, None], dst, num_segments=n)
            return agg + b

        def bn(h, g, be):
            mu = h.mean(0)
            var = h.var(0)
            return (h - mu) * jax.lax.rsqrt(var + BN_EPS) * g + be
        h = jax.nn.relu(bn(conv(x, W1, b1), g1, be1))
        h = jax.nn.relu(bn(conv(h, W2, b2), g2, be2))
        return h @ Wf + bf

    def _L3_gnn_ref(h, src, dst, gamma, beta, W_self, W_neigh, b):
        import jax, jax.numpy as jnp
        import numpy as np
        N_NODES = 12500
        N_EDGES = 80000
        D_IN = 128
        D_OUT = 128
        EPS = 1e-05
        mu = jnp.mean(h, axis=-1, keepdims=True)
        var = jnp.mean(jnp.square(h - mu), axis=-1, keepdims=True)
        hn = (h - mu) * jax.lax.rsqrt(var + EPS) * gamma + beta
        n = h.shape[0]
        msg_sum = jax.ops.segment_sum(hn[src], dst, num_segments=n)
        deg = jax.ops.segment_sum(jnp.ones_like(dst, dtype=hn.dtype), dst, num_segments=n)
        h_neigh = msg_sum / jnp.maximum(deg, 1.0)[:, None]
        out = hn @ W_self + h_neigh @ W_neigh + b
        return out
    edge_index = jnp.stack([src, dst])
    h = jnp.maximum(_layernorm(x, axis=-1), 0.0)
    x = x + _L0_gnn_ref(h, edge_index, L0_gnn_W1, L0_gnn_a_src1, L0_gnn_a_dst1, L0_gnn_b1, L0_gnn_W2, L0_gnn_a_src2, L0_gnn_a_dst2, L0_gnn_b2)
    h = jnp.maximum(_layernorm(x, axis=-1), 0.0)
    x = x + _L1_gnn_ref(h, edge_index, edge_attr_16, L1_gnn_eW1, L1_gnn_eb1, L1_gnn_eW2, L1_gnn_eb2, L1_gnn_nW1, L1_gnn_nb1, L1_gnn_nW2, L1_gnn_nb2)
    h = jnp.maximum(_layernorm(x, axis=-1), 0.0)
    x = x + _L2_gnn_ref(h, edge_index, L2_gnn_W1, L2_gnn_b1, L2_gnn_g1, L2_gnn_be1, L2_gnn_W2, L2_gnn_b2, L2_gnn_g2, L2_gnn_be2, L2_gnn_Wf, L2_gnn_bf)
    h = jnp.maximum(_layernorm(x, axis=-1), 0.0)
    x = x + _L3_gnn_ref(h, src, dst, L3_gnn_gamma, L3_gnn_beta, L3_gnn_W_self, L3_gnn_W_neigh, L3_gnn_b)
    return x

_drawn_inputs = setup_inputs


def setup_inputs(seed=0):
    import zlib

    import numpy as np

    out = dict(_drawn_inputs(seed))
    spreads = {'L0_gnn_b1': (0.0, 0.323),
     'L0_gnn_b2': (0.0, 0.1),
     'L2_gnn_b1': (0.0, 2.0),
     'L2_gnn_g1': (1.0, 0.2),
     'L2_gnn_be1': (0.0, 0.513),
     'L2_gnn_b2': (0.0, 2.0),
     'L2_gnn_g2': (1.0, 0.2),
     'L2_gnn_be2': (0.0, 0.467),
     'L2_gnn_bf': (0.0, 0.338),
     'L3_gnn_gamma': (1.0, 0.2),
     'L3_gnn_beta': (0.0, 0.326),
     'L3_gnn_b': (0.0, 0.409)}
    factors = {'edge_attr_16': 8.0,
     'L0_gnn_a_src1': 6.097,
     'L0_gnn_a_dst1': 43.589,
     'L0_gnn_a_src2': 8.0,
     'L0_gnn_a_dst2': 64.0,
     'L1_gnn_eb1': 8.0,
     'L1_gnn_eb2': 3.931,
     'L1_gnn_nb1': 8.0,
     'L1_gnn_nb2': 4.641}
    for name, (base, spread) in spreads.items():
        noise = np.random.default_rng([zlib.crc32(name.encode()), seed]).standard_normal(out[name].shape)
        drawn = base * np.exp(spread * noise) if base else spread * noise
        out[name] = jnp.asarray(drawn.astype(out[name].dtype))
    for name, factor in factors.items():
        out[name] = (out[name] * factor).astype(out[name].dtype)
    return out
```

```python
from contextlib import ExitStack

import concourse.bass as bass
from concourse import mybir

F32 = mybir.dt.float32
I32 = mybir.dt.int32
ALU = mybir.AluOpType
ACT = mybir.ActivationFunctionType
AX_X = mybir.AxisListType.X

P = 128
N = 12500
E = 212500
D = 128
NT = (N + P - 1) // P
NP = NT * P
WIN = NP + P
ROW = 1664
G = ROW // P
K = G * P
EP = K * P
LAST = E - (P - 1) * ROW
GRP = 7
GW = GRP * P
NG = NT // GRP
HALF = 8
EI = K // (2 * HALF)
HEADS = 4
HID = 32
SLOPE = 0.2
BIG = 1e30
EPS = 1e-5
LEAD = 16
AGG = 4


class Signal:

    def __init__(self, sem, at):
        self.sem, self.at = sem, at

    def after(self, n):
        return n + self.at

    def passed(self, n):
        self.at += n


def build(nc, t, out, stop=99):
    ctx = ExitStack()
    with ctx:
        ctx.enter_context(nc.allow_non_contiguous_dma(reason="columns of one element a row, all short"))
        def sb(name, shape, dt=F32):
            return ctx.enter_context(nc.sbuf_tensor(name, shape, dt))

        signals = []

        def sig(name, lead=LEAD):
            signals.append(Signal(ctx.enter_context(nc.semaphore(name)), lead))
            return signals[-1]

        def dram(name, shape, dt=F32):
            return nc.dram_tensor(name, shape, dt, kind="Internal").ap()

        tab = dram("tab", (NP, D))
        tab_b = dram("tab_b", (WIN, D))
        tab_al = dram("tab_al", (NP, HEADS))
        tab_al1 = dram("tab_al1", (NP, 1))
        ald_rows = dram("ald_rows", (NP, HEADS))
        ald_rows1 = dram("ald_rows1", (NP, 1))
        ex4 = dram("ex4", (EP, HEADS))
        ex1 = dram("ex1", (EP, 1))
        src_d = dram("src_d", (K, P), I32)
        dst_d = dram("dst_d", (K, P), I32)
        attr_d = dram("attr_d", (EP, 16))
        agg = [dram(f"agg{a}", (WIN, D)) for a in range(AGG)]
        eb_i_d = dram("eb_i_d", (G, P), I32)
        eb_f_d = dram("eb_f_d", (G, P))
        start_d = dram("start_d", (NP + P,))
        dinv_d = dram("dinv_d", (NP,))
        same_d = dram("same_d", (P, ROW))

        xs = sb("xs", [P, NP])
        hs = sb("hs", [P, NP])
        F = sb("F", [P, WIN])
        srcT = sb("srcT", [P, K], I32)
        locT = sb("locT", [P, K])
        ebi = sb("ebi", [1, K], I32)
        wk = sb("wk", [P, 6 * GW])
        wts = sb("wts", [P, 7 * P])
        ident = sb("ident", [P, P])
        iota_row = sb("iota_row", [P, P])
        lower = sb("lower", [P, P])
        pcol = sb("pcol", [P, 1])
        link_next = sb("link_next", [P, 1])
        ones = sb("ones", [1, P])
        brow = sb("brow", [1, 2 * P])
        bcol = sb("bcol", [P, 8])
        idx = sb("idx", [P, 2 * HALF], I32)
        start_i = sb("start_i", [P, NT], I32)
        ald = sb("ald", [P, NT * HEADS])
        dinv = sb("dinv", [P, NT])
        rdeg = sb("rdeg", [P, NT])
        st6 = sb("st6", [P, 5 * P])
        rstd = sb("rstd", [P, NT])
        nmr = sb("nmr", [P, NT])
        sm = sb("sm", [P, 4 * NT])
        PS = ctx.enter_context(nc.psum_tensor("PS", [P, 8 * 512], F32))

        def bank(b, w=512):
            return PS[:, b * 512:b * 512 + w]

        def hslot(n):
            return hs[:, n * ROW:(n + 1) * ROW]

        def fslot(n):
            return F[:, n * ROW:(n + 1) * ROW]

        row = lambda ap: ap.rearrange("(a n) -> a n", a=1)
        colv = lambda ap: ap.rearrange("(n a) -> n a", a=1)
        gathered = [sig(f"gathered{j}", 0) for j in range(2 * HALF)]
        idx_ready = sig("idx_ready")
        onehot_ready = sig("onehot_ready")
        scaled = sig("scaled")
        summed = sig("summed")
        added = sig("added")
        chain = sig("chain")
        achain = sig("achain")
        loads = sig("loads")
        loads2 = sig("loads2")
        stores = sig("stores")
        pe_a = sig("pe_a")
        pe_b = sig("pe_b")
        pe_c = sig("pe_c")
        act_a = sig("act_a")
        act_b = sig("act_b")
        act_c = sig("act_c")
        dve_a = sig("dve_a")
        dve_b = sig("dve_b")
        dve_c = sig("dve_c")
        pool_a = sig("pool_a")
        pe_t, pe_z, pe_m, pe_d = (sig(n) for n in ("pe_t", "pe_z", "pe_m", "pe_d"))
        ohT_ready, h1_ready, msg_ready, msum_ready, sidx_ready, picked_rows, q_made, dups_made = (
            sig(n) for n in ("ohT_ready", "h1_ready", "msg_ready", "msum_ready", "sidx_ready", "picked_rows", "q_made",
                             "dups_made"))
        scattered = [sig(f"scattered{a}", 0) for a in range(AGG)]
        idx_taken = sig("idx_taken")
        spread = sig("spread", 0)
        picked = sig("picked", 0)
        half_in = [sig(f"half_in{b}", 0) for b in range(2)]
        half_out = [sig(f"half_out{b}") for b in range(2)]
        more_in = [sig(f"more_in{b}") for b in range(4)]

        def linker(eng, s=chain):
            def link(ins):
                s.at += 1
                ins.then_inc(s.sem, 1)
                eng.wait_ge(s.sem, s.at)
            return link

        with nc.Block() as block:
            @block.sync
            def _(sp):
                for s in signals:
                    if s.at:
                        sp.sem_inc(s.sem, LEAD)

        dstI, srcI = hslot(0).bitcast(I32), hslot(1).bitcast(I32)
        dstF, srcF, locF = hslot(2), hslot(3), hslot(4)
        ebB, junk = hslot(5), hslot(6)
        same = hslot(6)
        prevI = idx[:, 0:1]
        flat = lambda a: a.rearrange("(p j) -> p j", p=1)
        with nc.Block() as block:
            @block.gpsimd
            def _(pool):
                nc.gpsimd.iota(st6[:, 0:P].bitcast(I32), pattern=[[1, P]], base=0, channel_multiplier=0).then_inc(pool_a.sem, 1)
                nc.gpsimd.iota(sm[:, 0:NT].bitcast(I32), pattern=[[P, NT]], base=0, channel_multiplier=1).then_inc(pool_a.sem, 1)

            @block.scalar
            def _(act):
                act.dma_start(attr_d[0:E, :].rearrange("(a b) d -> a (b d)", a=100),
                              t["edge_attr_16"].rearrange("(a b) d -> a (b d)", a=100)).then_inc(stores.sem, 16)
                act.wait_ge(dve_a.sem, dve_a.after(1))
                act.dma_start(attr_d[E:EP, :].rearrange("(a b) d -> a (b d)", a=4),
                              F[0:4, 0:(EP - E) * 4]).then_inc(stores.sem, 16)
                act.dma_start(ex4.rearrange("(p j) h -> p (j h)", p=P), F[:, 0:ROW * HEADS]).then_inc(stores.sem, 16)
                act.dma_start(ex1.rearrange("(p j) h -> p (j h)", p=P), F[:, 0:ROW]).then_inc(stores.sem, 16)
                for a in range(AGG):
                    act.dma_start(agg[a].rearrange("(p i) d -> p (i d)", p=P), F[:, 0:WIN]).then_inc(stores.sem, 16)
                act.dma_start(tab_b[NP:WIN, :], F[:, 0:D]).then_inc(stores.sem, 16)
                act.wait_ge(stores.sem, stores.after(16 * (6 + AGG)))

            @block.sync
            def _(sp):
                sp.wait_ge(dve_b.sem, dve_b.after(4))
                srcf, dstf = t["src"], t["dst"]
                for buf, ap in ((dstI, dstf), (srcI, srcf)):
                    sp.dma_start(buf[0:127, :], ap[0:127 * ROW].rearrange("(p j) -> p j", p=127)).then_inc(loads.sem, 16)
                    sp.dma_start(buf[127:128, 0:LAST], flat(ap[127 * ROW:E])).then_inc(loads.sem, 16)
                sp.dma_start(prevI[1:P, :], dstf[0:127 * ROW].rearrange("(p j) -> p j", j=ROW)[:, ROW - 1:ROW]).then_inc(loads.sem, 16)
                sp.dma_start(xs[:, 0:(NT - 1) * D].rearrange("p (i f) -> p i f", f=D),
                             t["x"][0:(NT - 1) * P, :].rearrange("(i p) f -> p i f", p=P)).then_inc(loads.sem, 16)
                sp.dma_start(xs[0:N - (NT - 1) * P, (NT - 1) * D:NT * D], t["x"][(NT - 1) * P:N, :]).then_inc(loads.sem, 16)
                sp.dma_start(idx[0:P - 1, 1:2], dstf[LAST:E].rearrange("(p j) -> p j", j=ROW)[:, ROW - LAST:ROW - LAST + 1]).then_inc(loads.sem, 16)
                sp.wait_ge(loads.sem, loads.after(16 * 8))
                sp.dma_start(src_d.rearrange("(p g) c -> p (g c)", p=P), srcI).then_inc(loads.sem, 16)
                sp.dma_start(dst_d.rearrange("(p g) c -> p (g c)", p=P), dstI).then_inc(loads.sem, 16)
                sp.wait_ge(loads.sem, loads.after(16 * 10))
                sp.wait_ge(dve_c.sem, dve_c.after(2))
                sp.dma_start(same_d, same).then_inc(stores.sem, 16)
                sp.dma_start(eb_i_d, st6[0:G, 4 * P:5 * P].bitcast(I32)).then_inc(loads2.sem, 16)
                sp.dma_start(eb_f_d, st6[0:G, 3 * P:4 * P]).then_inc(loads2.sem, 16)
                sp.wait_ge(loads2.sem, loads2.after(32))
                sp.dma_start(ebi[0:1, :], eb_i_d.rearrange("(a g) p -> a (g p)", a=1)).then_inc(loads2.sem, 16)
                sp.dma_start(ebB, eb_f_d.rearrange("(a g) p -> a (g p)", a=1).broadcast_to([P, K])).then_inc(loads2.sem, 16)
                sp.wait_ge(loads2.sem, loads2.after(64))

            @block.vector
            def _(v):
                link = linker(v)
                v.memset(F[:, :], 0.0).then_inc(dve_a.sem, 1)
                v.memset(dstI[96:128, LAST:], N).then_inc(dve_b.sem, 1)
                v.memset(srcI[96:128, LAST:], N).then_inc(dve_b.sem, 1)
                v.memset(idx[:, 0:2], -1).then_inc(dve_b.sem, 1)
                v.memset(xs[:, (NT - 1) * D:], 0.0).then_inc(dve_b.sem, 1)
                v.memset(ones[:, :], 1.0)
                v.wait_ge(pool_a.sem, pool_a.after(2))
                v.tensor_copy(iota_row[:, :], st6[:, 0:P].bitcast(I32))
                link(v.tensor_copy(sm[:, NT:2 * NT], sm[:, 0:NT].bitcast(I32)))
                link(v.tensor_copy(pcol[:, :], sm[:, NT:NT + 1]))
                v.tensor_scalar(lower[:, :], iota_row[:, :], pcol[:, 0:1], None, ALU.is_lt)
                link(v.tensor_scalar(ident[:, :], iota_row[:, :], pcol[:, 0:1], None, ALU.is_equal))
                v.wait_ge(loads.sem, loads.after(16 * 8))
                v.tensor_copy(srcF, srcI)
                v.tensor_copy(st6[:, 2 * P:2 * P + 2], idx[:, 0:2])
                link(v.tensor_copy(dstF, dstI))
                v.tensor_tensor(link_next[:, :], dstF[:, ROW - 1:ROW], st6[:, 2 * P + 1:2 * P + 2], ALU.is_equal)
                v.tensor_tensor(same[:, 1:], dstF[:, 1:], dstF[:, :-1], ALU.is_equal)
                v.tensor_tensor(same[:, 0:1], dstF[:, 0:1], st6[:, 2 * P:2 * P + 1], ALU.is_equal)
                first = dstF.rearrange("p (g c) -> p g c", c=P)[:, :, 0:1]
                v.tensor_tensor(locF.rearrange("p (g c) -> p g c", c=P), dstF.rearrange("p (g c) -> p g c", c=P),
                                first.broadcast_to([P, G, P]), ALU.subtract)
                link(v.tensor_copy(st6[:, P:P + G], first.rearrange("p g c -> p (g c)")))
                v.nop().then_inc(dve_c.sem, 1)
                v.wait_ge(pe_a.sem, pe_a.after(1))
                v.tensor_copy(st6[0:G, 4 * P:5 * P].bitcast(I32), PS[0:G, 0:P])
                link(v.tensor_copy(st6[0:G, 3 * P:4 * P], PS[0:G, 0:P]))
                v.nop().then_inc(dve_c.sem, 1)
                for g in range(G):
                    b = 1 + g % 3
                    v.wait_ge(pe_b.sem, pe_b.after(g + 1))
                    v.tensor_copy(locT[:, g * P:(g + 1) * P], PS[:, b * 1024:b * 1024 + P])
                    link(v.tensor_copy(srcT[:, g * P:(g + 1) * P], PS[:, b * 1024 + 512:b * 1024 + 512 + P]))
                    v.nop().then_inc(dve_b.sem, 1)

            @block.tensor
            def _(pe):
                pe.wait_ge(dve_c.sem, dve_c.after(1))
                pe.transpose(PS[0:G, 0:P], st6[:, P:P + G], ident[:, :]).then_inc(pe_a.sem, 1)
                for g in range(G):
                    b = 1 + g % 3
                    if g >= 3:
                        pe.wait_ge(dve_b.sem, dve_b.after(4 + g - 2))
                    pe.transpose(PS[:, b * 1024:b * 1024 + P], locF[:, g * P:(g + 1) * P], ident[:, :])
                    pe.transpose(PS[:, b * 1024 + 512:b * 1024 + 512 + P], srcF[:, g * P:(g + 1) * P], ident[:, :]).then_inc(pe_b.sem, 1)
        pool_a.passed(2); dve_a.passed(1); dve_b.passed(4 + G); dve_c.passed(2); pe_a.passed(1); pe_b.passed(G)
        loads.passed(16 * 10); loads2.passed(64); stores.passed(16 * (6 + AGG))
        if stop <= 0: return

        nodeid = sm[:, NT:2 * NT]
        cnt, cnt2 = sm[:, 2 * NT:3 * NT], sm[:, 3 * NT:4 * NT]
        tix = ald[:, 0:NT].bitcast(I32)
        rows = F[:, 0:2 * GRP * P].bitcast(I32)
        ji = junk
        with nc.Block() as block:
            @block.vector
            def _(v):
                link = linker(v)
                with v.Fori(0, NG) as i:
                    for j in range(GRP):
                        c = i * GRP + j
                        v.tensor_scalar(junk, ebB, nodeid[:, bass.ds(c, 1)], 0.0, ALU.is_lt, ALU.add,
                                        accum_out=cnt[:, bass.ds(c, 1)]).then_inc(dve_a.sem, 1)
                        v.wait_ge(dve_a.sem, dve_a.after(c + 1))
                link(v.tensor_scalar(cnt, cnt, -1.0, 0.0, ALU.add, ALU.max))
                link(v.tensor_copy(tix, cnt))
                with v.Fori(0, NG // 2) as i:
                    for b in range(2):
                        q = i * 2 + b
                        v.wait_ge(half_in[b].sem, half_in[b].after(i * (16 * GRP)))
                        v.tensor_copy(idx[:, b * HALF:b * HALF + GRP], tix[:, bass.ds(q * GRP, GRP)]).then_inc(idx_ready.sem, 1)
                    for b in range(2):
                        q = i * 2 + b
                        v.wait_ge(half_in[b].sem, half_in[b].after((i + 1) * (16 * GRP)))
                        for j in range(GRP):
                            c = q * GRP + j
                            v.tensor_scalar(junk[:, 0:P], rows[:, (b * GRP + j) * P:(b * GRP + j + 1) * P],
                                            nodeid[:, bass.ds(c, 1)], 0.0, ALU.is_lt, ALU.add,
                                            accum_out=cnt2[:, bass.ds(c, 1)]).then_inc(dve_b.sem, 1)
                            v.wait_ge(dve_b.sem, dve_b.after(c + 1))
                link(v.scalar_tensor_tensor(cnt2, cnt, float(P), cnt2, ALU.mult, ALU.add))
                v.memset(wk[:, 0:P], 0.0)
                link(v.tensor_copy(start_i[:, :], cnt2))
                v.nop().then_inc(dve_c.sem, 1)
                v.wait_ge(pe_a.sem, pe_a.after(1))
                startT = wk[0:NT, P:2 * P]
                link(v.tensor_copy(startT, PS[0:NT, 0:P]))
                v.nop().then_inc(dve_c.sem, 1)
                v.wait_ge(loads2.sem, loads2.after(16))
                degT = wk[0:NT, 3 * P:4 * P]
                link(v.tensor_tensor(degT, wk[0:NT, 2 * P:3 * P], startT, ALU.subtract))
                link(v.tensor_scalar(wk[0:NT, 4 * P:5 * P], degT, 0.0, 1.0, ALU.max, ALU.add))
                link(v.tensor_scalar(degT, degT, 1.0, None, ALU.max))
                v.nop().then_inc(dve_c.sem, 1)
                v.wait_ge(act_a.sem, act_a.after(1))
                v.reciprocal(wk[0:NT, 5 * P:6 * P], wk[0:NT, 4 * P:5 * P])
                link(v.reciprocal(degT, degT))
                v.nop().then_inc(dve_c.sem, 1)
                v.wait_ge(pe_a.sem, pe_a.after(2))
                v.tensor_copy(dinv[:, :], PS[:, 1024:1024 + NT])
                v.tensor_copy(rdeg[:, :], PS[:, 2048:2048 + NT])

            @block.scalar
            def _(act):
                act.wait_ge(dve_c.sem, dve_c.after(3))
                act.activation(wk[0:NT, 4 * P:5 * P], wk[0:NT, 4 * P:5 * P], ACT.Sqrt).then_inc(act_a.sem, 1)

            @block.tensor
            def _(pe):
                pe.wait_ge(dve_c.sem, dve_c.after(1))
                pe.transpose(PS[0:NT, 0:P], cnt2, ident[:, :]).then_inc(pe_a.sem, 1)
                pe.wait_ge(dve_c.sem, dve_c.after(4))
                pe.transpose(PS[:, 1024:1024 + NT], wk[0:NT, 5 * P:6 * P], ident[0:NT, 0:NT])
                pe.transpose(PS[:, 2048:2048 + NT], wk[0:NT, 3 * P:4 * P], ident[0:NT, 0:NT]).then_inc(pe_a.sem, 1)

            @block.sync
            def _(sp):
                sp.wait_ge(dve_c.sem, dve_c.after(2))
                sp.dma_start(start_d[0:NP].rearrange("(i p) -> i p", p=P), wk[0:NT, P:2 * P]).then_inc(loads.sem, 16)
                sp.dma_start(flat(start_d[NP:NP + P]), wk[0:1, 0:P]).then_inc(loads.sem, 16)
                sp.wait_ge(loads.sem, loads.after(32))
                sp.dma_start(wk[0:NT, 2 * P:3 * P], start_d[1:NP + 1].rearrange("(i p) -> i p", p=P)).then_inc(loads2.sem, 16)
                sp.wait_ge(dve_c.sem, dve_c.after(4))
                sp.dma_start(dinv_d.rearrange("(i p) -> i p", p=P), wk[0:NT, 5 * P:6 * P]).then_inc(stores.sem, 16)
                sp.wait_ge(stores.sem, stores.after(16))

            @block.gpsimd
            def _(pool):
                with pool.Fori(0, NG // 2) as i:
                    for b in range(2):
                        pool.wait_ge(idx_ready.sem, idx_ready.after(i * 2 + b + 1))
                        pool.wait_ge(dve_b.sem, dve_b.after(i * (2 * GRP)))
                        pool.sem_inc(idx_taken.sem, 1)
                        for j in range(GRP):
                            pool.indirect_dma_start(rows[:, (b * GRP + j) * P:(b * GRP + j + 1) * P], None, dst_d,
                                                    bass.IndirectOffsetOnAxis(idx[:, b * HALF + j:b * HALF + j + 1], 0))\
                                .then_inc(half_in[b].sem, 16)
        dve_a.passed(NT); dve_b.passed(NT); dve_c.passed(4); act_a.passed(1); pe_a.passed(2)
        idx_ready.passed(NG); loads.passed(32); loads2.passed(16); stores.passed(16)
        for s in half_in: s.passed(16 * GRP * (NG // 2))
        if stop <= 1: return

        def layer_norm(src, dst, func):
            st = st6[:, 0:NT * 6].rearrange("p (i s) -> p i s", s=6)
            col = lambda n: st[:, :, n:n + 1].rearrange("p i s -> p (i s)")
            a, b = sm[:, 0:NT], sm[:, 2 * NT:3 * NT]
            with nc.Block() as block:
                @block.vector
                def _(v):
                    link = linker(v)
                    with v.Fori(0, NG) as i:
                        for j in range(GRP):
                            c = i * GRP + j
                            v.bn_stats(st6[:, bass.ds(c * 6, 6)], src[:, bass.ds(c * D, D)]).then_inc(dve_a.sem, 1)
                    v.wait_ge(dve_a.sem, dve_a.after(NT))
                    v.tensor_tensor(a, col(1), col(4), ALU.add)
                    v.tensor_tensor(b, col(1), col(4), ALU.subtract)
                    link(v.tensor_tensor(rstd[:, :], col(2), col(5), ALU.add))
                    link(v.tensor_tensor(b, b, b, ALU.mult))
                    link(v.tensor_scalar(rstd[:, :], rstd[:, :], 1.0 / D, EPS, ALU.mult, ALU.add))
                    link(v.scalar_tensor_tensor(rstd[:, :], b, 0.25, rstd[:, :], ALU.mult, ALU.add))
                    v.nop().then_inc(dve_b.sem, 1)
                    v.wait_ge(act_a.sem, act_a.after(1))
                    link(v.reciprocal(rstd[:, :], rstd[:, :]))
                    link(v.scalar_tensor_tensor(nmr[:, :], a, -0.5, rstd[:, :], ALU.mult, ALU.mult))
                    v.nop().then_inc(dve_b.sem, 1)

                @block.scalar
                def _(act):
                    act.wait_ge(dve_b.sem, dve_b.after(1))
                    act.activation(rstd[:, :], rstd[:, :], ACT.Sqrt).then_inc(act_a.sem, 1)
                    act.wait_ge(dve_b.sem, dve_b.after(2))
                    with act.Fori(0, NG) as i:
                        for j in range(GRP):
                            c = i * GRP + j
                            act.activation(dst[:, bass.ds(c * D, D)], src[:, bass.ds(c * D, D)], func,
                                           bias=nmr[:, bass.ds(c, 1)], scale=rstd[:, bass.ds(c, 1)])
            dve_a.passed(NT); dve_b.passed(2); act_a.passed(1)

        hT = [wk[:, b * GW:(b + 1) * GW] for b in range(2)]
        ost = [wk[:, (2 + b) * GW:(3 + b) * GW] for b in range(2)]
        psA = [PS[:, b * 2048:b * 2048 + GW] for b in range(2)]
        psB = [PS[:, b * 2048 + 1024:b * 2048 + 1024 + GW] for b in range(2)]
        W = [wts[:, n * P:(n + 1) * P] for n in range(7)]

        group = lambda a: a.rearrange("p (i f) -> p i f", f=P)

        def tile_of(buf, j, w=P):
            return buf[:, j * w:(j + 1) * w]

        def rows_of(table, q):
            return table[bass.ds(q * GW, GW), :].rearrange("(i p) f -> p i f", p=P)

        def project(weight, table, from_f=False, bias=None, scale=False, init_f=False, al=None, heads=0,
                    al_table=None, ald_table=None):
            with nc.Block() as block:
                @block.tensor
                def _(pe):
                    with pe.Fori(0, NG // 2) as i:
                        for b in range(2):
                            q = i * 2 + b
                            if not from_f:
                                pe.wait_ge(pool_a.sem, pool_a.after(q + 1))
                                pe.wait_ge(act_a.sem, act_a.after(q - 1))
                                if init_f:
                                    pe.wait_ge(dve_c.sem, dve_c.after(q - 1))
                                if al is not None:
                                    pe.wait_ge(dve_b.sem, dve_b.after(q - 1))
                                for j in range(GRP):
                                    last = pe.transpose(tile_of(psA[b], j), tile_of(stage, j), ident[:, :])
                                last.then_inc(pe_a.sem, 1)
                            pe.wait_ge(act_a.sem, act_a.after(q + 1))
                            pe.wait_ge(dve_a.sem, dve_a.after(q - 1))
                            for j in range(GRP):
                                last = pe.matmul(tile_of(psB[b], j), tile_of(hT[b], j), weight, start=True, stop=bias is None)
                                if bias is not None:
                                    last = pe.matmul(tile_of(psB[b], j), ones[:, :], bias, start=False, stop=True)
                            last.then_inc(pe_b.sem, 1)
                            if al is not None:
                                pe.wait_ge(dve_b.sem, dve_b.after(q - 1))
                                for j in range(GRP):
                                    c = b * 2048 + j * 2 * heads
                                    last = pe.matmul(PS[:, c:c + 2 * heads], tile_of(hT[b], j), al, start=True, stop=True)
                                last.then_inc(pe_c.sem, 1)
                            if init_f:
                                pe.wait_ge(dve_c.sem, dve_c.after(q - 1))
                                for a, z in ((0, 512), (512, GW)):
                                    last = pe.matmul(psA[b][:, a:z], weight, hT[b][:, a:z], start=True, stop=True)
                                last.then_inc(pe_c.sem, 1)

                @block.gpsimd
                def _(pool):
                    with pool.Fori(0, NG // 2) as i:
                        for b in range(2):
                            q = i * 2 + b
                            if from_f:
                                pool.wait_ge(pe_b.sem, pe_b.after(q - 1))
                                if init_f or al is not None:
                                    pool.wait_ge(pe_c.sem, pe_c.after(q - 1))
                                pool.tensor_copy(hT[b], F[:, bass.ds(q * GW, GW)]).then_inc(act_a.sem, 1)
                            else:
                                pool.wait_ge(pe_a.sem, pe_a.after(q))
                                pool.tensor_copy(stage, hs[:, bass.ds(q * GW, GW)]).then_inc(pool_a.sem, 1)

                @block.scalar
                def _(act):
                    if not from_f:
                        with act.Fori(0, NG // 2) as i:
                            for b in range(2):
                                q = i * 2 + b
                                act.wait_ge(pe_a.sem, pe_a.after(q + 1))
                                act.wait_ge(pe_b.sem, pe_b.after(q - 1))
                                if init_f or al is not None:
                                    act.wait_ge(pe_c.sem, pe_c.after(q - 1))
                                act.copy(hT[b], psA[b]).then_inc(act_a.sem, 1)

                @block.vector
                def _(v):
                    with v.Fori(0, NG // 2) as i:
                        for b in range(2):
                            q = i * 2 + b
                            v.wait_ge(pe_b.sem, pe_b.after(q + 1))
                            v.wait_ge(half_out[b].sem, half_out[b].after(i * 16))
                            if scale:
                                d = dinv[:, bass.ds(q * GRP, GRP)].unsqueeze(2).broadcast_to([P, GRP, P])
                                v.tensor_tensor(group(ost[b]), group(psB[b]), d, ALU.mult).then_inc(dve_a.sem, 1)
                            else:
                                v.tensor_copy(ost[b], psB[b]).then_inc(dve_a.sem, 1)
                            if al is not None:
                                v.wait_ge(pe_c.sem, pe_c.after(q + 1))
                                both = PS[:, b * 2048:b * 2048 + GRP * 2 * heads].rearrange("p (i h) -> p i h", h=2 * heads)
                                cols = bass.ds(q * GRP * heads, GRP * heads)
                                v.tensor_copy(als[:, cols].rearrange("p (i h) -> p i h", h=heads), both[:, :, 0:heads])
                                v.tensor_copy(ald[:, cols].rearrange("p (i h) -> p i h", h=heads), both[:, :, heads:])\
                                    .then_inc(dve_b.sem, 1)
                            if init_f:
                                v.wait_ge(pe_c.sem, pe_c.after(q + 1))
                                v.wait_ge(more_in[0].sem, more_in[0].after((q + 1) * 16))
                                v.tensor_tensor(F[:, bass.ds(q * GW, GW)], psA[b], dB, ALU.mult).then_inc(dve_c.sem, 1)

                @block.sync
                def _(sp):
                    with sp.Fori(0, NG // 2) as i:
                        for b in range(2):
                            q = i * 2 + b
                            if init_f:
                                sp.wait_ge(dve_c.sem, dve_c.after(q))
                                sp.dma_start(dB, row(dinv_d[bass.ds(q * GW, GW)]).broadcast_to([P, GW])).then_inc(more_in[0].sem, 16)
                            sp.wait_ge(dve_a.sem, dve_a.after(q + 1))
                            sp.dma_start(rows_of(table, q), group(ost[b])).then_inc(half_out[b].sem, 16)
                    for b in range(2):
                        sp.wait_ge(half_out[b].sem, half_out[b].after(16 * (NG // 2)))
                    if al is not None:
                        sp.wait_ge(dve_b.sem, dve_b.after(NG))
                        for tb, buf in ((al_table, als), (ald_table, ald)):
                            sp.dma_start(tb.rearrange("(i p) h -> p i h", p=P),
                                         buf[:, 0:NT * heads].rearrange("p (i h) -> p i h", h=heads)).then_inc(stores.sem, 16)
                        sp.wait_ge(stores.sem, stores.after(32))
            act_a.passed(NG)
            if not from_f:
                pool_a.passed(NG)
                pe_a.passed(NG)
            pe_b.passed(NG)
            dve_a.passed(NG)
            for s in half_out:
                s.passed(16 * (NG // 2))
            if al is not None:
                pe_c.passed(NG)
                dve_b.passed(NG)
                stores.passed(32)
            if init_f:
                pe_c.passed(NG)
                dve_c.passed(NG)
                more_in[0].passed(16 * NG)

        def bring(pool, table, to, free, ready=pool_a):
            with pool.Fori(0, NG // 2) as i:
                for b in range(2):
                    q = i * 2 + b
                    pool.wait_ge(free.sem, free.after(q - 1))
                    pool.tensor_copy(to[b], table[:, bass.ds(q * GW, GW)]).then_inc(ready.sem, 1)

        als = st6
        dB = wk[:, 4 * GW:5 * GW]
        stage = wk[:, 5 * GW:6 * GW]
        gbuf = [wk[:, j * P:(j + 1) * P] for j in range(2 * HALF)]
        onehot = [wk[:, (2 * HALF + j) * P:(2 * HALF + j + 1) * P] for j in range(2 * HALF)]

        def aggregate(table, clear=False, w=None, heads=0):
            with nc.Block() as block:
                @block.scalar
                def _(act):
                    with act.Fori(0, EI) as i:
                        for b in range(2):
                            k0 = i * (2 * HALF) + b * HALF
                            act.wait_ge(summed.sem, summed.after(k0 - HALF))
                            act.copy(idx[:, b * HALF:(b + 1) * HALF], srcT[:, bass.ds(k0, HALF)]).then_inc(idx_ready.sem, 1)

                @block.gpsimd
                def _(pool):
                    with pool.Fori(0, EI) as i:
                        for b in range(2):
                            pool.wait_ge(idx_ready.sem, idx_ready.after(i * 2 + b + 1))
                            pool.sem_inc(idx_taken.sem, 1)
                            for j in range(b * HALF, (b + 1) * HALF):
                                pool.indirect_dma_start(gbuf[j], None, table, bass.IndirectOffsetOnAxis(idx[:, j:j + 1], 0))\
                                    .then_inc(gathered[j].sem, 16)

                @block.tensor
                def _(pe):
                    with pe.Fori(0, EI) as i:
                        for j in range(2 * HALF):
                            k = i * (2 * HALF) + j
                            if heads > 1:
                                pe.wait_ge(scaled.sem, scaled.after(k + 1))
                            else:
                                pe.wait_ge(gathered[j].sem, gathered[j].after((i + 1) * 16))
                            pe.wait_ge(onehot_ready.sem, onehot_ready.after(k + 1))
                            pe.wait_ge(added.sem, added.after(k - 7))
                            pe.matmul(bank(j % 8, P), gbuf[j], onehot[j], start=True, stop=True).then_inc(summed.sem, 1)

                @block.vector
                def _(v):
                    if clear:
                        linker(v)(v.memset(F[:, :], 0.0))
                    with v.Fori(0, EI) as i:
                        for b in range(2):
                            k0 = i * (2 * HALF) + b * HALF
                            v.wait_ge(summed.sem, summed.after(k0 - HALF))
                            for j in range(HALF):
                                s2, op1 = (w[:, bass.ds(k0 + j, 1)], ALU.mult) if heads == 1 else (None, ALU.bypass)
                                v.tensor_scalar(onehot[b * HALF + j], iota_row[:, :], locT[:, bass.ds(k0 + j, 1)], s2,
                                                ALU.is_equal, op1).then_inc(onehot_ready.sem, 1)
                            if heads > 1:
                                for j in range(HALF):
                                    v.wait_ge(gathered[b * HALF + j].sem, gathered[b * HALF + j].after((i + 1) * 16))
                                    g3 = gbuf[b * HALF + j].rearrange("p (h d) -> p h d", h=heads)
                                    w3 = w[:, bass.ds((k0 + j) * heads, heads)].unsqueeze(2).broadcast_to([P, heads, D // heads])
                                    v.tensor_tensor(g3, g3, w3, ALU.mult).then_inc(scaled.sem, 1)
                            _, first_dst = nc.values_load_multi_w_load_instructions(
                                ebi[0:1, bass.ds(k0, HALF)], engines=[mybir.EngineType.DVE], min_val=0, max_val=NP,
                                skip_runtime_bounds_check_because="dst holds node numbers")
                            for j in range(HALF):
                                cols = F[:, bass.ds(first_dst[j], P)]
                                v.wait_ge(summed.sem, summed.after(k0 + j + 1))
                                v.wait_ge(added.sem, added.after(k0 + j))
                                v.tensor_tensor(cols, cols, bank((b * HALF + j) % 8, P), ALU.add).then_inc(added.sem, 1)
            for s in gathered:
                s.passed(16 * EI)
            summed.passed(K)
            added.passed(K)
            onehot_ready.passed(K)
            idx_ready.passed(2 * EI)
            if heads > 1:
                scaled.passed(K)

        def attention_weights(heads, al_table, ald_table, ex, w):
            z = hs[:, 0:ROW * heads]
            zh = [z[:, h * ROW:(h + 1) * ROW] for h in range(heads)]
            raw = F[:, 0:ROW * heads]
            alh = ald[:, 0:HEADS]
            t1 = F[:, ROW * HEADS:ROW * (HEADS + 1)]
            same = F[:, ROW * (HEADS + 1):ROW * (HEADS + 2)]
            carry = wk[:, 2 * P:2 * P + 4 * HEADS]
            crow = wk[0:HEADS, 3 * P:6 * P]
            runh = [raw[:, h * ROW:(h + 1) * ROW] for h in range(heads)]
            cut = hs[:, ROW * HEADS:ROW * (HEADS + 1)]
            cut_next = hs[:, ROW * (HEADS + 1):ROW * (HEADS + 2)]
            small = wk[:, 0:2 * HALF * HEADS]
            first_dst = wk[:, P:P + 1].bitcast(I32)
            with nc.Block() as block:
                @block.scalar
                def _(act):
                    with act.Fori(0, EI) as i:
                        for b in range(2):
                            k0 = i * (2 * HALF) + b * HALF
                            act.wait_ge(scaled.sem, scaled.after(i * 2 + b - 1))
                            act.copy(idx[:, b * HALF:(b + 1) * HALF], srcT[:, bass.ds(k0, HALF)]).then_inc(idx_ready.sem, 1)

                @block.gpsimd
                def _(pool):
                    for i in range(NT):
                        n = min(P, N + 1 - i * P)
                        pool.indirect_dma_start(ex, bass.IndirectOffsetOnAxis(start_i[0:n, i:i + 1], 0),
                                                ald[0:n, i * heads:(i + 1) * heads], None).then_inc(spread.sem, 16)
                    with pool.Fori(0, EI) as i:
                        for b in range(2):
                            pool.wait_ge(idx_ready.sem, idx_ready.after(i * 2 + b + 1))
                            pool.sem_inc(idx_taken.sem, 1)
                            for j in range(b * HALF, (b + 1) * HALF):
                                pool.indirect_dma_start(small[:, j * heads:(j + 1) * heads], None, al_table,
                                                        bass.IndirectOffsetOnAxis(idx[:, j:j + 1], 0)).then_inc(half_in[b].sem, 16)
                    pool.wait_ge(spread.sem, spread.after(16 * NT))
                    pool.wait_ge(loads.sem, loads.after(16))
                    pool.indirect_dma_start(alh[:, 0:heads], None, ald_table,
                                            bass.IndirectOffsetOnAxis(first_dst, 0)).then_inc(picked.sem, 16)
                    pool.wait_ge(picked.sem, picked.after(16))

                @block.vector
                def _(v):
                    with v.Fori(0, EI) as i:
                        for b in range(2):
                            k0 = i * (2 * HALF) + b * HALF
                            v.wait_ge(half_in[b].sem, half_in[b].after((i + 1) * (16 * HALF)))
                            v.tensor_copy(raw[:, bass.ds(k0 * heads, HALF * heads)],
                                          small[:, b * HALF * heads:(b + 1) * HALF * heads]).then_inc(scaled.sem, 1)

                @block.sync
                def _(sp):
                    sp.dma_start(same, same_d).then_inc(more_in[0].sem, 16)
                    sp.wait_ge(more_in[0].sem, more_in[0].after(16))
                    sp.dma_start(first_dst, dst_d.rearrange("(p g) c -> p (g c)", p=P)[:, 0:1]).then_inc(loads.sem, 16)
            idx_ready.passed(2 * EI)
            scaled.passed(2 * EI)
            spread.passed(16 * NT)
            picked.passed(16)
            loads.passed(16)
            more_in[0].passed(16)
            for s in half_in[0:2]:
                s.passed(16 * HALF * EI)


            TR = G * heads
            NB = (TR + 3) // 4
            parts = [(n, h, n * P - h * ROW) for n in range(TR) for h in [n // G]]
            with nc.Block() as block:
                @block.tensor
                def _(pe):
                    for n, h, c in parts:
                        if n % 4 == 0 and n >= 32:
                            pe.wait_ge(dve_a.sem, dve_a.after(n // 4 - 7))
                        tiles = raw[:, c * heads:(c + P) * heads].rearrange("p (k h) -> p k h", h=heads)[:, :, h]
                        last = pe.transpose(bank(n // 4 % 8)[:, n % 4 * P:(n % 4 + 1) * P], tiles, ident[:, :])
                        if n % 4 == 3 or n == TR - 1:
                            last.then_inc(pe_a.sem, 1)

                @block.sync
                def _(sp):
                    sp.wait_ge(pe_a.sem, pe_a.after(NB))
                    sp.dma_start(raw, ex.rearrange("(p j) h -> p (j h)", p=P)).then_inc(loads.sem, 16)

                @block.vector
                def _(v):
                    link = linker(v)
                    v.tensor_scalar(cut, same[:, :], -1.0, BIG, ALU.add, ALU.mult)
                    v.tensor_scalar(cut_next[:, 0:ROW - 1], same[:, 1:], -1.0, BIG, ALU.add, ALU.mult)
                    v.tensor_scalar(cut_next[:, ROW - 1:ROW], link_next[:, :], -1.0, BIG, ALU.add, ALU.mult)
                    for n in range(NB):
                        v.wait_ge(pe_a.sem, pe_a.after(n + 1))
                        wd = min(4, TR - 4 * n) * P
                        v.tensor_copy(z[:, n * 512:n * 512 + wd], bank(n % 8)[:, 0:wd]).then_inc(dve_a.sem, 1)
                    v.wait_ge(loads.sem, loads.after(16))
                    v.wait_ge(dve_a.sem, dve_a.after(NB))
                    for h in range(heads):
                        ad = raw.rearrange("p (j h) -> p j h", h=heads)[:, :, h]
                        link(v.tensor_tensor_scan(t1, same[:, :], ad, alh[:, h:h + 1], ALU.mult, ALU.add))
                        link(v.tensor_tensor(t1, zh[h], t1, ALU.add))
                        link(v.scalar_tensor_tensor(zh[h], t1, SLOPE, t1, ALU.mult, ALU.max))
            pe_a.passed(NB)
            dve_a.passed(NB)
            loads.passed(16)

            def carries(v, link, whole, backward, keep_op, keep, none):
                link(v.tensor_copy(carry[:, HEADS:HEADS + heads], whole.broadcast_to([P, heads])))
                v.nop().then_inc(dve_b.sem, 1)
                v.wait_ge(pe_b.sem, pe_b.after(keep["n"] + 1))
                link(v.memset(crow[0:heads, :], none))
                if keep_op == ALU.mult:
                    link(v.tensor_copy(crow[0:heads, 0:P], PS[0:heads, 512:512 + P]))
                else:
                    link(v.tensor_scalar(crow[0:heads, 0:P], PS[0:heads, 512:512 + P], -1.0, BIG, ALU.add, ALU.mult))
                op1 = ALU.add if keep_op == ALU.mult else ALU.max
                if backward:
                    link(v.tensor_tensor_scan(crow[0:heads, P:2 * P][:, ::-1], crow[0:heads, 0:P][:, ::-1],
                                              PS[0:heads, 0:P][:, ::-1], none, keep_op, op1))
                    into = crow[0:heads, P + 1:2 * P + 1]
                else:
                    link(v.tensor_tensor_scan(crow[0:heads, P + 1:2 * P + 1], crow[0:heads, 0:P], PS[0:heads, 0:P],
                                              none, keep_op, op1))
                    into = crow[0:heads, P:2 * P]
                v.nop().then_inc(dve_b.sem, 1)
                v.wait_ge(pe_b.sem, pe_b.after(keep["n"] + 2))
                keep["n"] += 2
                link(v.tensor_copy(carry[:, 0:heads], PS[:, 1024:1024 + heads]))

            def segment_total(kind):
                hold, op0, op1, none = {"max": (cut, ALU.add, ALU.max, -BIG), "sum": (same[:, :], ALU.mult, ALU.add, 0.0)}[kind]
                with nc.Block() as block:
                    @block.tensor
                    def _(pe):
                        for r in range(2):
                            pe.wait_ge(dve_b.sem, dve_b.after(2 * r + 1))
                            for n in range(2):
                                last = pe.transpose(PS[0:heads, n * 512:n * 512 + P], carry[:, n * HEADS:n * HEADS + heads],
                                                    ident[:, :])
                            last.then_inc(pe_b.sem, 1)
                            pe.wait_ge(dve_b.sem, dve_b.after(2 * r + 2))
                            c = P + 1 if r else P
                            pe.transpose(PS[:, 1024:1024 + heads], crow[0:heads, c:c + P], ident[0:heads, 0:heads])\
                                .then_inc(pe_b.sem, 1)

                    @block.vector
                    def _(v):
                        link = linker(v)
                        keep = {"n": 0}
                        link(v.tensor_reduce(carry[:, 2 * HEADS:2 * HEADS + 1], same[:, :], AX_X, ALU.min))
                        link(v.tensor_reduce(carry[:, 2 * HEADS + 1:2 * HEADS + 2], cut_next, AX_X, ALU.min))
                        link(v.tensor_scalar(carry[:, 2 * HEADS + 1:2 * HEADS + 2], carry[:, 2 * HEADS + 1:2 * HEADS + 2],
                                             0.0, None, ALU.is_ge))
                        for h in range(heads):
                            link(v.tensor_tensor_scan(t1, hold, zh[h], none, op0, op1))
                            link(v.tensor_copy(carry[:, h:h + 1], t1[:, ROW - 1:ROW]))
                        carries(v, link, carry[:, 2 * HEADS:2 * HEADS + 1], False, op0, keep, none)
                        for h in range(heads):
                            link(v.tensor_tensor_scan(runh[h], hold, zh[h], carry[:, h:h + 1], op0, op1))
                        for h in range(heads):
                            link(v.tensor_tensor_scan(t1[:, ::-1], cut_next[:, ::-1], runh[h][:, ::-1], -BIG, ALU.add, ALU.max))
                            link(v.tensor_copy(carry[:, h:h + 1], t1[:, 0:1]))
                        carries(v, link, carry[:, 2 * HEADS + 1:2 * HEADS + 2], True, ALU.add, keep, -BIG)
                        for h in range(heads):
                            link(v.tensor_tensor_scan(runh[h][:, ::-1], cut_next[:, ::-1], runh[h][:, ::-1],
                                                      carry[:, h:h + 1], ALU.add, ALU.max))
                            if kind == "max":
                                link(v.tensor_tensor(zh[h], zh[h], runh[h], ALU.subtract))
                            else:
                                link(v.tensor_scalar(runh[h], runh[h], 1e-16, None, ALU.add))
                                link(v.reciprocal(runh[h], runh[h]))
                                link(v.tensor_tensor(zh[h], zh[h], runh[h], ALU.mult))
                dve_b.passed(4)
                pe_b.passed(4)

            segment_total("max")
            with nc.Block() as block:
                @block.scalar
                def _(act):
                    for h in range(heads):
                        act.activation(zh[h], zh[h], ACT.Exp)
            segment_total("sum")
            with nc.Block() as block:
                @block.tensor
                def _(pe):
                    for n, h, c in parts:
                        if n % 4 == 0 and n >= 32:
                            pe.wait_ge(dve_a.sem, dve_a.after(n // 4 - 7))
                        last = pe.transpose(bank(n // 4 % 8)[:, n % 4 * P:(n % 4 + 1) * P], zh[h][:, c:c + P], ident[:, :])
                        if n % 4 == 3 or n == TR - 1:
                            last.then_inc(pe_a.sem, 1)

                @block.vector
                def _(v):
                    for n in range(NB):
                        v.wait_ge(pe_a.sem, pe_a.after(n + 1))
                        for m in range(min(4, TR - 4 * n)):
                            _, h, c = parts[4 * n + m]
                            o = raw[:, c * heads:(c + P) * heads].rearrange("p (k h) -> p k h", h=heads)[:, :, h]
                            last = v.tensor_copy(o, bank(n % 8)[:, m * P:(m + 1) * P])
                        last.then_inc(dve_a.sem, 1)
                    v.wait_ge(dve_a.sem, dve_a.after(NB))
                    v.tensor_copy(w, raw)
            pe_a.passed(NB)
            dve_a.passed(NB)

        group = lambda a: a.rearrange("p (i f) -> p i f", f=P)

        def load_weights(items, rows=()):
            with nc.Block() as block:
                @block.sync
                def _(sp):
                    for dst, s in items:
                        sp.dma_start(dst, s).then_inc(loads.sem, 16)
                    sp.wait_ge(loads.sem, loads.after(16 * len(items)))
            loads.passed(16 * len(items))

        def attention_columns(w_sb, wt_sb, a_sb, al_sb, heads):
            with nc.Block() as block:
                @block.tensor
                def _(pe):
                    pe.transpose(bank(0, P), w_sb, ident[:, :]).then_inc(pe_a.sem, 1)
                    pe.wait_ge(dve_a.sem, dve_a.after(1))
                    pe.matmul(bank(1, 2 * heads), wt_sb, a_sb, start=True, stop=True).then_inc(pe_a.sem, 1)

                @block.vector
                def _(v):
                    v.wait_ge(pe_a.sem, pe_a.after(1))
                    v.tensor_copy(wt_sb, bank(0, P)).then_inc(dve_a.sem, 1)
                    v.wait_ge(pe_a.sem, pe_a.after(2))
                    v.tensor_copy(al_sb, bank(1, 2 * heads))
            pe_a.passed(2)
            dve_a.passed(1)

        def bias_relu():
            with nc.Block() as block:
                @block.scalar
                def _(act):
                    act.activation(F[:, 0:NP], F[:, 0:NP], ACT.Relu, bias=bcol[:, 0:1])

        layer_norm(xs, hs, ACT.Relu)
        with nc.Block() as block:
            @block.vector
            def _(v):
                v.memset(W[2][:, 0:2 * HEADS], 0.0).then_inc(dve_a.sem, 1)

            @block.sync
            def _(sp):
                sp.dma_start(W[0], t["L0_gnn_W1"]).then_inc(loads.sem, 16)
                sp.wait_ge(dve_a.sem, dve_a.after(1))
                for n, name in enumerate(("L0_gnn_a_src1", "L0_gnn_a_dst1")):
                    for h in range(HEADS):
                        sp.dma_start(W[2][h * HID:(h + 1) * HID, n * HEADS + h:n * HEADS + h + 1], colv(t[name][h, :])).then_inc(loads.sem, 16)
                sp.wait_ge(loads.sem, loads.after(16 * (1 + 2 * HEADS)))
        dve_a.passed(1)
        loads.passed(16 * (1 + 2 * HEADS))
        attention_columns(W[0], W[1], W[2][:, 0:2 * HEADS], W[3][:, 0:2 * HEADS], HEADS)
        project(W[0], tab, al=W[3][:, 0:2 * HEADS], heads=HEADS, al_table=tab_al, ald_table=ald_rows)
        if stop <= 2: return
        w_edges = hs[:, 0:K * HEADS]
        attention_weights(HEADS, tab_al, ald_rows, ex4, w_edges)
        if stop <= 3: return
        aggregate(tab, clear=True, w=w_edges, heads=HEADS)
        if stop <= 4: return
        load_weights([(W[0], t["L0_gnn_W2"]), (W[2][:, 0:1], colv(t["L0_gnn_a_src2"][0, :])),
                      (W[2][:, 1:2], colv(t["L0_gnn_a_dst2"][0, :])), (bcol[:, 0:1], colv(t["L0_gnn_b1"])),
                      (brow[:, 0:D], row(t["L0_gnn_b2"]))])
        attention_columns(W[0], W[1], W[2][:, 0:2], W[3][:, 0:2], 1)
        bias_relu()
        project(W[0], tab, from_f=True, al=W[3][:, 0:2], heads=1, al_table=tab_al1, ald_table=ald_rows1)
        w_edges = hs[:, 0:K]
        attention_weights(1, tab_al1, ald_rows1, ex1, w_edges)
        aggregate(tab, clear=True, w=w_edges, heads=1)
        if stop <= 5: return

        tmp, ex_ = ost, [wk[:, (4 + b) * GW:(5 + b) * GW] for b in range(2)]
        with nc.Block() as block:
            @block.gpsimd
            def _(pool):
                bring(pool, F, hT, pe_a)

            @block.tensor
            def _(pe):
                with pe.Fori(0, NG // 2) as i:
                    for b in range(2):
                        q = i * 2 + b
                        pe.wait_ge(pool_a.sem, pool_a.after(q + 1))
                        pe.wait_ge(dve_a.sem, dve_a.after(q - 1))
                        for j in range(GRP):
                            pe.matmul(tile_of(psB[b], j), tile_of(hT[b], j), ident[:, :], start=True, stop=False)
                            last = pe.matmul(tile_of(psB[b], j), ones[:, :], brow[:, 0:D], start=False, stop=True)
                        last.then_inc(pe_a.sem, 1)

            @block.scalar
            def _(act):
                with act.Fori(0, NG // 2) as i:
                    for b in range(2):
                        q = i * 2 + b
                        act.wait_ge(dve_a.sem, dve_a.after(q + 1))
                        act.activation(ex_[b], tmp[b], ACT.Exp).then_inc(act_a.sem, 1)
                        act.wait_ge(dve_b.sem, dve_b.after(q + 1))
                        act.activation(sm[:, b * NT + GRP:b * NT + 2 * GRP], sm[:, b * NT + 2 * GRP:b * NT + 3 * GRP], ACT.Ln)\
                            .then_inc(act_b.sem, 1)

            @block.vector
            def _(v):
                link = linker(v)
                with v.Fori(0, NG // 2) as i:
                    for b in range(2):
                        q = i * 2 + b
                        mx, lns, ssum = (sm[:, b * NT + n * GRP:b * NT + (n + 1) * GRP] for n in range(3))
                        wide = lambda a: a.unsqueeze(2).broadcast_to([P, GRP, P])
                        v.wait_ge(pe_a.sem, pe_a.after(q + 1))
                        v.tensor_reduce(mx, group(psB[b]), AX_X, ALU.max).then_inc(dve_c.sem, 1)
                        v.wait_ge(dve_c.sem, dve_c.after(q * 3 + 1))
                        v.tensor_tensor(group(tmp[b]), group(psB[b]), wide(mx), ALU.subtract).then_inc(dve_a.sem, 1)
                        v.wait_ge(act_a.sem, act_a.after(q + 1))
                        v.tensor_reduce(ssum, group(ex_[b]), AX_X, ALU.add).then_inc(dve_b.sem, 1)
                        v.wait_ge(act_b.sem, act_b.after(q + 1))
                        v.tensor_tensor(group(tmp[b]), group(tmp[b]), wide(lns), ALU.subtract).then_inc(dve_c.sem, 1)
                        v.wait_ge(dve_c.sem, dve_c.after(q * 3 + 2))
                        xg = xs[:, bass.ds(q * GW, GW)]
                        v.tensor_tensor(xg, xg, tmp[b], ALU.add).then_inc(dve_c.sem, 1)
                        v.wait_ge(dve_c.sem, dve_c.after(q * 3 + 3))
        for s in (dve_a, act_a, act_b, dve_b, pe_a, pool_a):
            s.passed(NG)
        dve_c.passed(3 * NG)
        if stop <= 6: return

        layer_norm(xs, hs, ACT.Relu)
        QT = 4
        NQ = K // QT
        place = [0]

        def in_f(width, dt=F32):
            a = F[:, place[0]:place[0] + width]
            place[0] += width
            return a.bitcast(dt) if dt != F32 else a

        QW = QT * P
        two = lambda width, dt=F32: [in_f(width, dt) for _ in range(2)]
        a_rows, b_win, src_rows, attrs = two(QW), two(QW), two(QW, I32), two(QT * 16)
        oh, ohT, eq, attrT, h1, msg, msum = two(QW), two(QW), two(QW), two(P), two(QW), two(QW), two(QW)
        seen, dups, delta, picks = in_f(QW), two(QT), two(QT), two(QT)
        wc = [in_f(P) for _ in range(QT)]
        sidx = two(QT, I32)
        trash = in_f(1)
        with nc.Block() as block:
            @block.vector
            def _(v):
                for w_ in wc:
                    last = v.memset(w_[0:QT * 16, :], 0.0)
                last.then_inc(dve_a.sem, 1)
                v.tensor_scalar(trash, pcol[:, :], float(NP), None, ALU.add)

            @block.sync
            def _(sp):
                for dst, s in ((W[0], t["L1_gnn_eW1"][0:D, :]), (W[1], t["L1_gnn_eW1"][D:2 * D, :]),
                               (W[2], t["L1_gnn_eW2"]), (brow[:, 0:D], row(t["L1_gnn_eb1"])),
                               (brow[:, D:2 * D], row(t["L1_gnn_eb2"]))):
                    sp.dma_start(dst, s).then_inc(loads.sem, 16)
                sp.wait_ge(dve_a.sem, dve_a.after(1))
                for u in range(QT):
                    sp.dma_start(wc[u][16 * u:16 * (u + 1), :], t["L1_gnn_eW1"][2 * D:, :]).then_inc(loads.sem, 16)
                sp.wait_ge(loads.sem, loads.after(16 * (5 + QT)))
        dve_a.passed(1)
        loads.passed(16 * (5 + QT))
        project(W[0], tab, bias=brow[:, 0:D])
        project(W[1], tab_b)

        src_by_row = src_d.rearrange("(p g) c -> g p c", g=G)
        attr_by_row = attr_d.rearrange("(p g c) d -> g c p d", g=G, c=P)
        with nc.Block() as block:
            @block.sync
            def _(sp):
                with sp.Fori(0, G) as g:
                    with sp.Fori(0, P // (2 * QT)) as r:
                        i = g * (P // (2 * QT)) + r
                        _, first_dst = nc.values_load_multi_w_load_instructions(
                            ebi[0:1, bass.ds(i * (2 * QT), 2 * QT)], engines=[mybir.EngineType.SP], min_val=0, max_val=NP,
                            skip_runtime_bounds_check_because="dst holds node numbers")
                        for b in range(2):
                            n = i * 2 + b
                            p0 = r * (2 * QT) + b * QT
                            sp.wait_ge(q_made.sem, q_made.after((n - 1) * QT))
                            sp.dma_start(src_rows[b].rearrange("p (u c) -> p u c", u=QT),
                                         src_by_row[bass.ds(g, 1), bass.ds(p0, QT), :].broadcast_to([P, QT, P]))\
                                .then_inc(more_in[2 + b].sem, 16)
                            sp.wait_ge(pe_t.sem, pe_t.after(n - 1))
                            sp.dma_start(attrs[b].rearrange("c (u d) -> c u d", u=QT),
                                         attr_by_row[bass.ds(g, 1), :, bass.ds(p0, QT), :].rearrange("g c p d -> (g c) p d"))\
                                .then_inc(more_in[2 + b].sem, 16)
                            sp.wait_ge(pe_z.sem, pe_z.after(n - 1))
                            for u in range(QT):
                                sp.dma_start(tile_of(b_win[b], u), tab_b[bass.ds(first_dst[b * QT + u], P), :])\
                                    .then_inc(more_in[b].sem, 16)

            @block.gpsimd
            def _(pool):
                def gather(n, b):
                    pool.wait_ge(idx_ready.sem, idx_ready.after(n + 1))
                    pool.sem_inc(idx_taken.sem, 1)
                    for u in range(QT):
                        pool.indirect_dma_start(tile_of(a_rows[b], u), None, tab,
                                                bass.IndirectOffsetOnAxis(idx[:, b * QT + u:b * QT + u + 1], 0))\
                            .then_inc(gathered[b * QT + u].sem, 16)

                def scatter(n, b):
                    pool.wait_ge(msum_ready.sem, msum_ready.after(n + 1))
                    pool.wait_ge(sidx_ready.sem, sidx_ready.after(n + 1))
                    for u in range(QT):
                        pool.wait_ge(scattered[u].sem, scattered[u].after(n * 16))
                        pool.sem_inc(idx_taken.sem, 1)
                        pool.indirect_dma_start(agg[u], bass.IndirectOffsetOnAxis(sidx[b][:, u:u + 1], 0),
                                                tile_of(msum[b], u), None, compute_op=ALU.add).then_inc(scattered[u].sem, 16)

                gather(0, 0)
                gather(1, 1)
                with pool.Fori(0, NQ // 2 - 1) as i:
                    for b in range(2):
                        gather(i * 2 + b + 2, b)
                        scatter(i * 2 + b, b)
                scatter(NQ - 2, 0)
                scatter(NQ - 1, 1)
                for u in range(QT):
                    pool.wait_ge(scattered[u].sem, scattered[u].after(NQ * 16))

            def steps(eng, step):
                step(0, 0, 0)
                with eng.Fori(0, NQ // 2 - 1) as i:
                    step(i * 2 + 1, 1, i)
                    step(i * 2 + 2, 0, i + 1)
                step(NQ - 1, 1, NQ // 2 - 1)
                step(NQ, 0, NQ // 2)

            inside = lambda n: not isinstance(n, int) or n < NQ
            behind = lambda n: not isinstance(n, int) or n > 0

            @block.tensor
            def _(pe):
                def step(n, b, h):
                    if inside(n):
                        pe.wait_ge(onehot_ready.sem, onehot_ready.after(n + 1))
                        pe.wait_ge(more_in[2 + b].sem, more_in[2 + b].after((h + 1) * 32))
                        pe.wait_ge(ohT_ready.sem, ohT_ready.after(n))
                        for u in range(QT):
                            pe.transpose(tile_of(bank(b), u), tile_of(oh[b], u), ident[:, :])
                        pe.transpose(PS[0:QT * 16, 7 * 512:7 * 512 + P], attrs[b], ident[:, :]).then_inc(pe_t.sem, 1)
                    if behind(n):
                        pe.wait_ge(h1_ready.sem, h1_ready.after(n))
                        pe.wait_ge(msg_ready.sem, msg_ready.after(n - 2))
                        for u in range(QT):
                            pe.matmul(tile_of(bank(5 - b), u), tile_of(h1[1 - b], u), W[2], start=True, stop=False)
                            last = pe.matmul(tile_of(bank(5 - b), u), ones[:, :], brow[:, D:2 * D], start=False, stop=True)
                        last.then_inc(pe_m.sem, 1)
                    if inside(n):
                        pe.wait_ge(ohT_ready.sem, ohT_ready.after(n + 1))
                        pe.wait_ge(more_in[b].sem, more_in[b].after((h + 1) * (16 * QT)))
                        pe.wait_ge(h1_ready.sem, h1_ready.after(n - 1))
                        for u in range(QT):
                            pe.wait_ge(gathered[b * QT + u].sem, gathered[b * QT + u].after((h + 1) * 16))
                            z = tile_of(bank(2 + b), u)
                            pe.matmul(z, tile_of(a_rows[b], u), ident[:, :], start=True, stop=False)
                            pe.matmul(z, wc[u][0:QT * 16, :], attrT[b][0:QT * 16, :], start=False, stop=False)
                            last = pe.matmul(z, tile_of(b_win[b], u), tile_of(ohT[b], u), start=False, stop=True)
                        last.then_inc(pe_z.sem, 1)
                    if behind(n):
                        pe.wait_ge(msg_ready.sem, msg_ready.after(n))
                        pe.wait_ge(q_made.sem, q_made.after(n * QT))
                        pe.wait_ge(msum_ready.sem, msum_ready.after(n - 1))
                        for u in range(QT):
                            last = pe.matmul(tile_of(bank(6), u), tile_of(eq[1 - b], u), tile_of(msg[1 - b], u),
                                             start=True, stop=True)
                        last.then_inc(pe_d.sem, 1)
                steps(pe, step)

            @block.scalar
            def _(act):
                def take(n, b):
                    act.wait_ge(pe_z.sem, pe_z.after(n - 1))
                    act.copy(idx[:, b * QT:(b + 1) * QT], srcT[:, bass.ds(n * QT, QT)]).then_inc(idx_ready.sem, 1)

                def step(n, b, h):
                    if isinstance(n, int) and n == 0:
                        take(0, 0)
                        take(1, 1)
                    elif not isinstance(n, int):
                        take(n + 1, 1 - b)
                    if inside(n):
                        act.wait_ge(pe_t.sem, pe_t.after(n + 1))
                        act.wait_ge(pe_z.sem, pe_z.after(n - 1))
                        act.copy(ohT[b], bank(b))
                        act.copy(attrT[b][0:QT * 16, :], PS[0:QT * 16, 7 * 512:7 * 512 + P]).then_inc(ohT_ready.sem, 1)
                    if behind(n):
                        act.wait_ge(pe_m.sem, pe_m.after(n))
                        act.wait_ge(pe_d.sem, pe_d.after(n - 2))
                        act.activation(msg[1 - b], bank(5 - b), ACT.Silu).then_inc(msg_ready.sem, 1)
                    if inside(n):
                        act.wait_ge(pe_z.sem, pe_z.after(n + 1))
                        act.wait_ge(pe_m.sem, pe_m.after(n - 1))
                        act.activation(h1[b], bank(2 + b), ACT.Silu).then_inc(h1_ready.sem, 1)
                steps(act, step)

            @block.vector
            def _(v):
                def step(n, b, h):
                    if inside(n):
                        v.wait_ge(pe_t.sem, pe_t.after(n - 1))
                        for u in range(QT):
                            last = v.tensor_scalar(tile_of(oh[b], u), iota_row[:, :], locT[:, bass.ds(n * QT + u, 1)], None,
                                                   ALU.is_equal)
                        last.then_inc(onehot_ready.sem, 1)
                        v.wait_ge(more_in[2 + b].sem, more_in[2 + b].after((h + 1) * 32))
                        v.wait_ge(pe_d.sem, pe_d.after(n - 1))
                        for u in range(QT):
                            v.tensor_scalar(tile_of(eq[b], u), tile_of(src_rows[b], u), srcT[:, bass.ds(n * QT + u, 1)], None,
                                            ALU.is_equal).then_inc(q_made.sem, 1)
                        v.tensor_scalar(delta[b], srcT[:, bass.ds(n * QT, QT)], trash, None, ALU.subtract)
                        for u in range(QT):
                            v.wait_ge(q_made.sem, q_made.after(n * QT + u + 1))
                            v.scalar_tensor_tensor(tile_of(seen, u), tile_of(eq[b], u), 1.0, lower[:, :], ALU.mult, ALU.mult,
                                                   accum_out=dups[b][:, u:u + 1]).then_inc(dups_made.sem, 1)
                        v.wait_ge(dups_made.sem, dups_made.after((n + 1) * QT))
                        v.scalar_tensor_tensor(picks[b], dups[b], 0.0, delta[b], ALU.is_equal, ALU.mult).then_inc(picked_rows.sem, 1)
                    if behind(n):
                        v.wait_ge(pe_d.sem, pe_d.after(n))
                        v.tensor_copy(msum[1 - b], bank(6)).then_inc(msum_ready.sem, 1)
                    if inside(n):
                        v.wait_ge(picked_rows.sem, picked_rows.after(n + 1))
                        if behind(n):
                            for u in range(QT):
                                v.wait_ge(scattered[u].sem, scattered[u].after((n - 1) * 16))
                        v.tensor_scalar(sidx[b], picks[b], trash, None, ALU.add).then_inc(sidx_ready.sem, 1)
                steps(v, step)
        for s in (pe_t, pe_m, pe_z, pe_d, ohT_ready, h1_ready, msg_ready, msum_ready, sidx_ready, picked_rows, onehot_ready,
                  idx_ready):
            s.passed(NQ)
        for s in (q_made, dups_made):
            s.passed(NQ * QT)
        for s in gathered[0:2 * QT]:
            s.passed(16 * (NQ // 2))
        for s in more_in[0:2]:
            s.passed(16 * QT * (NQ // 2))
        for s in more_in[2:4]:
            s.passed(32 * (NQ // 2))
        if stop <= 7: return

        load_weights([(W[0], t["L1_gnn_nW1"][0:D, :]), (W[1], t["L1_gnn_nW1"][D:2 * D, :]), (W[2], t["L1_gnn_nW2"]),
                      (bcol[:, 0:1], colv(t["L1_gnn_nb1"])), (brow[:, 0:D], row(t["L1_gnn_nb2"]))])
        place[0] = 0
        parts_in = [[in_f(GW) for a in range(AGG)] for b in range(2)]
        aT, uT = two(GW), two(GW)
        with nc.Block() as block:
            @block.sync
            def _(sp):
                with sp.Fori(0, NG // 2) as i:
                    for b in range(2):
                        q = i * 2 + b
                        sp.wait_ge(pe_t.sem, pe_t.after(q - 1))
                        for a in range(AGG):
                            sp.dma_start(group(parts_in[b][a]), rows_of(agg[a], q)).then_inc(more_in[b].sem, 16)

            @block.gpsimd
            def _(pool):
                with pool.Fori(0, NG) as q:
                    pool.wait_ge(pe_a.sem, pe_a.after(q))
                    pool.tensor_copy(stage, hs[:, bass.ds(q * GW, GW)]).then_inc(pool_a.sem, 1)

            @block.vector
            def _(v):
                with v.Fori(0, NG // 2) as i:
                    for b in range(2):
                        q = i * 2 + b
                        v.wait_ge(more_in[b].sem, more_in[b].after((i + 1) * (16 * AGG)))
                        total = parts_in[b][0]
                        for a in range(1, AGG):
                            v.tensor_tensor(total, total, parts_in[b][a], ALU.add).then_inc(dve_a.sem, 1)
                            v.wait_ge(dve_a.sem, dve_a.after(q * (AGG - 1) + a))
                        xg = xs[:, bass.ds(q * GW, GW)]
                        v.tensor_tensor(xg, xg, hs[:, bass.ds(q * GW, GW)], ALU.add).then_inc(dve_b.sem, 1)
                        v.wait_ge(pe_c.sem, pe_c.after(q + 1))
                        v.wait_ge(dve_b.sem, dve_b.after(q + 1))
                        v.tensor_tensor(xg, xg, psB[b], ALU.add).then_inc(dve_c.sem, 1)

            @block.tensor
            def _(pe):
                with pe.Fori(0, NG // 2) as i:
                    for b in range(2):
                        q = i * 2 + b
                        pe.wait_ge(pool_a.sem, pool_a.after(q + 1))
                        pe.wait_ge(act_b.sem, act_b.after(q - 1))
                        for j in range(GRP):
                            last = pe.transpose(tile_of(psA[b], j), tile_of(stage, j), ident[:, :])
                        last.then_inc(pe_a.sem, 1)
                        pe.wait_ge(dve_a.sem, dve_a.after((q + 1) * (AGG - 1)))
                        pe.wait_ge(dve_c.sem, dve_c.after(q - 1))
                        for j in range(GRP):
                            last = pe.transpose(tile_of(psB[b], j), tile_of(parts_in[b][0], j), ident[:, :])
                        last.then_inc(pe_t.sem, 1)
                        pe.wait_ge(act_a.sem, act_a.after(q * 2 + 2))
                        for a, z in ((0, 512), (512, GW)):
                            pe.matmul(psA[b][:, a:z], W[0], hT[b][:, a:z], start=True, stop=False)
                            last = pe.matmul(psA[b][:, a:z], W[1], aT[b][:, a:z], start=False, stop=True)
                        last.then_inc(pe_b.sem, 1)
                        pe.wait_ge(act_b.sem, act_b.after(q + 1))
                        for j in range(GRP):
                            pe.matmul(tile_of(psB[b], j), tile_of(uT[b], j), W[2], start=True, stop=False)
                            last = pe.matmul(tile_of(psB[b], j), ones[:, :], brow[:, 0:D], start=False, stop=True)
                        last.then_inc(pe_c.sem, 1)

            @block.scalar
            def _(act):
                with act.Fori(0, NG // 2) as i:
                    for b in range(2):
                        q = i * 2 + b
                        act.wait_ge(pe_b.sem, pe_b.after(q - 1))
                        act.wait_ge(pe_a.sem, pe_a.after(q + 1))
                        act.copy(hT[b], psA[b]).then_inc(act_a.sem, 1)
                        act.wait_ge(pe_t.sem, pe_t.after(q + 1))
                        act.copy(aT[b], psB[b]).then_inc(act_a.sem, 1)
                        act.wait_ge(pe_b.sem, pe_b.after(q + 1))
                        act.wait_ge(pe_c.sem, pe_c.after(q - 1))
                        act.activation(uT[b], psA[b], ACT.Silu, bias=bcol[:, 0:1]).then_inc(act_b.sem, 1)
        for s in (pe_a, pe_t, pe_b, pe_c, pool_a, dve_b, dve_c, act_b):
            s.passed(NG)
        act_a.passed(2 * NG)
        dve_a.passed((AGG - 1) * NG)
        for s in more_in[0:2]:
            s.passed(16 * AGG * (NG // 2))
        if stop <= 8: return

        def batch_norm():
            chunks = [(c, min(c + 512, N)) for c in range(0, N, 512)]
            bst = wk[:, 5 * GW:5 * GW + 6 * len(chunks)]
            mv, am, cm = bcol[:, 4:6], bcol[:, 6:7], bcol[:, 7:8]
            db2 = [wk[:, (2 + b) * GW:(3 + b) * GW] for b in range(2)]
            with nc.Block() as block:
                @block.sync
                def _(sp):
                    with sp.Fori(0, NG // 2) as i:
                        for b in range(2):
                            q = i * 2 + b
                            sp.wait_ge(dve_a.sem, dve_a.after(q - 1))
                            sp.dma_start(db2[b], row(dinv_d[bass.ds(q * GW, GW)]).broadcast_to([P, GW])).then_inc(more_in[b].sem, 16)

                @block.scalar
                def _(act):
                    with act.Fori(0, NG) as q:
                        act.wait_ge(dve_a.sem, dve_a.after(q + 1))
                        fg = F[:, bass.ds(q * GW, GW)]
                        act.activation(fg, fg, ACT.Identity, bias=bcol[:, 0:1]).then_inc(act_a.sem, 1)
                    act.wait_ge(dve_b.sem, dve_b.after(1))
                    act.activation(am, am, ACT.Sqrt).then_inc(act_b.sem, 1)
                    act.wait_ge(dve_b.sem, dve_b.after(2))
                    act.activation(F[:, 0:NP], F[:, 0:NP], ACT.Relu, bias=cm, scale=am)

                @block.vector
                def _(v):
                    link = linker(v)
                    with v.Fori(0, NG // 2) as i:
                        for b in range(2):
                            q = i * 2 + b
                            fg = F[:, bass.ds(q * GW, GW)]
                            v.wait_ge(more_in[b].sem, more_in[b].after((i + 1) * 16))
                            v.tensor_tensor(fg, fg, db2[b], ALU.mult).then_inc(dve_a.sem, 1)
                    v.wait_ge(act_a.sem, act_a.after(NG))
                    for n, (a, z) in enumerate(chunks):
                        last = v.bn_stats(bst[:, 6 * n:6 * n + 6], F[:, a:z])
                    link(last)
                    link(v.bn_aggr(mv, bst))
                    link(v.tensor_scalar(am, mv[:, 1:2], EPS, None, ALU.add))
                    v.nop().then_inc(dve_b.sem, 1)
                    v.wait_ge(act_b.sem, act_b.after(1))
                    link(v.reciprocal(am, am))
                    link(v.tensor_tensor(am, am, bcol[:, 1:2], ALU.mult))
                    link(v.tensor_tensor(cm, mv[:, 0:1], am, ALU.mult))
                    link(v.tensor_tensor(cm, bcol[:, 2:3], cm, ALU.subtract))
                    v.nop().then_inc(dve_b.sem, 1)
            act_a.passed(NG)
            act_b.passed(1)
            dve_a.passed(NG)
            dve_b.passed(2)
            for s in more_in[0:2]:
                s.passed(16 * (NG // 2))

        layer_norm(xs, hs, ACT.Relu)
        for n, from_f in (("1", False), ("2", True)):
            load_weights([(W[0], t["L2_gnn_W" + n])] +
                         [(bcol[:, m:m + 1], colv(t["L2_gnn_" + name + n])) for m, name in enumerate(("b", "g", "be"))])
            project(W[0], tab, from_f=from_f, scale=True, init_f=True)
            aggregate(tab)
            batch_norm()
        load_weights([(W[0], t["L2_gnn_Wf"]), (brow[:, 0:D], row(t["L2_gnn_bf"]))])
        with nc.Block() as block:
            @block.gpsimd
            def _(pool):
                bring(pool, F, hT, pe_a)

            @block.tensor
            def _(pe):
                with pe.Fori(0, NG // 2) as i:
                    for b in range(2):
                        q = i * 2 + b
                        pe.wait_ge(pool_a.sem, pool_a.after(q + 1))
                        pe.wait_ge(dve_a.sem, dve_a.after(q - 1))
                        for j in range(GRP):
                            pe.matmul(tile_of(psB[b], j), tile_of(hT[b], j), W[0], start=True, stop=False)
                            last = pe.matmul(tile_of(psB[b], j), ones[:, :], brow[:, 0:D], start=False, stop=True)
                        last.then_inc(pe_a.sem, 1)

            @block.vector
            def _(v):
                with v.Fori(0, NG // 2) as i:
                    for b in range(2):
                        q = i * 2 + b
                        v.wait_ge(pe_a.sem, pe_a.after(q + 1))
                        xg = xs[:, bass.ds(q * GW, GW)]
                        v.tensor_tensor(xg, xg, psB[b], ALU.add).then_inc(dve_a.sem, 1)
        for s in (pool_a, pe_a, dve_a):
            s.passed(NG)
        if stop <= 9: return

        layer_norm(xs, hs, ACT.Relu)
        layer_norm(hs, hs, ACT.Identity)
        load_weights([(W[0], t["L3_gnn_W_self"]), (W[1], t["L3_gnn_W_neigh"]), (brow[:, 0:D], row(t["L3_gnn_b"])),
                      (W[2], row(t["L3_gnn_gamma"]).broadcast_to([P, D])), (W[3], row(t["L3_gnn_beta"]).broadcast_to([P, D]))])
        every = lambda a: a.unsqueeze(1).broadcast_to([P, GRP, P])
        with nc.Block() as block:
            @block.vector
            def _(v):
                with v.Fori(0, NG) as q:
                    hg = group(hs[:, bass.ds(q * GW, GW)])
                    v.tensor_tensor(hg, hg, every(W[2]), ALU.mult).then_inc(dve_a.sem, 1)
                    v.wait_ge(dve_a.sem, dve_a.after(q + 1))
                    v.tensor_tensor(hg, hg, every(W[3]), ALU.add).then_inc(dve_b.sem, 1)

            @block.sync
            def _(sp):
                with sp.Fori(0, NG) as q:
                    sp.wait_ge(dve_b.sem, dve_b.after(q + 1))
                    sp.dma_start(rows_of(tab, q), group(hs[:, bass.ds(q * GW, GW)])).then_inc(stores.sem, 16)
                sp.wait_ge(stores.sem, stores.after(16 * NG))
        dve_a.passed(NG)
        dve_b.passed(NG)
        stores.passed(16 * NG)
        aggregate(tab, clear=True)

        fT = [wk[:, (4 + b) * GW:(5 + b) * GW] for b in range(2)]
        with nc.Block() as block:
            @block.gpsimd
            def _(pool):
                with pool.Fori(0, NG // 2) as i:
                    for b in range(2):
                        q = i * 2 + b
                        pool.wait_ge(pe_a.sem, pe_a.after(q - 1))
                        pool.tensor_copy(ost[b], hs[:, bass.ds(q * GW, GW)]).then_inc(pool_a.sem, 1)
                        pool.wait_ge(pe_b.sem, pe_b.after(q - 1))
                        pool.tensor_copy(fT[b], F[:, bass.ds(q * GW, GW)]).then_inc(pool_a.sem, 1)

            @block.tensor
            def _(pe):
                with pe.Fori(0, NG // 2) as i:
                    for b in range(2):
                        q = i * 2 + b
                        pe.wait_ge(pool_a.sem, pool_a.after(q * 2 + 1))
                        pe.wait_ge(dve_a.sem, dve_a.after(q - 1))
                        for j in range(GRP):
                            last = pe.transpose(tile_of(psA[b], j), tile_of(ost[b], j), ident[:, :])
                        last.then_inc(pe_a.sem, 1)
                        pe.wait_ge(act_a.sem, act_a.after(q + 1))
                        pe.wait_ge(pool_a.sem, pool_a.after(q * 2 + 2))
                        pe.wait_ge(dve_c.sem, dve_c.after(q - 1))
                        for j in range(GRP):
                            pe.matmul(tile_of(psB[b], j), tile_of(hT[b], j), W[0], start=True, stop=False)
                            pe.matmul(tile_of(psB[b], j), ones[:, :], brow[:, 0:D], start=False, stop=True)
                        for j in range(GRP):
                            last = pe.matmul(tile_of(psA[b], j), tile_of(fT[b], j), W[1], start=True, stop=True)
                        last.then_inc(pe_b.sem, 1)

            @block.scalar
            def _(act):
                with act.Fori(0, NG // 2) as i:
                    for b in range(2):
                        q = i * 2 + b
                        act.wait_ge(pe_a.sem, pe_a.after(q + 1))
                        act.wait_ge(pe_b.sem, pe_b.after(q - 1))
                        act.copy(hT[b], psA[b]).then_inc(act_a.sem, 1)

            @block.vector
            def _(v):
                with v.Fori(0, NG // 2) as i:
                    for b in range(2):
                        q = i * 2 + b
                        v.wait_ge(pe_b.sem, pe_b.after(q + 1))
                        r3 = rdeg[:, bass.ds(q * GRP, GRP)].unsqueeze(2).broadcast_to([P, GRP, P])
                        xg = xs[:, bass.ds(q * GW, GW)]
                        fg = F[:, bass.ds(q * GW, GW)]
                        v.tensor_tensor(group(fg), group(psA[b]), r3, ALU.mult).then_inc(dve_a.sem, 1)
                        v.tensor_tensor(xg, xg, psB[b], ALU.add).then_inc(dve_c.sem, 1)
                        v.wait_ge(dve_a.sem, dve_a.after(q + 1))
                        v.wait_ge(dve_c.sem, dve_c.after(q + 1))
                        v.tensor_tensor(xg, xg, fg, ALU.add).then_inc(dve_b.sem, 1)

            @block.sync
            def _(sp):
                with sp.Fori(0, NG - 1) as q:
                    sp.wait_ge(dve_b.sem, dve_b.after(q + 1))
                    sp.dma_start(rows_of(out, q), group(xs[:, bass.ds(q * GW, GW)])).then_inc(stores.sem, 16)
                sp.wait_ge(dve_b.sem, dve_b.after(NG))
                c = (NG - 1) * GW
                sp.dma_start(out[c:c + (GRP - 1) * P, :].rearrange("(i p) f -> p i f", p=P),
                             group(xs[:, c:c + (GRP - 1) * P])).then_inc(stores.sem, 16)
                sp.dma_start(out[(NT - 1) * P:N, :], xs[0:N - (NT - 1) * P, (NT - 1) * P:]).then_inc(stores.sem, 16)
                sp.wait_ge(stores.sem, stores.after(16 * (NG + 1)))


_FIELDS = ["x", "src", "dst", "edge_attr_16",
           "L0_gnn_W1", "L0_gnn_a_src1", "L0_gnn_a_dst1", "L0_gnn_b1", "L0_gnn_W2", "L0_gnn_a_src2", "L0_gnn_a_dst2",
           "L0_gnn_b2", "L1_gnn_eW1", "L1_gnn_eb1", "L1_gnn_eW2", "L1_gnn_eb2", "L1_gnn_nW1", "L1_gnn_nb1", "L1_gnn_nW2",
           "L1_gnn_nb2", "L2_gnn_W1", "L2_gnn_b1", "L2_gnn_g1", "L2_gnn_be1", "L2_gnn_W2", "L2_gnn_b2", "L2_gnn_g2",
           "L2_gnn_be2", "L2_gnn_Wf", "L2_gnn_bf", "L3_gnn_gamma", "L3_gnn_beta", "L3_gnn_W_self", "L3_gnn_W_neigh",
           "L3_gnn_b"]


def kernel(**inputs):
    import numpy as np
    import concourse.bacc as bacc
    from concourse.bass_utils import run_bass_kernel_spmd

    nc = bacc.Bacc("TRN2", target_bir_lowering=False, num_devices=1)
    arrays, t = {}, {}
    for name in _FIELDS:
        a = np.ascontiguousarray(inputs[name])
        arrays[f"in_{name}_dram"] = a
        t[name] = nc.dram_tensor(f"in_{name}_dram", a.shape, mybir.dt.from_np(a.dtype), kind="ExternalInput").ap()
    out = nc.dram_tensor("out_0_dram", (N, D), F32, kind="ExternalOutput").ap()
    build(nc, t, out)
    r = run_bass_kernel_spmd(nc, [arrays], core_ids=[0])
    return r.results[0]["out_0_dram"]
```

```python
from contextlib import ExitStack

import concourse.bass as bass
from concourse import mybir

F32 = mybir.dt.float32
I32 = mybir.dt.int32
ALU = mybir.AluOpType
ACT = mybir.ActivationFunctionType
AX_X = mybir.AxisListType.X

P = 128
N = 12500
E = 212500
D = 128
NT = (N + P - 1) // P
NP = NT * P
WIN = NP + P
ROW = 1664
G = ROW // P
K = G * P
EP = K * P
LAST = E - (P - 1) * ROW
GRP = 7
GW = GRP * P
NG = NT // GRP
HALF = 8
EI = K // (2 * HALF)
BT = 32
NBT = K // BT
HEADS = 4
HID = 32
SLOPE = 0.2
BIG = 1e30
EPS = 1e-5
LEAD = 16
AGG = 4


class Signal:

    def __init__(self, sem, at):
        self.sem, self.at = sem, at

    def after(self, n):
        return n + self.at

    def passed(self, n):
        self.at += n


def build(nc, t, out, stop=99):
    ctx = ExitStack()
    with ctx:
        ctx.enter_context(nc.allow_non_contiguous_dma(reason="columns of one element a row, all short"))
        def sb(name, shape, dt=F32):
            return ctx.enter_context(nc.sbuf_tensor(name, shape, dt))

        signals = []

        def sig(name, lead=LEAD):
            signals.append(Signal(ctx.enter_context(nc.semaphore(name)), lead))
            return signals[-1]

        def dram(name, shape, dt=F32):
            return nc.dram_tensor(name, shape, dt, kind="Internal").ap()

        tab = dram("tab", (NP, D))
        tab_b = dram("tab_b", (WIN, D))
        tab_g1 = dram("tab_g1", (NP, D + HEADS))
        tab_g2 = dram("tab_g2", (NP, D + 1))
        ald_e = dram("ald_e", (K * HEADS, P))
        ald_rows = dram("ald_rows", (NP, HEADS))
        ald_rows1 = dram("ald_rows1", (NP, 1))
        ex4 = dram("ex4", (EP, HEADS))
        ex1 = dram("ex1", (EP, 1))
        src_d = dram("src_d", (K, P), I32)
        dst_d = dram("dst_d", (K, P), I32)
        attr_d = dram("attr_d", (EP, 16))
        agg_all = [dram(f"agg{a}", (NP + 2 * K, D)) for a in range(AGG)]
        agg = [a[0:WIN, :] for a in agg_all]
        whole_rows = agg_all[0:2]
        eb_i_d = dram("eb_i_d", (G, P), I32)
        eb_f_d = dram("eb_f_d", (G, P))
        piece_d = dram("piece_d", (2 * K,), I32)
        keep_d = dram("keep_d", (2 * K,))
        loc_d = dram("loc_d", (P, K))
        start_d = dram("start_d", (NP + P,))
        dinv_d = dram("dinv_d", (NP,))
        same_d = dram("same_d", (P, ROW))

        xs = sb("xs", [P, NP])
        hs = sb("hs", [P, NP])
        F = sb("F", [P, WIN])
        srcT = sb("srcT", [P, K + BT], I32)
        locT = sb("locT", [P, K])
        ebi = sb("ebi", [1, K], I32)
        wk = sb("wk", [P, 6 * GW])
        wts = sb("wts", [P, 7 * P])
        ident = sb("ident", [P, P])
        iota_row = sb("iota_row", [P, P])
        lower = sb("lower", [P, P])
        pcol = sb("pcol", [P, 1])
        link_next = sb("link_next", [P, 1])
        same_ends = sb("same_ends", [P, 2 * G])
        piece_idx = sb("piece_idx", [P, 2 * G], I32)
        ones = sb("ones", [1, P])
        brow = sb("brow", [1, 2 * P])
        bcol = sb("bcol", [P, 8])
        idx = sb("idx", [P, 2 * HALF], I32)
        start_i = sb("start_i", [P, NT], I32)
        ald = sb("ald", [P, NT * HEADS])
        dinv = sb("dinv", [P, NT])
        rdeg = sb("rdeg", [P, NT])
        st6 = sb("st6", [P, 5 * P])
        rstd = sb("rstd", [P, NT])
        nmr = sb("nmr", [P, NT])
        sm = sb("sm", [P, 4 * NT])
        PS = ctx.enter_context(nc.psum_tensor("PS", [P, 8 * 512], F32))

        def bank(b, w=512):
            return PS[:, b * 512:b * 512 + w]

        def hslot(n):
            return hs[:, n * ROW:(n + 1) * ROW]

        def fslot(n):
            return F[:, n * ROW:(n + 1) * ROW]

        row = lambda ap: ap.rearrange("(a n) -> a n", a=1)
        colv = lambda ap: ap.rearrange("(n a) -> n a", a=1)
        gathered = [sig(f"gathered{j}", 0) for j in range(2 * HALF)]
        idx_ready = sig("idx_ready")
        onehot_ready = sig("onehot_ready")
        scaled = sig("scaled")
        summed = sig("summed")
        added = sig("added")
        chain = sig("chain")
        achain = sig("achain")
        loads = sig("loads")
        loads2 = sig("loads2")
        stores = sig("stores")
        pe_a = sig("pe_a")
        pe_b = sig("pe_b")
        pe_c = sig("pe_c")
        act_a = sig("act_a")
        act_b = sig("act_b")
        act_c = sig("act_c")
        dve_a = sig("dve_a")
        dve_b = sig("dve_b")
        dve_c = sig("dve_c")
        pool_a = sig("pool_a")
        pe_t, pe_z, pe_m, pe_d = (sig(n) for n in ("pe_t", "pe_z", "pe_m", "pe_d"))
        ohT_ready, h1_ready, msg_ready, msum_ready, sidx_ready, picked_rows, q_made, dups_made = (
            sig(n) for n in ("ohT_ready", "h1_ready", "msg_ready", "msum_ready", "sidx_ready", "picked_rows", "q_made",
                             "dups_made"))
        packed, turned, loc_rows, softmax_step, exped, w_turned, w_ready, ends_kept, pieces_kept, ald_in = (
            sig(n) for n in ("packed", "turned", "loc_rows", "softmax_step", "exped", "w_turned", "w_ready", "ends_kept",
                             "pieces_kept", "ald_in"))
        scattered = [sig(f"scattered{a}", 0) for a in range(AGG)]
        idx_taken = sig("idx_taken")
        spread = sig("spread", 0)
        picked = sig("picked", 0)
        half_in = [sig(f"half_in{b}", 0) for b in range(2)]
        half_out = [sig(f"half_out{b}") for b in range(2)]
        more_in = [sig(f"more_in{b}") for b in range(4)]

        def linker(eng, s=chain):
            def link(ins):
                s.at += 1
                ins.then_inc(s.sem, 1)
                eng.wait_ge(s.sem, s.at)
            return link

        with nc.Block() as block:
            @block.sync
            def _(sp):
                for s in signals:
                    if s.at:
                        sp.sem_inc(s.sem, LEAD)

        dstI, srcI = hslot(0).bitcast(I32), hslot(1).bitcast(I32)
        dstF, srcF, locF = hslot(2), hslot(3), hslot(4)
        ebB, junk = hslot(5), hslot(6)
        same = hslot(6)
        prevI = idx[:, 0:1]
        locA, loc_plain = wk[:, 0:K], wk[:, K:2 * K]
        small = lambda n: wk[:, 2 * K + 2 * n * G:2 * K + 2 * (n + 1) * G]
        ends_flat, piece_no, piece_to, piece_i = small(0), small(1), small(2), small(3).bitcast(I32)
        ends_dst = ends_flat.rearrange("p (g e) -> p g e", e=2)
        to_end, ends_up = (small(4)[:, n * G:(n + 1) * G].unsqueeze(2) for n in range(2))
        flat = lambda a: a.rearrange("(p j) -> p j", p=1)
        with nc.Block() as block:
            @block.gpsimd
            def _(pool):
                nc.gpsimd.iota(st6[:, 0:P].bitcast(I32), pattern=[[1, P]], base=0, channel_multiplier=0).then_inc(pool_a.sem, 1)
                nc.gpsimd.iota(sm[:, 0:NT].bitcast(I32), pattern=[[P, NT]], base=0, channel_multiplier=1).then_inc(pool_a.sem, 1)
                nc.gpsimd.iota(piece_i, pattern=[[1, 2 * G]], base=0, channel_multiplier=2 * G).then_inc(pool_a.sem, 1)

            @block.scalar
            def _(act):
                act.dma_start(attr_d[0:E, :].rearrange("(a b) d -> a (b d)", a=100),
                              t["edge_attr_16"].rearrange("(a b) d -> a (b d)", a=100)).then_inc(stores.sem, 16)
                act.wait_ge(dve_a.sem, dve_a.after(1))
                act.dma_start(attr_d[E:EP, :].rearrange("(a b) d -> a (b d)", a=4),
                              F[0:4, 0:(EP - E) * 4]).then_inc(stores.sem, 16)
                act.dma_start(ex4.rearrange("(p j) h -> p (j h)", p=P), F[:, 0:ROW * HEADS]).then_inc(stores.sem, 16)
                act.dma_start(ex1.rearrange("(p j) h -> p (j h)", p=P), F[:, 0:ROW]).then_inc(stores.sem, 16)
                for a in range(AGG):
                    act.dma_start(agg[a].rearrange("(p i) d -> p (i d)", p=P), F[:, 0:WIN]).then_inc(stores.sem, 16)
                act.dma_start(tab_b[NP:WIN, :], F[:, 0:D]).then_inc(stores.sem, 16)
                act.wait_ge(stores.sem, stores.after(16 * (7 + AGG)))

            @block.sync
            def _(sp):
                sp.wait_ge(dve_b.sem, dve_b.after(4))
                srcf, dstf = t["src"], t["dst"]
                for buf, ap in ((dstI, dstf), (srcI, srcf)):
                    sp.dma_start(buf[0:127, :], ap[0:127 * ROW].rearrange("(p j) -> p j", p=127)).then_inc(loads.sem, 16)
                    sp.dma_start(buf[127:128, 0:LAST], flat(ap[127 * ROW:E])).then_inc(loads.sem, 16)
                sp.dma_start(prevI[1:P, :], dstf[0:127 * ROW].rearrange("(p j) -> p j", j=ROW)[:, ROW - 1:ROW]).then_inc(loads.sem, 16)
                sp.dma_start(xs[:, 0:(NT - 1) * D].rearrange("p (i f) -> p i f", f=D),
                             t["x"][0:(NT - 1) * P, :].rearrange("(i p) f -> p i f", p=P)).then_inc(loads.sem, 16)
                sp.dma_start(xs[0:N - (NT - 1) * P, (NT - 1) * D:NT * D], t["x"][(NT - 1) * P:N, :]).then_inc(loads.sem, 16)
                sp.dma_start(idx[0:P - 1, 1:2], dstf[LAST:E].rearrange("(p j) -> p j", j=ROW)[:, ROW - LAST:ROW - LAST + 1]).then_inc(loads.sem, 16)
                sp.wait_ge(loads.sem, loads.after(16 * 8))
                sp.dma_start(src_d.rearrange("(p g) c -> p (g c)", p=P), srcI).then_inc(loads.sem, 16)
                sp.dma_start(dst_d.rearrange("(p g) c -> p (g c)", p=P), dstI).then_inc(loads.sem, 16)
                sp.wait_ge(loads.sem, loads.after(16 * 10))
                sp.wait_ge(dve_c.sem, dve_c.after(2))
                sp.dma_start(same_d, same).then_inc(stores.sem, 16)
                sp.dma_start(keep_d.rearrange("(p n) -> p n", p=P), same_ends[:, :]).then_inc(stores.sem, 16)
                sp.dma_start(piece_d.rearrange("(p n) -> p n", p=P), piece_i).then_inc(loads2.sem, 16)
                sp.dma_start(eb_i_d, st6[0:G, 4 * P:5 * P].bitcast(I32)).then_inc(loads2.sem, 16)
                sp.dma_start(eb_f_d, st6[0:G, 3 * P:4 * P]).then_inc(loads2.sem, 16)
                sp.wait_ge(loads2.sem, loads2.after(48))
                sp.dma_start(piece_idx[:, :].unsqueeze(2), piece_d.rearrange("(m c x) -> c m x", c=P, x=1)).then_inc(loads2.sem, 16)
                sp.dma_start(ebi[0:1, :], eb_i_d.rearrange("(a g) p -> a (g p)", a=1)).then_inc(loads2.sem, 16)
                sp.dma_start(ebB, eb_f_d.rearrange("(a g) p -> a (g p)", a=1).broadcast_to([P, K])).then_inc(loads2.sem, 16)
                sp.wait_ge(dve_b.sem, dve_b.after(4 + G))
                sp.dma_start(loc_d, loc_plain).then_inc(loads2.sem, 16)
                sp.wait_ge(loads2.sem, loads2.after(112))

            @block.vector
            def _(v):
                link = linker(v)
                v.memset(F[:, :], 0.0).then_inc(dve_a.sem, 1)
                v.memset(dstI[96:128, LAST:], N).then_inc(dve_b.sem, 1)
                v.memset(srcI[96:128, LAST:], N).then_inc(dve_b.sem, 1)
                v.memset(idx[:, 0:2], -1).then_inc(dve_b.sem, 1)
                v.memset(xs[:, (NT - 1) * D:], 0.0).then_inc(dve_b.sem, 1)
                v.memset(ones[:, :], 1.0)
                v.memset(srcT[:, K:], 0)
                v.wait_ge(pool_a.sem, pool_a.after(3))
                v.tensor_copy(iota_row[:, :], st6[:, 0:P].bitcast(I32))
                link(v.tensor_copy(sm[:, NT:2 * NT], sm[:, 0:NT].bitcast(I32)))
                link(v.tensor_copy(pcol[:, :], sm[:, NT:NT + 1]))
                v.tensor_scalar(lower[:, :], iota_row[:, :], pcol[:, 0:1], None, ALU.is_lt)
                link(v.tensor_scalar(ident[:, :], iota_row[:, :], pcol[:, 0:1], None, ALU.is_equal))
                v.wait_ge(loads.sem, loads.after(16 * 8))
                v.tensor_copy(srcF, srcI)
                v.tensor_copy(st6[:, 2 * P:2 * P + 2], idx[:, 0:2])
                link(v.tensor_copy(dstF, dstI))
                v.tensor_tensor(link_next[:, :], dstF[:, ROW - 1:ROW], st6[:, 2 * P + 1:2 * P + 2], ALU.is_equal)
                v.tensor_tensor(same[:, 1:], dstF[:, 1:], dstF[:, :-1], ALU.is_equal)
                v.tensor_tensor(same[:, 0:1], dstF[:, 0:1], st6[:, 2 * P:2 * P + 1], ALU.is_equal)
                first = dstF.rearrange("p (g c) -> p g c", c=P)[:, :, 0:1]
                v.tensor_tensor(locF.rearrange("p (g c) -> p g c", c=P), dstF.rearrange("p (g c) -> p g c", c=P),
                                first.broadcast_to([P, G, P]), ALU.subtract)
                last = dstF.rearrange("p (g c) -> p g c", c=P)[:, :, P - 1:P]
                ends = same_ends[:, :].rearrange("p (g e) -> p g e", e=2)
                v.tensor_tensor(ends[:, :, 1:2], last, first, ALU.is_equal)
                v.tensor_copy(ends_dst[:, :, 0:1], first)
                v.tensor_copy(ends_dst[:, :, 1:2], last)
                link(v.tensor_copy(st6[:, P:P + G], first.rearrange("p g c -> p (g c)")))
                link(v.tensor_copy(ends[:, :, 0:1], same.rearrange("p (g c) -> p g c", c=P)[:, :, 0:1]))
                loc3, locA3 = (a.rearrange("p (g c) -> p g c", c=P) for a in (locF, locA))
                last_loc = loc3[:, :, P - 1:P]
                link(v.tensor_scalar(to_end, last_loc, 0.0, None, ALU.is_gt))
                link(v.scalar_tensor_tensor(ends_up, last_loc, float(1 - P), to_end, ALU.add, ALU.mult))
                link(v.tensor_tensor(locA3, loc3, last_loc.broadcast_to([P, G, P]), ALU.is_equal))
                link(v.tensor_tensor(locA3, locA3, ends_up.broadcast_to([P, G, P]), ALU.mult))
                link(v.tensor_tensor(locA3, loc3, locA3, ALU.subtract))
                link(v.tensor_copy(piece_no, piece_i))
                link(v.tensor_scalar(piece_no, piece_no, float(NP), None, ALU.add))
                link(v.tensor_tensor(piece_to, piece_no, ends_flat, ALU.subtract))
                link(v.tensor_tensor(piece_to[:, 0:2 * G - 1], piece_to[:, 0:2 * G - 1], same_ends[:, 1:], ALU.mult))
                link(v.tensor_tensor(piece_to[:, 2 * G - 1:], piece_to[:, 2 * G - 1:], link_next[:, :], ALU.mult))
                link(v.tensor_tensor(piece_to, piece_to, ends_flat, ALU.add))
                link(v.tensor_copy(piece_i, piece_to))
                v.nop().then_inc(dve_c.sem, 1)
                v.wait_ge(pe_a.sem, pe_a.after(1))
                v.tensor_copy(st6[0:G, 4 * P:5 * P].bitcast(I32), PS[0:G, 0:P])
                link(v.tensor_copy(st6[0:G, 3 * P:4 * P], PS[0:G, 0:P]))
                v.nop().then_inc(dve_c.sem, 1)
                for g in range(G):
                    b = 1 + g % 3
                    v.wait_ge(pe_b.sem, pe_b.after(g + 1))
                    v.tensor_copy(loc_plain[:, g * P:(g + 1) * P], PS[:, b * 1024:b * 1024 + P])
                    v.tensor_copy(locT[:, g * P:(g + 1) * P], PS[:, b * 1024 + P:b * 1024 + 2 * P])
                    link(v.tensor_copy(srcT[:, g * P:(g + 1) * P], PS[:, b * 1024 + 512:b * 1024 + 512 + P]))
                    v.nop().then_inc(dve_b.sem, 1)

            @block.tensor
            def _(pe):
                pe.wait_ge(dve_c.sem, dve_c.after(1))
                pe.transpose(PS[0:G, 0:P], st6[:, P:P + G], ident[:, :]).then_inc(pe_a.sem, 1)
                for g in range(G):
                    b = 1 + g % 3
                    if g >= 3:
                        pe.wait_ge(dve_b.sem, dve_b.after(4 + g - 2))
                    pe.transpose(PS[:, b * 1024:b * 1024 + P], locF[:, g * P:(g + 1) * P], ident[:, :])
                    pe.transpose(PS[:, b * 1024 + P:b * 1024 + 2 * P], locA[:, g * P:(g + 1) * P], ident[:, :])
                    pe.transpose(PS[:, b * 1024 + 512:b * 1024 + 512 + P], srcF[:, g * P:(g + 1) * P], ident[:, :]).then_inc(pe_b.sem, 1)
        pool_a.passed(3); dve_a.passed(1); dve_b.passed(4 + G); dve_c.passed(2); pe_a.passed(1); pe_b.passed(G)
        loads.passed(16 * 10); loads2.passed(112); stores.passed(16 * (7 + AGG))
        if stop <= 0: return

        nodeid = sm[:, NT:2 * NT]
        cnt, cnt2 = sm[:, 2 * NT:3 * NT], sm[:, 3 * NT:4 * NT]
        tix = ald[:, 0:NT].bitcast(I32)
        rows = F[:, 0:2 * GRP * P].bitcast(I32)
        ji = junk
        with nc.Block() as block:
            @block.vector
            def _(v):
                link = linker(v)
                with v.Fori(0, NG) as i:
                    for j in range(GRP):
                        c = i * GRP + j
                        v.tensor_scalar(junk, ebB, nodeid[:, bass.ds(c, 1)], 0.0, ALU.is_lt, ALU.add,
                                        accum_out=cnt[:, bass.ds(c, 1)]).then_inc(dve_a.sem, 1)
                        v.wait_ge(dve_a.sem, dve_a.after(c + 1))
                link(v.tensor_scalar(cnt, cnt, -1.0, 0.0, ALU.add, ALU.max))
                link(v.tensor_copy(tix, cnt))
                with v.Fori(0, NG // 2) as i:
                    for b in range(2):
                        q = i * 2 + b
                        v.wait_ge(half_in[b].sem, half_in[b].after(i * (16 * GRP)))
                        v.tensor_copy(idx[:, b * HALF:b * HALF + GRP], tix[:, bass.ds(q * GRP, GRP)]).then_inc(idx_ready.sem, 1)
                    for b in range(2):
                        q = i * 2 + b
                        v.wait_ge(half_in[b].sem, half_in[b].after((i + 1) * (16 * GRP)))
                        for j in range(GRP):
                            c = q * GRP + j
                            v.tensor_scalar(junk[:, 0:P], rows[:, (b * GRP + j) * P:(b * GRP + j + 1) * P],
                                            nodeid[:, bass.ds(c, 1)], 0.0, ALU.is_lt, ALU.add,
                                            accum_out=cnt2[:, bass.ds(c, 1)]).then_inc(dve_b.sem, 1)
                            v.wait_ge(dve_b.sem, dve_b.after(c + 1))
                link(v.scalar_tensor_tensor(cnt2, cnt, float(P), cnt2, ALU.mult, ALU.add))
                v.memset(wk[:, 0:P], 0.0)
                link(v.tensor_copy(start_i[:, :], cnt2))
                v.nop().then_inc(dve_c.sem, 1)
                v.wait_ge(pe_a.sem, pe_a.after(1))
                startT = wk[0:NT, P:2 * P]
                link(v.tensor_copy(startT, PS[0:NT, 0:P]))
                v.nop().then_inc(dve_c.sem, 1)
                v.wait_ge(loads2.sem, loads2.after(16))
                degT = wk[0:NT, 3 * P:4 * P]
                link(v.tensor_tensor(degT, wk[0:NT, 2 * P:3 * P], startT, ALU.subtract))
                link(v.tensor_scalar(wk[0:NT, 4 * P:5 * P], degT, 0.0, 1.0, ALU.max, ALU.add))
                link(v.tensor_scalar(degT, degT, 1.0, None, ALU.max))
                v.nop().then_inc(dve_c.sem, 1)
                v.wait_ge(act_a.sem, act_a.after(1))
                v.reciprocal(wk[0:NT, 5 * P:6 * P], wk[0:NT, 4 * P:5 * P])
                link(v.reciprocal(degT, degT))
                v.nop().then_inc(dve_c.sem, 1)
                v.wait_ge(pe_a.sem, pe_a.after(2))
                v.tensor_copy(dinv[:, :], PS[:, 1024:1024 + NT])
                v.tensor_copy(rdeg[:, :], PS[:, 2048:2048 + NT])

            @block.scalar
            def _(act):
                act.wait_ge(dve_c.sem, dve_c.after(3))
                act.activation(wk[0:NT, 4 * P:5 * P], wk[0:NT, 4 * P:5 * P], ACT.Sqrt).then_inc(act_a.sem, 1)

            @block.tensor
            def _(pe):
                pe.wait_ge(dve_c.sem, dve_c.after(1))
                pe.transpose(PS[0:NT, 0:P], cnt2, ident[:, :]).then_inc(pe_a.sem, 1)
                pe.wait_ge(dve_c.sem, dve_c.after(4))
                pe.transpose(PS[:, 1024:1024 + NT], wk[0:NT, 5 * P:6 * P], ident[0:NT, 0:NT])
                pe.transpose(PS[:, 2048:2048 + NT], wk[0:NT, 3 * P:4 * P], ident[0:NT, 0:NT]).then_inc(pe_a.sem, 1)

            @block.sync
            def _(sp):
                sp.wait_ge(dve_c.sem, dve_c.after(2))
                sp.dma_start(start_d[0:NP].rearrange("(i p) -> i p", p=P), wk[0:NT, P:2 * P]).then_inc(loads.sem, 16)
                sp.dma_start(flat(start_d[NP:NP + P]), wk[0:1, 0:P]).then_inc(loads.sem, 16)
                sp.wait_ge(loads.sem, loads.after(32))
                sp.dma_start(wk[0:NT, 2 * P:3 * P], start_d[1:NP + 1].rearrange("(i p) -> i p", p=P)).then_inc(loads2.sem, 16)
                sp.wait_ge(dve_c.sem, dve_c.after(4))
                sp.dma_start(dinv_d.rearrange("(i p) -> i p", p=P), wk[0:NT, 5 * P:6 * P]).then_inc(stores.sem, 16)
                sp.wait_ge(stores.sem, stores.after(16))

            @block.gpsimd
            def _(pool):
                with pool.Fori(0, NG // 2) as i:
                    for b in range(2):
                        pool.wait_ge(idx_ready.sem, idx_ready.after(i * 2 + b + 1))
                        pool.wait_ge(dve_b.sem, dve_b.after(i * (2 * GRP)))
                        pool.sem_inc(idx_taken.sem, 1)
                        for j in range(GRP):
                            pool.indirect_dma_start(rows[:, (b * GRP + j) * P:(b * GRP + j + 1) * P], None, dst_d,
                                                    bass.IndirectOffsetOnAxis(idx[:, b * HALF + j:b * HALF + j + 1], 0))\
                                .then_inc(half_in[b].sem, 16)
        dve_a.passed(NT); dve_b.passed(NT); dve_c.passed(4); act_a.passed(1); pe_a.passed(2)
        idx_ready.passed(NG); loads.passed(32); loads2.passed(16); stores.passed(16)
        for s in half_in: s.passed(16 * GRP * (NG // 2))
        if stop <= 1: return

        def layer_norm(src, dst, func):
            st = st6[:, 0:NT * 6].rearrange("p (i s) -> p i s", s=6)
            col = lambda n: st[:, :, n:n + 1].rearrange("p i s -> p (i s)")
            a, b = sm[:, 0:NT], sm[:, 2 * NT:3 * NT]
            with nc.Block() as block:
                @block.vector
                def _(v):
                    link = linker(v)
                    with v.Fori(0, NG) as i:
                        for j in range(GRP):
                            c = i * GRP + j
                            v.bn_stats(st6[:, bass.ds(c * 6, 6)], src[:, bass.ds(c * D, D)]).then_inc(dve_a.sem, 1)
                    v.wait_ge(dve_a.sem, dve_a.after(NT))
                    v.tensor_tensor(a, col(1), col(4), ALU.add)
                    v.tensor_tensor(b, col(1), col(4), ALU.subtract)
                    link(v.tensor_tensor(rstd[:, :], col(2), col(5), ALU.add))
                    link(v.tensor_tensor(b, b, b, ALU.mult))
                    link(v.tensor_scalar(rstd[:, :], rstd[:, :], 1.0 / D, EPS, ALU.mult, ALU.add))
                    link(v.scalar_tensor_tensor(rstd[:, :], b, 0.25, rstd[:, :], ALU.mult, ALU.add))
                    v.nop().then_inc(dve_b.sem, 1)
                    v.wait_ge(act_a.sem, act_a.after(1))
                    link(v.reciprocal(rstd[:, :], rstd[:, :]))
                    link(v.scalar_tensor_tensor(nmr[:, :], a, -0.5, rstd[:, :], ALU.mult, ALU.mult))
                    v.nop().then_inc(dve_b.sem, 1)

                @block.scalar
                def _(act):
                    act.wait_ge(dve_b.sem, dve_b.after(1))
                    act.activation(rstd[:, :], rstd[:, :], ACT.Sqrt).then_inc(act_a.sem, 1)
                    act.wait_ge(dve_b.sem, dve_b.after(2))
                    with act.Fori(0, NG) as i:
                        for j in range(GRP):
                            c = i * GRP + j
                            act.activation(dst[:, bass.ds(c * D, D)], src[:, bass.ds(c * D, D)], func,
                                           bias=nmr[:, bass.ds(c, 1)], scale=rstd[:, bass.ds(c, 1)])
            dve_a.passed(NT); dve_b.passed(2); act_a.passed(1)

        hT = [wk[:, b * GW:(b + 1) * GW] for b in range(2)]
        ost = [wk[:, (2 + b) * GW:(3 + b) * GW] for b in range(2)]
        psA = [PS[:, b * 2048:b * 2048 + GW] for b in range(2)]
        psB = [PS[:, b * 2048 + 1024:b * 2048 + 1024 + GW] for b in range(2)]
        W = [wts[:, n * P:(n + 1) * P] for n in range(7)]

        group = lambda a: a.rearrange("p (i f) -> p i f", f=P)

        def tile_of(buf, j, w=P):
            return buf[:, j * w:(j + 1) * w]

        def rows_of(table, q):
            return table[bass.ds(q * GW, GW), 0:D].rearrange("(i p) f -> p i f", p=P)

        def project(weight, table, from_f=False, bias=None, scale=False, init_f=False, al=None, heads=0,
                    ald_table=None):
            with nc.Block() as block:
                @block.tensor
                def _(pe):
                    with pe.Fori(0, NG // 2) as i:
                        for b in range(2):
                            q = i * 2 + b
                            if not from_f:
                                pe.wait_ge(pool_a.sem, pool_a.after(q + 1))
                                pe.wait_ge(act_a.sem, act_a.after(q - 1))
                                if init_f:
                                    pe.wait_ge(dve_c.sem, dve_c.after(q - 1))
                                if al is not None:
                                    pe.wait_ge(dve_b.sem, dve_b.after(q - 1))
                                for j in range(GRP):
                                    last = pe.transpose(tile_of(psA[b], j), tile_of(stage, j), ident[:, :])
                                last.then_inc(pe_a.sem, 1)
                            pe.wait_ge(act_a.sem, act_a.after(q + 1))
                            pe.wait_ge(dve_a.sem, dve_a.after(q - 1))
                            for j in range(GRP):
                                last = pe.matmul(tile_of(psB[b], j), tile_of(hT[b], j), weight, start=True, stop=bias is None)
                                if bias is not None:
                                    last = pe.matmul(tile_of(psB[b], j), ones[:, :], bias, start=False, stop=True)
                            last.then_inc(pe_b.sem, 1)
                            if al is not None:
                                pe.wait_ge(dve_b.sem, dve_b.after(q - 1))
                                for j in range(GRP):
                                    c = b * 2048 + j * 2 * heads
                                    last = pe.matmul(PS[:, c:c + 2 * heads], tile_of(hT[b], j), al, start=True, stop=True)
                                last.then_inc(pe_c.sem, 1)
                            if init_f:
                                pe.wait_ge(dve_c.sem, dve_c.after(q - 1))
                                for a, z in ((0, 512), (512, GW)):
                                    last = pe.matmul(psA[b][:, a:z], weight, hT[b][:, a:z], start=True, stop=True)
                                last.then_inc(pe_c.sem, 1)

                @block.gpsimd
                def _(pool):
                    with pool.Fori(0, NG // 2) as i:
                        for b in range(2):
                            q = i * 2 + b
                            if from_f:
                                pool.wait_ge(pe_b.sem, pe_b.after(q - 1))
                                if init_f or al is not None:
                                    pool.wait_ge(pe_c.sem, pe_c.after(q - 1))
                                pool.tensor_copy(hT[b], F[:, bass.ds(q * GW, GW)]).then_inc(act_a.sem, 1)
                            else:
                                pool.wait_ge(pe_a.sem, pe_a.after(q))
                                pool.tensor_copy(stage, hs[:, bass.ds(q * GW, GW)]).then_inc(pool_a.sem, 1)

                @block.scalar
                def _(act):
                    if not from_f:
                        with act.Fori(0, NG // 2) as i:
                            for b in range(2):
                                q = i * 2 + b
                                act.wait_ge(pe_a.sem, pe_a.after(q + 1))
                                act.wait_ge(pe_b.sem, pe_b.after(q - 1))
                                if init_f or al is not None:
                                    act.wait_ge(pe_c.sem, pe_c.after(q - 1))
                                act.copy(hT[b], psA[b]).then_inc(act_a.sem, 1)

                @block.vector
                def _(v):
                    with v.Fori(0, NG // 2) as i:
                        for b in range(2):
                            q = i * 2 + b
                            v.wait_ge(pe_b.sem, pe_b.after(q + 1))
                            v.wait_ge(half_out[b].sem, half_out[b].after(i * 16))
                            if scale:
                                d = dinv[:, bass.ds(q * GRP, GRP)].unsqueeze(2).broadcast_to([P, GRP, P])
                                v.tensor_tensor(group(ost[b]), group(psB[b]), d, ALU.mult).then_inc(dve_a.sem, 1)
                            else:
                                v.tensor_copy(ost[b], psB[b]).then_inc(dve_a.sem, 1)
                            if al is not None:
                                v.wait_ge(pe_c.sem, pe_c.after(q + 1))
                                both = PS[:, b * 2048:b * 2048 + GRP * 2 * heads].rearrange("p (i h) -> p i h", h=2 * heads)
                                cols = bass.ds(q * GRP * heads, GRP * heads)
                                v.tensor_copy(als[:, cols].rearrange("p (i h) -> p i h", h=heads), both[:, :, 0:heads])
                                v.tensor_copy(ald[:, cols].rearrange("p (i h) -> p i h", h=heads), both[:, :, heads:])\
                                    .then_inc(dve_b.sem, 1)
                            if init_f:
                                v.wait_ge(pe_c.sem, pe_c.after(q + 1))
                                v.wait_ge(more_in[0].sem, more_in[0].after((q + 1) * 16))
                                v.tensor_tensor(F[:, bass.ds(q * GW, GW)], psA[b], dB, ALU.mult).then_inc(dve_c.sem, 1)

                @block.sync
                def _(sp):
                    with sp.Fori(0, NG // 2) as i:
                        for b in range(2):
                            q = i * 2 + b
                            if init_f:
                                sp.wait_ge(dve_c.sem, dve_c.after(q))
                                sp.dma_start(dB, row(dinv_d[bass.ds(q * GW, GW)]).broadcast_to([P, GW])).then_inc(more_in[0].sem, 16)
                            sp.wait_ge(dve_a.sem, dve_a.after(q + 1))
                            sp.dma_start(rows_of(table, q), group(ost[b])).then_inc(half_out[b].sem, 16)
                    for b in range(2):
                        sp.wait_ge(half_out[b].sem, half_out[b].after(16 * (NG // 2)))
                    if al is not None:
                        sp.wait_ge(dve_b.sem, dve_b.after(NG))
                        for tb, buf in ((table[:, D:], als), (ald_table, ald)):
                            sp.dma_start(tb.rearrange("(i p) h -> p i h", p=P),
                                         buf[:, 0:NT * heads].rearrange("p (i h) -> p i h", h=heads)).then_inc(stores.sem, 16)
                        sp.wait_ge(stores.sem, stores.after(32))
            act_a.passed(NG)
            if not from_f:
                pool_a.passed(NG)
                pe_a.passed(NG)
            pe_b.passed(NG)
            dve_a.passed(NG)
            for s in half_out:
                s.passed(16 * (NG // 2))
            if al is not None:
                pe_c.passed(NG)
                dve_b.passed(NG)
                stores.passed(32)
            if init_f:
                pe_c.passed(NG)
                dve_c.passed(NG)
                more_in[0].passed(16 * NG)

        def bring(pool, table, to, free, ready=pool_a):
            with pool.Fori(0, NG // 2) as i:
                for b in range(2):
                    q = i * 2 + b
                    pool.wait_ge(free.sem, free.after(q - 1))
                    pool.tensor_copy(to[b], table[:, bass.ds(q * GW, GW)]).then_inc(ready.sem, 1)

        als = st6
        dB = wk[:, 4 * GW:5 * GW]
        stage = wk[:, 5 * GW:6 * GW]
        gbuf = [wk[:, j * P:(j + 1) * P] for j in range(2 * HALF)]
        onehot = [wk[:, (2 * HALF + j) * P:(2 * HALF + j + 1) * P] for j in range(2 * HALF)]

        def aggregate(table, clear=False):
            with nc.Block() as block:
                @block.scalar
                def _(act):
                    with act.Fori(0, EI) as i:
                        for b in range(2):
                            k0 = i * (2 * HALF) + b * HALF
                            act.wait_ge(summed.sem, summed.after(k0 - HALF))
                            act.copy(idx[:, b * HALF:(b + 1) * HALF], srcT[:, bass.ds(k0, HALF)]).then_inc(idx_ready.sem, 1)

                @block.gpsimd
                def _(pool):
                    with pool.Fori(0, EI) as i:
                        for b in range(2):
                            pool.wait_ge(idx_ready.sem, idx_ready.after(i * 2 + b + 1))
                            pool.sem_inc(idx_taken.sem, 1)
                            for j in range(b * HALF, (b + 1) * HALF):
                                pool.indirect_dma_start(gbuf[j], None, table, bass.IndirectOffsetOnAxis(idx[:, j:j + 1], 0))\
                                    .then_inc(gathered[j].sem, 16)

                @block.tensor
                def _(pe):
                    with pe.Fori(0, EI) as i:
                        for j in range(2 * HALF):
                            k = i * (2 * HALF) + j
                            pe.wait_ge(gathered[j].sem, gathered[j].after((i + 1) * 16))
                            pe.wait_ge(onehot_ready.sem, onehot_ready.after(k + 1))
                            pe.wait_ge(added.sem, added.after(k - 7))
                            pe.matmul(bank(j % 8, P), gbuf[j], onehot[j], start=True, stop=True).then_inc(summed.sem, 1)

                @block.vector
                def _(v):
                    if clear:
                        linker(v)(v.memset(F[:, :], 0.0))
                    with v.Fori(0, EI) as i:
                        for b in range(2):
                            k0 = i * (2 * HALF) + b * HALF
                            v.wait_ge(summed.sem, summed.after(k0 - HALF))
                            for j in range(HALF):
                                v.tensor_scalar(onehot[b * HALF + j], iota_row[:, :], locT[:, bass.ds(k0 + j, 1)], None,
                                                ALU.is_equal).then_inc(onehot_ready.sem, 1)
                            _, first_dst = nc.values_load_multi_w_load_instructions(
                                ebi[0:1, bass.ds(k0, HALF)], engines=[mybir.EngineType.DVE], min_val=0, max_val=NP,
                                skip_runtime_bounds_check_because="dst holds node numbers")
                            for j in range(HALF):
                                cols = F[:, bass.ds(first_dst[j], P)]
                                v.wait_ge(summed.sem, summed.after(k0 + j + 1))
                                v.wait_ge(added.sem, added.after(k0 + j))
                                v.tensor_tensor(cols, cols, bank((b * HALF + j) % 8, P), ALU.add).then_inc(added.sem, 1)
            for s in gathered:
                s.passed(16 * EI)
            summed.passed(K)
            added.passed(K)
            onehot_ready.passed(K)
            idx_ready.passed(2 * EI)

        def attention(heads, table, ald_table, ex, whole_rows):
            R = heads * BT
            TW = D + heads
            raw = hs[:, 0:ROW * heads]
            held = [F[:, h * ROW:(h + 1) * ROW] for h in range(heads)]
            same = hs[:, ROW * HEADS:ROW * (HEADS + 1)]
            alh = wk[:, 0:heads]
            first_dst = wk[:, P:P + 1].bitcast(I32)
            gt = [hs[:, s * BT * TW:(s + 1) * BT * TW].rearrange("p (j f) -> p j f", f=TW) for s in range(2)]
            kept = hs[:, NP - 2 * K:]
            used = [2 * HALF * P]

            def in_wk(width):
                used[0] += width
                return wk[:, used[0] - width:used[0]]

            onehot = [wk[:, j * P:(j + 1) * P] for j in range(2 * HALF)]
            bidx = [in_wk(BT).bitcast(I32) for _ in range(2)]
            pack_al, pack_loc, loc_r, ald_r, z, t1, p_r, w_r, same_r = (in_wk(P) for _ in range(9))
            md, cut_r, w_c, ends = in_wk(2 * P), in_wk(P + 1), in_wk(P), in_wk(NBT * 4)
            m_r, d_r = md[:, 0:P], md[:, P:2 * P]
            heads_of = lambda a: a[:, 0:R].rearrange("p (h j) -> p h j", j=BT)

            with nc.Block() as block:
                @block.gpsimd
                def _(pool):
                    for i in range(NT):
                        n = min(P, N + 1 - i * P)
                        pool.indirect_dma_start(ex, bass.IndirectOffsetOnAxis(start_i[0:n, i:i + 1], 0),
                                                ald[0:n, i * heads:(i + 1) * heads], None).then_inc(spread.sem, 16)
                    pool.wait_ge(loads.sem, loads.after(32))
                    pool.sem_inc(idx_taken.sem, 1)
                    pool.indirect_dma_start(alh, None, ald_table,
                                            bass.IndirectOffsetOnAxis(first_dst, 0)).then_inc(picked.sem, 16)

                @block.sync
                def _(sp):
                    sp.dma_start(same, same_d).then_inc(loads.sem, 16)
                    sp.dma_start(first_dst, dst_d.rearrange("(p g) c -> p (g c)", p=P)[:, 0:1]).then_inc(loads.sem, 16)
                    sp.wait_ge(spread.sem, spread.after(16 * NT))
                    sp.dma_start(raw, ex.rearrange("(p j) h -> p (j h)", p=P)).then_inc(ald_in.sem, 16)
                    rows = ald_e[0:K * heads, :].rearrange("(g u h j) c -> u h j g c", u=P // BT, h=heads, j=BT)
                    for h in range(heads):
                        sp.wait_ge(dve_a.sem, dve_a.after(h + 1))
                        for u in range(P // BT):
                            sp.dma_start(rows[u, h], held[h][u * BT:(u + 1) * BT, :].rearrange("j (g c) -> j g c", c=P))\
                                .then_inc(stores.sem, 16)
                    sp.wait_ge(stores.sem, stores.after(16 * heads * (P // BT)))

                @block.vector
                def _(v):
                    v.wait_ge(picked.sem, picked.after(16))
                    v.wait_ge(ald_in.sem, ald_in.after(16))
                    for h in range(heads):
                        ad = raw.rearrange("p (j h) -> p j h", h=heads)[:, :, h]
                        v.tensor_tensor_scan(held[h], same, ad, alh[:, h:h + 1], ALU.mult, ALU.add).then_inc(dve_a.sem, 1)
            spread.passed(16 * NT)
            loads.passed(32)
            picked.passed(16)
            ald_in.passed(16)
            dve_a.passed(heads)
            stores.passed(16 * heads * (P // BT))

            MASKS, SUMMED_AL, LOGITS, MAX, SHIFTED, SUM, WEIGHTS, STEPS = 2, 3, 4, 6, 7, 9, 11, 11
            QH = BT // HALF
            with nc.Block() as block:
                @block.scalar
                def _(act):
                    act.copy(bidx[0], srcT[:, 0:BT]).then_inc(idx_ready.sem, 1)
                    with act.Fori(0, NBT // 2) as i:
                        for s in range(2):
                            n = i * 2 + s
                            act.wait_ge(half_in[1 - s].sem, half_in[1 - s].after((i + s) * (16 * BT)))
                            act.copy(bidx[1 - s], srcT[:, bass.ds((n + 1) * BT, BT)]).then_inc(idx_ready.sem, 1)
                            act.wait_ge(turned.sem, turned.after(n * 2))
                            act.copy(heads_of(pack_loc), locT[:, bass.ds(n * BT, BT)].unsqueeze(1).broadcast_to([P, heads, BT]))\
                                .then_inc(packed.sem, 1)
                            act.wait_ge(turned.sem, turned.after(n * 2 + 1))
                            act.wait_ge(softmax_step.sem, softmax_step.after((n - 1) * STEPS + MASKS))
                            act.copy(loc_r[0:R, :], bank(4, P)[0:R, :]).then_inc(loc_rows.sem, 1)
                            act.wait_ge(half_in[s].sem, half_in[s].after((i + 1) * (16 * BT)))
                            act.copy(heads_of(pack_al), gt[s][:, :, D:].rearrange("p j h -> p h j")).then_inc(packed.sem, 1)
                            act.wait_ge(softmax_step.sem, softmax_step.after(n * STEPS + SHIFTED))
                            act.activation(p_r[0:R, :], p_r[0:R, :], ACT.Exp).then_inc(exped.sem, 1)
                            act.wait_ge(softmax_step.sem, softmax_step.after(n * STEPS + SUM))
                            act.copy(ends[0:R, bass.ds(n * 4, 4)].rearrange("p (w e) -> p w e", e=2),
                                     md[0:R, :].rearrange("p (w c) -> p w c", c=P)[:, :, 0:P:P - 1]).then_inc(ends_kept.sem, 1)
                            act.wait_ge(w_turned.sem, w_turned.after(n + 1))
                            act.copy(w_c[:, 0:R], bank(6, R)).then_inc(w_ready.sem, 1)
                            for h in range(QH):
                                q = n * QH + h
                                act.wait_ge(summed.sem, summed.after(q + 1))
                                act.copy(kept.rearrange("p (e k) -> p k e", e=2)[:, bass.ds(q * HALF, HALF), :],
                                         PS[:, h % 2 * 1024:(h % 2 + 1) * 1024].rearrange("p (j c) -> p j c", c=P)[:, :, 0:P:P - 1])\
                                    .then_inc(pieces_kept.sem, 1)

                @block.gpsimd
                def _(pool):
                    with pool.Fori(0, NBT // 2) as i:
                        for s in range(2):
                            n = i * 2 + s
                            pool.wait_ge(idx_ready.sem, idx_ready.after(n + 1))
                            for h in range(QH):
                                pool.wait_ge(summed.sem, summed.after(n * QH + h - 2 * QH + 1))
                                pool.sem_inc(idx_taken.sem, 1)
                                for j in range(h * HALF, (h + 1) * HALF):
                                    pool.indirect_dma_start(gt[s][:, j, :], None, table,
                                                            bass.IndirectOffsetOnAxis(bidx[s][:, j:j + 1], 0))\
                                        .then_inc(half_in[s].sem, 16)

                @block.sync
                def _(sp):
                    with sp.Fori(0, NBT) as n:
                        sp.wait_ge(softmax_step.sem, softmax_step.after((n - 1) * STEPS + SUMMED_AL))
                        sp.dma_start(ald_r[0:R, :], ald_e[bass.ds(n * R, R), :]).then_inc(ald_in.sem, 16)
                    sp.wait_ge(ald_in.sem, ald_in.after(16 * NBT))

                @block.tensor
                def _(pe):
                    with pe.Fori(0, NBT // 2) as i:
                        for s in range(2):
                            n = i * 2 + s
                            pe.wait_ge(packed.sem, packed.after(2 * n + 1))
                            pe.wait_ge(loc_rows.sem, loc_rows.after(n))
                            pe.transpose(bank(4, P)[0:R, :], pack_loc[:, 0:R], ident[:, :]).then_inc(turned.sem, 1)
                            pe.wait_ge(packed.sem, packed.after(2 * n + 2))
                            pe.wait_ge(softmax_step.sem, softmax_step.after((n - 1) * STEPS + SUMMED_AL))
                            pe.transpose(bank(5, P)[0:R, :], pack_al[:, 0:R], ident[:, :]).then_inc(turned.sem, 1)
                            pe.wait_ge(softmax_step.sem, softmax_step.after(n * STEPS + WEIGHTS))
                            pe.wait_ge(w_ready.sem, w_ready.after(n))
                            pe.transpose(bank(6, P), w_r, ident[:, :]).then_inc(w_turned.sem, 1)
                            for h in range(QH):
                                b, q = h % 2, n * QH + h
                                pe.wait_ge(added.sem, added.after((q - 1) * HALF))
                                pe.wait_ge(pieces_kept.sem, pieces_kept.after(q - 1))
                                for j in range(HALF):
                                    if heads > 1:
                                        pe.wait_ge(scaled.sem, scaled.after(q * HALF + j + 1))
                                    pe.wait_ge(onehot_ready.sem, onehot_ready.after(q * HALF + j + 1))
                                    last = pe.matmul(PS[:, (b * HALF + j) * P:(b * HALF + j + 1) * P],
                                                     gt[s][:, h * HALF + j, 0:D], onehot[b * HALF + j], start=True, stop=True)
                                last.then_inc(summed.sem, 1)

                @block.vector
                def _(v):
                    v.memset(same_r[0:R, 0:1], 0.0)
                    v.memset(w_r, 0.0)
                    v.memset(cut_r[0:R, 0:1], -BIG)
                    v.memset(cut_r[0:R, P:P + 1], -BIG)
                    linker(v)(v.memset(F[:, :], 0.0))
                    with v.Fori(0, NBT // 2) as i:
                        for s in range(2):
                            n = i * 2 + s

                            def onehots(h):
                                v.wait_ge(summed.sem, summed.after(n * QH + h - 1))
                                for j in range(h * HALF, (h + 1) * HALF):
                                    w, op = (w_c[:, j:j + 1], ALU.mult) if heads == 1 else (None, ALU.bypass)
                                    v.tensor_scalar(onehot[j % (2 * HALF)], iota_row[:, :], locT[:, bass.ds(n * BT + j, 1)], w,
                                                    ALU.is_equal, op).then_inc(onehot_ready.sem, 1)

                            def scale(h):
                                for j in range(h * HALF, (h + 1) * HALF):
                                    g3 = gt[s][:, j, 0:D].rearrange("p (h d) -> p h d", h=heads)
                                    w3 = heads_of(w_c)[:, :, j:j + 1].broadcast_to([P, heads, D // heads])
                                    v.tensor_tensor(g3, g3, w3, ALU.mult).then_inc(scaled.sem, 1)

                            def add(h):
                                k0 = n * BT + h * HALF
                                _, first_dst = nc.values_load_multi_w_load_instructions(
                                    ebi[0:1, bass.ds(k0, HALF)], engines=[mybir.EngineType.DVE], min_val=0, max_val=NP,
                                    skip_runtime_bounds_check_because="dst holds node numbers")
                                v.wait_ge(pieces_kept.sem, pieces_kept.after(n * QH + h + 1))
                                for j in range(HALF):
                                    cols = F[:, bass.ds(first_dst[j] + 1, P - 2)]
                                    v.wait_ge(added.sem, added.after(k0 + j))
                                    c = (h % 2 * HALF + j) * P
                                    v.tensor_tensor(cols, cols, PS[:, c + 1:c + P - 1], ALU.add).then_inc(added.sem, 1)

                            steps = [0]

                            def step(ins):
                                steps[0] += 1
                                ins.then_inc(softmax_step.sem, 1)
                                v.wait_ge(softmax_step.sem, softmax_step.after(n * STEPS + steps[0]))

                            v.wait_ge(loc_rows.sem, loc_rows.after(n + 1))
                            step(v.tensor_tensor(same_r[0:R, 1:], loc_r[0:R, 1:], loc_r[0:R, :-1], ALU.is_equal))
                            step(v.tensor_scalar(cut_r[0:R, 1:P], same_r[0:R, 1:], -1.0, BIG, ALU.add, ALU.mult))
                            if heads > 1:
                                onehots(0)
                            v.wait_ge(turned.sem, turned.after(2 * n + 2))
                            v.wait_ge(ald_in.sem, ald_in.after((n + 1) * 16))
                            step(v.tensor_tensor(z[0:R, :], bank(5, P)[0:R, :], ald_r[0:R, :], ALU.add))
                            step(v.scalar_tensor_tensor(z[0:R, :], z[0:R, :], SLOPE, z[0:R, :], ALU.mult, ALU.max))
                            step(v.tensor_tensor_scan(t1[0:R, :], cut_r[0:R, 0:P], z[0:R, :], -BIG, ALU.add, ALU.max))
                            v.wait_ge(ends_kept.sem, ends_kept.after(n))
                            step(v.tensor_tensor_scan(m_r[0:R, ::-1], cut_r[0:R, 1:][:, ::-1], t1[0:R, ::-1], -BIG, ALU.add, ALU.max))
                            step(v.tensor_tensor(p_r[0:R, :], z[0:R, :], m_r[0:R, :], ALU.subtract))
                            if heads > 1:
                                onehots(1)
                            v.wait_ge(exped.sem, exped.after(n + 1))
                            step(v.tensor_tensor_scan(t1[0:R, :], same_r[0:R, :], p_r[0:R, :], 0.0, ALU.mult, ALU.add))
                            step(v.tensor_tensor_scan(d_r[0:R, ::-1], cut_r[0:R, 1:][:, ::-1], t1[0:R, ::-1], -BIG, ALU.add, ALU.max))
                            step(v.reciprocal(t1[0:R, :], d_r[0:R, :]))
                            v.wait_ge(w_turned.sem, w_turned.after(n))
                            step(v.tensor_tensor(w_r[0:R, :], p_r[0:R, :], t1[0:R, :], ALU.mult))
                            v.wait_ge(w_ready.sem, w_ready.after(n + 1))
                            if heads > 1:
                                scale(0)
                                scale(1)
                            else:
                                onehots(0)
                                onehots(1)
                            for h in range(2, QH):
                                add(h - 2)
                                onehots(h)
                                if heads > 1:
                                    scale(h)
                            add(QH - 2)
                            add(QH - 1)
            idx_ready.passed(NBT + 1)
            packed.passed(2 * NBT)
            turned.passed(2 * NBT)
            softmax_step.passed(STEPS * NBT)
            for one in (loc_rows, exped, ends_kept, w_turned, w_ready):
                one.passed(NBT)
            summed.passed(NBT * QH)
            pieces_kept.passed(NBT * QH)
            ald_in.passed(16 * NBT)
            onehot_ready.passed(K)
            added.passed(K)
            if heads > 1:
                scaled.passed(K)
            for one in half_in:
                one.passed(16 * BT * (NBT // 2))

            WD = 2 * G
            used = [0]
            sq = in_wk(heads * NBT)
            pieces, runs, sums = in_wk(heads * WD), in_wk(heads * WD), in_wk(heads * WD)
            t1, cut, cut_next, carry, crow = (in_wk(w) for w in (WD, WD, WD, 4 * HEADS, 3 * P))
            crow = crow[0:HEADS, :]
            zh = [pieces[:, h * WD:(h + 1) * WD] for h in range(heads)]
            runh = [runs[:, h * WD:(h + 1) * WD] for h in range(heads)]
            in_tiles = lambda a: a.rearrange("p (h g e) -> p h g e", g=G, e=2)
            alone = same_ends[:, :].rearrange("p (g e) -> p g e", e=2)[:, :, 1]
            spread_c = in_wk(2 * K)
            coef = spread_c.rearrange("p (g e c) -> p g e c", e=2, c=P)
            run = spread_c
            weighed, keep_b = hs[:, 0:2 * K], hs[:, 2 * K:4 * K]
            piece_rows = weighed.rearrange("p (m f) -> p m f", f=D)
            whole = [hs[:, 2 * K + b * GW:2 * K + (b + 1) * GW] for b in range(2)]
            with nc.Block() as block:
                @block.sync
                def _(sp):
                    sp.dma_start(keep_b, row(keep_d).broadcast_to([P, 2 * K])).then_inc(loads.sem, 16)
                    for u in range(P // BT):
                        for h in range(heads):
                            sp.dma_start(sq[u * BT:(u + 1) * BT, h * NBT:(h + 1) * NBT].rearrange("j (g w) -> j g w", w=4),
                                         ends[h * BT:(h + 1) * BT, :].rearrange("j (g u w) -> j g u w", u=P // BT, w=4)[:, :, u])\
                                .then_inc(loads.sem, 16)
                    sp.wait_ge(loads.sem, loads.after(16 * (1 + heads * (P // BT))))

                @block.vector
                def _(v):
                    link = linker(v)
                    link(v.tensor_scalar(cut, same_ends[:, :], -1.0, BIG, ALU.add, ALU.mult))
                    link(v.tensor_copy(cut_next[:, 0:WD - 1], cut[:, 1:]))
                    link(v.tensor_scalar(cut_next[:, WD - 1:WD], link_next[:, :], -1.0, BIG, ALU.add, ALU.mult))
                    v.wait_ge(loads.sem, loads.after(16 * (1 + heads * (P // BT))))
                    for h in range(heads):
                        of_w = sq[:, h * NBT:(h + 1) * NBT].rearrange("p (g w e) -> p g w e", w=2, e=2)
                        v.tensor_copy(in_tiles(pieces)[:, h], of_w[:, :, 0])
                        link(v.tensor_copy(in_tiles(sums)[:, h], of_w[:, :, 1]))
                        link(v.tensor_scalar(t1[:, 0:G], alone, -1.0, -1.0, ALU.mult, ALU.subtract))
                        link(v.tensor_tensor(in_tiles(sums)[:, h, :, 1], in_tiles(sums)[:, h, :, 1], t1[:, 0:G], ALU.mult))
            loads.passed(16 * (1 + heads * (P // BT)))

            def carries(v, link, whole, backward, keep_op, keep, none):
                link(v.tensor_copy(carry[:, HEADS:HEADS + heads], whole.broadcast_to([P, heads])))
                v.nop().then_inc(dve_b.sem, 1)
                v.wait_ge(pe_b.sem, pe_b.after(keep["n"] + 1))
                link(v.memset(crow[0:heads, :], none))
                if keep_op == ALU.mult:
                    link(v.tensor_copy(crow[0:heads, 0:P], PS[0:heads, 512:512 + P]))
                else:
                    link(v.tensor_scalar(crow[0:heads, 0:P], PS[0:heads, 512:512 + P], -1.0, BIG, ALU.add, ALU.mult))
                op1 = ALU.add if keep_op == ALU.mult else ALU.max
                if backward:
                    link(v.tensor_tensor_scan(crow[0:heads, P:2 * P][:, ::-1], crow[0:heads, 0:P][:, ::-1],
                                              PS[0:heads, 0:P][:, ::-1], none, keep_op, op1))
                    into = crow[0:heads, P + 1:2 * P + 1]
                else:
                    link(v.tensor_tensor_scan(crow[0:heads, P + 1:2 * P + 1], crow[0:heads, 0:P], PS[0:heads, 0:P],
                                              none, keep_op, op1))
                    into = crow[0:heads, P:2 * P]
                v.nop().then_inc(dve_b.sem, 1)
                v.wait_ge(pe_b.sem, pe_b.after(keep["n"] + 2))
                keep["n"] += 2
                link(v.tensor_copy(carry[:, 0:heads], PS[:, 1024:1024 + heads]))

            def segment_total(kind):
                hold, op0, op1, none = {"max": (cut, ALU.add, ALU.max, -BIG), "sum": (same_ends[:, :], ALU.mult, ALU.add, 0.0)}[kind]
                with nc.Block() as block:
                    @block.tensor
                    def _(pe):
                        for r in range(2):
                            pe.wait_ge(dve_b.sem, dve_b.after(2 * r + 1))
                            for n in range(2):
                                last = pe.transpose(PS[0:heads, n * 512:n * 512 + P], carry[:, n * HEADS:n * HEADS + heads],
                                                    ident[:, :])
                            last.then_inc(pe_b.sem, 1)
                            pe.wait_ge(dve_b.sem, dve_b.after(2 * r + 2))
                            c = P + 1 if r else P
                            pe.transpose(PS[:, 1024:1024 + heads], crow[0:heads, c:c + P], ident[0:heads, 0:heads])\
                                .then_inc(pe_b.sem, 1)

                    @block.vector
                    def _(v):
                        link = linker(v)
                        keep = {"n": 0}
                        link(v.tensor_reduce(carry[:, 2 * HEADS:2 * HEADS + 1], same_ends[:, :], AX_X, ALU.min))
                        link(v.tensor_reduce(carry[:, 2 * HEADS + 1:2 * HEADS + 2], cut_next, AX_X, ALU.min))
                        link(v.tensor_scalar(carry[:, 2 * HEADS + 1:2 * HEADS + 2], carry[:, 2 * HEADS + 1:2 * HEADS + 2],
                                             0.0, None, ALU.is_ge))
                        for h in range(heads):
                            link(v.tensor_tensor_scan(t1, hold, zh[h], none, op0, op1))
                            link(v.tensor_copy(carry[:, h:h + 1], t1[:, WD - 1:WD]))
                        carries(v, link, carry[:, 2 * HEADS:2 * HEADS + 1], False, op0, keep, none)
                        for h in range(heads):
                            link(v.tensor_tensor_scan(runh[h], hold, zh[h], carry[:, h:h + 1], op0, op1))
                        for h in range(heads):
                            link(v.tensor_tensor_scan(t1[:, ::-1], cut_next[:, ::-1], runh[h][:, ::-1], -BIG, ALU.add, ALU.max))
                            link(v.tensor_copy(carry[:, h:h + 1], t1[:, 0:1]))
                        carries(v, link, carry[:, 2 * HEADS + 1:2 * HEADS + 2], True, ALU.add, keep, -BIG)
                        for h in range(heads):
                            link(v.tensor_tensor_scan(runh[h][:, ::-1], cut_next[:, ::-1], runh[h][:, ::-1],
                                                      carry[:, h:h + 1], ALU.add, ALU.max))
                            if kind == "max":
                                link(v.tensor_tensor(zh[h], zh[h], runh[h], ALU.subtract))
                            else:
                                link(v.tensor_scalar(runh[h], runh[h], 1e-16, None, ALU.add))
                                link(v.reciprocal(runh[h], runh[h]))
                                link(v.tensor_tensor(zh[h], zh[h], runh[h], ALU.mult))
                dve_b.passed(4)
                pe_b.passed(4)

            segment_total("max")
            with nc.Block() as block:
                @block.scalar
                def _(act):
                    act.activation(pieces, pieces, ACT.Exp).then_inc(act_a.sem, 1)

                @block.vector
                def _(v):
                    v.wait_ge(act_a.sem, act_a.after(1))
                    v.tensor_tensor(pieces, pieces, sums, ALU.mult)
            act_a.passed(1)
            segment_total("sum")

            with nc.Block() as block:
                @block.tensor
                def _(pe):
                    pe.wait_ge(dve_b.sem, dve_b.after(1))
                    for n in range(2 * G):
                        if n >= 8:
                            pe.wait_ge(dve_c.sem, dve_c.after(n - 7))
                        pe.transpose(bank(n % 8, P), coef[:, n // 2, n % 2], ident[:, :]).then_inc(pe_a.sem, 1)
                    pe.wait_ge(dve_b.sem, dve_b.after(2))
                    for n in range(2 * G):
                        pe.wait_ge(dve_c.sem, dve_c.after(2 * G + n - 7))
                        pe.transpose(bank(n % 8, P), run[:, n * P:(n + 1) * P], ident[:, :]).then_inc(pe_a.sem, 1)

                @block.vector
                def _(v):
                    link = linker(v)
                    for n in range(2 * G):
                        last = v.tensor_copy(coef[:, n // 2, n % 2].rearrange("p (h d) -> p h d", h=heads),
                                             in_tiles(pieces)[:, :, n // 2, n % 2].unsqueeze(2).broadcast_to([P, heads, D // heads]))
                    link(last)
                    v.nop().then_inc(dve_b.sem, 1)
                    for n in range(2 * G):
                        g, e = n // 2, n % 2
                        v.wait_ge(pe_a.sem, pe_a.after(n + 1))
                        v.tensor_tensor(weighed.rearrange("p (t n) -> p t n", n=2 * G)[:, :, n],
                                        kept[:, e * K + g * P:e * K + (g + 1) * P], bank(n % 8, P), ALU.mult).then_inc(dve_c.sem, 1)
                    v.wait_ge(dve_c.sem, dve_c.after(2 * G))
                    v.wait_ge(pe_a.sem, pe_a.after(2 * G))
                    link(v.tensor_tensor_scan(run, keep_b, weighed, 0.0, ALU.mult, ALU.add))
                    v.nop().then_inc(dve_b.sem, 1)
                    for n in range(2 * G):
                        v.wait_ge(pe_a.sem, pe_a.after(2 * G + n + 1))
                        v.tensor_copy(piece_rows[:, n], bank(n % 8, P)).then_inc(dve_c.sem, 1)

                @block.gpsimd
                def _(pool):
                    for n in range(2 * G):
                        pool.wait_ge(dve_c.sem, dve_c.after(2 * G + n + 1))
                        pool.indirect_dma_start(whole_rows, bass.IndirectOffsetOnAxis(piece_idx[:, n:n + 1], 0),
                                                piece_rows[:, n], None).then_inc(spread.sem, 16)
                    pool.wait_ge(spread.sem, spread.after(32 * G))
                    pool.sem_inc(idx_taken.sem, 1)
            dve_b.passed(2)
            dve_c.passed(4 * G)
            pe_a.passed(4 * G)
            spread.passed(32 * G)

            with nc.Block() as block:
                @block.sync
                def _(sp):
                    with sp.Fori(0, NG // 2) as i:
                        for b in range(2):
                            q = i * 2 + b
                            sp.wait_ge(pe_a.sem, pe_a.after(q - 1))
                            sp.dma_start(group(whole[b]), rows_of(whole_rows, q)).then_inc(more_in[b].sem, 16)

                @block.tensor
                def _(pe):
                    with pe.Fori(0, NG // 2) as i:
                        for b in range(2):
                            q = i * 2 + b
                            pe.wait_ge(more_in[b].sem, more_in[b].after(i * 16 + 16))
                            pe.wait_ge(dve_a.sem, dve_a.after(q - 1))
                            for j in range(GRP):
                                last = pe.transpose(tile_of(psA[b], j), tile_of(whole[b], j), ident[:, :])
                            last.then_inc(pe_a.sem, 1)

                @block.vector
                def _(v):
                    with v.Fori(0, NG // 2) as i:
                        for b in range(2):
                            q = i * 2 + b
                            cols = F[:, bass.ds(q * GW, GW)]
                            v.wait_ge(pe_a.sem, pe_a.after(q + 1))
                            v.tensor_tensor(cols, cols, psA[b], ALU.add).then_inc(dve_a.sem, 1)
            pe_a.passed(NG)
            dve_a.passed(NG)
            for b in range(2):
                more_in[b].passed(16 * (NG // 2))

        group = lambda a: a.rearrange("p (i f) -> p i f", f=P)

        def load_weights(items, rows=()):
            with nc.Block() as block:
                @block.sync
                def _(sp):
                    for dst, s in items:
                        sp.dma_start(dst, s).then_inc(loads.sem, 16)
                    sp.wait_ge(loads.sem, loads.after(16 * len(items)))
            loads.passed(16 * len(items))

        def attention_columns(w_sb, wt_sb, a_sb, al_sb, heads):
            with nc.Block() as block:
                @block.tensor
                def _(pe):
                    pe.transpose(bank(0, P), w_sb, ident[:, :]).then_inc(pe_a.sem, 1)
                    pe.wait_ge(dve_a.sem, dve_a.after(1))
                    pe.matmul(bank(1, 2 * heads), wt_sb, a_sb, start=True, stop=True).then_inc(pe_a.sem, 1)

                @block.vector
                def _(v):
                    v.wait_ge(pe_a.sem, pe_a.after(1))
                    v.tensor_copy(wt_sb, bank(0, P)).then_inc(dve_a.sem, 1)
                    v.wait_ge(pe_a.sem, pe_a.after(2))
                    v.tensor_copy(al_sb, bank(1, 2 * heads))
            pe_a.passed(2)
            dve_a.passed(1)

        def bias_relu():
            with nc.Block() as block:
                @block.scalar
                def _(act):
                    act.activation(F[:, 0:NP], F[:, 0:NP], ACT.Relu, bias=bcol[:, 0:1])

        layer_norm(xs, hs, ACT.Relu)
        with nc.Block() as block:
            @block.vector
            def _(v):
                v.memset(W[2][:, 0:2 * HEADS], 0.0).then_inc(dve_a.sem, 1)

            @block.sync
            def _(sp):
                sp.dma_start(W[0], t["L0_gnn_W1"]).then_inc(loads.sem, 16)
                sp.wait_ge(dve_a.sem, dve_a.after(1))
                for n, name in enumerate(("L0_gnn_a_src1", "L0_gnn_a_dst1")):
                    for h in range(HEADS):
                        sp.dma_start(W[2][h * HID:(h + 1) * HID, n * HEADS + h:n * HEADS + h + 1], colv(t[name][h, :])).then_inc(loads.sem, 16)
                sp.wait_ge(loads.sem, loads.after(16 * (1 + 2 * HEADS)))
        dve_a.passed(1)
        loads.passed(16 * (1 + 2 * HEADS))
        attention_columns(W[0], W[1], W[2][:, 0:2 * HEADS], W[3][:, 0:2 * HEADS], HEADS)
        project(W[0], tab_g1, al=W[3][:, 0:2 * HEADS], heads=HEADS, ald_table=ald_rows)
        if stop <= 2: return
        attention(HEADS, tab_g1, ald_rows, ex4, whole_rows[0])
        if stop <= 4: return
        load_weights([(W[0], t["L0_gnn_W2"]), (W[2][:, 0:1], colv(t["L0_gnn_a_src2"][0, :])),
                      (W[2][:, 1:2], colv(t["L0_gnn_a_dst2"][0, :])), (bcol[:, 0:1], colv(t["L0_gnn_b1"])),
                      (brow[:, 0:D], row(t["L0_gnn_b2"]))])
        attention_columns(W[0], W[1], W[2][:, 0:2], W[3][:, 0:2], 1)
        bias_relu()
        project(W[0], tab_g2, from_f=True, al=W[3][:, 0:2], heads=1, ald_table=ald_rows1)
        attention(1, tab_g2, ald_rows1, ex1, whole_rows[1])
        if stop <= 5: return

        tmp, ex_ = ost, [wk[:, (4 + b) * GW:(5 + b) * GW] for b in range(2)]
        with nc.Block() as block:
            @block.gpsimd
            def _(pool):
                bring(pool, F, hT, pe_a)

            @block.sync
            def _(sp):
                sp.dma_start(locT[:, :], loc_d).then_inc(loads.sem, 16)
                for a in range(2):
                    sp.dma_start(agg[a].rearrange("(p i) d -> p (i d)", p=P), agg[2].rearrange("(p i) d -> p (i d)", p=P))\
                        .then_inc(loads.sem, 16)
                sp.wait_ge(loads.sem, loads.after(48))

            @block.tensor
            def _(pe):
                with pe.Fori(0, NG // 2) as i:
                    for b in range(2):
                        q = i * 2 + b
                        pe.wait_ge(pool_a.sem, pool_a.after(q + 1))
                        pe.wait_ge(dve_a.sem, dve_a.after(q - 1))
                        for j in range(GRP):
                            pe.matmul(tile_of(psB[b], j), tile_of(hT[b], j), ident[:, :], start=True, stop=False)
                            last = pe.matmul(tile_of(psB[b], j), ones[:, :], brow[:, 0:D], start=False, stop=True)
                        last.then_inc(pe_a.sem, 1)

            @block.scalar
            def _(act):
                with act.Fori(0, NG // 2) as i:
                    for b in range(2):
                        q = i * 2 + b
                        act.wait_ge(dve_a.sem, dve_a.after(q + 1))
                        act.activation(ex_[b], tmp[b], ACT.Exp).then_inc(act_a.sem, 1)
                        act.wait_ge(dve_b.sem, dve_b.after(q + 1))
                        act.activation(sm[:, b * NT + GRP:b * NT + 2 * GRP], sm[:, b * NT + 2 * GRP:b * NT + 3 * GRP], ACT.Ln)\
                            .then_inc(act_b.sem, 1)

            @block.vector
            def _(v):
                link = linker(v)
                with v.Fori(0, NG // 2) as i:
                    for b in range(2):
                        q = i * 2 + b
                        mx, lns, ssum = (sm[:, b * NT + n * GRP:b * NT + (n + 1) * GRP] for n in range(3))
                        wide = lambda a: a.unsqueeze(2).broadcast_to([P, GRP, P])
                        v.wait_ge(pe_a.sem, pe_a.after(q + 1))
                        v.tensor_reduce(mx, group(psB[b]), AX_X, ALU.max).then_inc(dve_c.sem, 1)
                        v.wait_ge(dve_c.sem, dve_c.after(q * 3 + 1))
                        v.tensor_tensor(group(tmp[b]), group(psB[b]), wide(mx), ALU.subtract).then_inc(dve_a.sem, 1)
                        v.wait_ge(act_a.sem, act_a.after(q + 1))
                        v.tensor_reduce(ssum, group(ex_[b]), AX_X, ALU.add).then_inc(dve_b.sem, 1)
                        v.wait_ge(act_b.sem, act_b.after(q + 1))
                        v.tensor_tensor(group(tmp[b]), group(tmp[b]), wide(lns), ALU.subtract).then_inc(dve_c.sem, 1)
                        v.wait_ge(dve_c.sem, dve_c.after(q * 3 + 2))
                        xg = xs[:, bass.ds(q * GW, GW)]
                        v.tensor_tensor(xg, xg, tmp[b], ALU.add).then_inc(dve_c.sem, 1)
                        v.wait_ge(dve_c.sem, dve_c.after(q * 3 + 3))
        for s in (dve_a, act_a, act_b, dve_b, pe_a, pool_a):
            s.passed(NG)
        dve_c.passed(3 * NG)
        loads.passed(48)
        if stop <= 6: return

        layer_norm(xs, hs, ACT.Relu)
        QT = 4
        NQ = K // QT
        place = [0]

        def in_f(width, dt=F32):
            a = F[:, place[0]:place[0] + width]
            place[0] += width
            return a.bitcast(dt) if dt != F32 else a

        QW = QT * P
        two = lambda width, dt=F32: [in_f(width, dt) for _ in range(2)]
        a_rows, b_win, src_rows, attrs = two(QW), two(QW), two(QW, I32), two(QT * 16)
        oh, ohT, eq, attrT, h1, msg, msum = two(QW), two(QW), two(QW), two(P), two(QW), two(QW), two(QW)
        seen, dups, delta, picks = in_f(QW), two(QT), two(QT), two(QT)
        wc = [in_f(P) for _ in range(QT)]
        sidx = two(QT, I32)
        trash = in_f(1)
        with nc.Block() as block:
            @block.vector
            def _(v):
                for w_ in wc:
                    last = v.memset(w_[0:QT * 16, :], 0.0)
                last.then_inc(dve_a.sem, 1)
                v.tensor_scalar(trash, pcol[:, :], float(NP), None, ALU.add)

            @block.sync
            def _(sp):
                for dst, s in ((W[0], t["L1_gnn_eW1"][0:D, :]), (W[1], t["L1_gnn_eW1"][D:2 * D, :]),
                               (W[2], t["L1_gnn_eW2"]), (brow[:, 0:D], row(t["L1_gnn_eb1"])),
                               (brow[:, D:2 * D], row(t["L1_gnn_eb2"]))):
                    sp.dma_start(dst, s).then_inc(loads.sem, 16)
                sp.wait_ge(dve_a.sem, dve_a.after(1))
                for u in range(QT):
                    sp.dma_start(wc[u][16 * u:16 * (u + 1), :], t["L1_gnn_eW1"][2 * D:, :]).then_inc(loads.sem, 16)
                sp.wait_ge(loads.sem, loads.after(16 * (5 + QT)))
        dve_a.passed(1)
        loads.passed(16 * (5 + QT))
        project(W[0], tab, bias=brow[:, 0:D])
        project(W[1], tab_b)

        src_by_row = src_d.rearrange("(p g) c -> g p c", g=G)
        attr_by_row = attr_d.rearrange("(p g c) d -> g c p d", g=G, c=P)
        with nc.Block() as block:
            @block.sync
            def _(sp):
                with sp.Fori(0, G) as g:
                    with sp.Fori(0, P // (2 * QT)) as r:
                        i = g * (P // (2 * QT)) + r
                        _, first_dst = nc.values_load_multi_w_load_instructions(
                            ebi[0:1, bass.ds(i * (2 * QT), 2 * QT)], engines=[mybir.EngineType.SP], min_val=0, max_val=NP,
                            skip_runtime_bounds_check_because="dst holds node numbers")
                        for b in range(2):
                            n = i * 2 + b
                            p0 = r * (2 * QT) + b * QT
                            sp.wait_ge(q_made.sem, q_made.after((n - 1) * QT))
                            sp.dma_start(src_rows[b].rearrange("p (u c) -> p u c", u=QT),
                                         src_by_row[bass.ds(g, 1), bass.ds(p0, QT), :].broadcast_to([P, QT, P]))\
                                .then_inc(more_in[2 + b].sem, 16)
                            sp.wait_ge(pe_t.sem, pe_t.after(n - 1))
                            sp.dma_start(attrs[b].rearrange("c (u d) -> c u d", u=QT),
                                         attr_by_row[bass.ds(g, 1), :, bass.ds(p0, QT), :].rearrange("g c p d -> (g c) p d"))\
                                .then_inc(more_in[2 + b].sem, 16)
                            sp.wait_ge(pe_z.sem, pe_z.after(n - 1))
                            for u in range(QT):
                                sp.dma_start(tile_of(b_win[b], u), tab_b[bass.ds(first_dst[b * QT + u], P), :])\
                                    .then_inc(more_in[b].sem, 16)

            @block.gpsimd
            def _(pool):
                def gather(n, b):
                    pool.wait_ge(idx_ready.sem, idx_ready.after(n + 1))
                    pool.sem_inc(idx_taken.sem, 1)
                    for u in range(QT):
                        pool.indirect_dma_start(tile_of(a_rows[b], u), None, tab,
                                                bass.IndirectOffsetOnAxis(idx[:, b * QT + u:b * QT + u + 1], 0))\
                            .then_inc(gathered[b * QT + u].sem, 16)

                def scatter(n, b):
                    pool.wait_ge(msum_ready.sem, msum_ready.after(n + 1))
                    pool.wait_ge(sidx_ready.sem, sidx_ready.after(n + 1))
                    for u in range(QT):
                        pool.wait_ge(scattered[u].sem, scattered[u].after(n * 16))
                        pool.sem_inc(idx_taken.sem, 1)
                        pool.indirect_dma_start(agg[u], bass.IndirectOffsetOnAxis(sidx[b][:, u:u + 1], 0),
                                                tile_of(msum[b], u), None, compute_op=ALU.add).then_inc(scattered[u].sem, 16)

                gather(0, 0)
                gather(1, 1)
                with pool.Fori(0, NQ // 2 - 1) as i:
                    for b in range(2):
                        gather(i * 2 + b + 2, b)
                        scatter(i * 2 + b, b)
                scatter(NQ - 2, 0)
                scatter(NQ - 1, 1)
                for u in range(QT):
                    pool.wait_ge(scattered[u].sem, scattered[u].after(NQ * 16))

            def steps(eng, step):
                step(0, 0, 0)
                with eng.Fori(0, NQ // 2 - 1) as i:
                    step(i * 2 + 1, 1, i)
                    step(i * 2 + 2, 0, i + 1)
                step(NQ - 1, 1, NQ // 2 - 1)
                step(NQ, 0, NQ // 2)

            inside = lambda n: not isinstance(n, int) or n < NQ
            behind = lambda n: not isinstance(n, int) or n > 0

            @block.tensor
            def _(pe):
                def step(n, b, h):
                    if inside(n):
                        pe.wait_ge(onehot_ready.sem, onehot_ready.after(n + 1))
                        pe.wait_ge(more_in[2 + b].sem, more_in[2 + b].after((h + 1) * 32))
                        pe.wait_ge(ohT_ready.sem, ohT_ready.after(n))
                        for u in range(QT):
                            pe.transpose(tile_of(bank(b), u), tile_of(oh[b], u), ident[:, :])
                        pe.transpose(PS[0:QT * 16, 7 * 512:7 * 512 + P], attrs[b], ident[:, :]).then_inc(pe_t.sem, 1)
                    if behind(n):
                        pe.wait_ge(h1_ready.sem, h1_ready.after(n))
                        pe.wait_ge(msg_ready.sem, msg_ready.after(n - 2))
                        for u in range(QT):
                            pe.matmul(tile_of(bank(5 - b), u), tile_of(h1[1 - b], u), W[2], start=True, stop=False)
                            last = pe.matmul(tile_of(bank(5 - b), u), ones[:, :], brow[:, D:2 * D], start=False, stop=True)
                        last.then_inc(pe_m.sem, 1)
                    if inside(n):
                        pe.wait_ge(ohT_ready.sem, ohT_ready.after(n + 1))
                        pe.wait_ge(more_in[b].sem, more_in[b].after((h + 1) * (16 * QT)))
                        pe.wait_ge(h1_ready.sem, h1_ready.after(n - 1))
                        for u in range(QT):
                            pe.wait_ge(gathered[b * QT + u].sem, gathered[b * QT + u].after((h + 1) * 16))
                            z = tile_of(bank(2 + b), u)
                            pe.matmul(z, tile_of(a_rows[b], u), ident[:, :], start=True, stop=False)
                            pe.matmul(z, wc[u][0:QT * 16, :], attrT[b][0:QT * 16, :], start=False, stop=False)
                            last = pe.matmul(z, tile_of(b_win[b], u), tile_of(ohT[b], u), start=False, stop=True)
                        last.then_inc(pe_z.sem, 1)
                    if behind(n):
                        pe.wait_ge(msg_ready.sem, msg_ready.after(n))
                        pe.wait_ge(q_made.sem, q_made.after(n * QT))
                        pe.wait_ge(msum_ready.sem, msum_ready.after(n - 1))
                        for u in range(QT):
                            last = pe.matmul(tile_of(bank(6), u), tile_of(eq[1 - b], u), tile_of(msg[1 - b], u),
                                             start=True, stop=True)
                        last.then_inc(pe_d.sem, 1)
                steps(pe, step)

            @block.scalar
            def _(act):
                def take(n, b):
                    act.wait_ge(pe_z.sem, pe_z.after(n - 1))
                    act.copy(idx[:, b * QT:(b + 1) * QT], srcT[:, bass.ds(n * QT, QT)]).then_inc(idx_ready.sem, 1)

                def step(n, b, h):
                    if isinstance(n, int) and n == 0:
                        take(0, 0)
                        take(1, 1)
                    elif not isinstance(n, int):
                        take(n + 1, 1 - b)
                    if inside(n):
                        act.wait_ge(pe_t.sem, pe_t.after(n + 1))
                        act.wait_ge(pe_z.sem, pe_z.after(n - 1))
                        act.copy(ohT[b], bank(b))
                        act.copy(attrT[b][0:QT * 16, :], PS[0:QT * 16, 7 * 512:7 * 512 + P]).then_inc(ohT_ready.sem, 1)
                    if behind(n):
                        act.wait_ge(pe_m.sem, pe_m.after(n))
                        act.wait_ge(pe_d.sem, pe_d.after(n - 2))
                        act.activation(msg[1 - b], bank(5 - b), ACT.Silu).then_inc(msg_ready.sem, 1)
                    if inside(n):
                        act.wait_ge(pe_z.sem, pe_z.after(n + 1))
                        act.wait_ge(pe_m.sem, pe_m.after(n - 1))
                        act.activation(h1[b], bank(2 + b), ACT.Silu).then_inc(h1_ready.sem, 1)
                steps(act, step)

            @block.vector
            def _(v):
                def step(n, b, h):
                    if inside(n):
                        v.wait_ge(pe_t.sem, pe_t.after(n - 1))
                        for u in range(QT):
                            last = v.tensor_scalar(tile_of(oh[b], u), iota_row[:, :], locT[:, bass.ds(n * QT + u, 1)], None,
                                                   ALU.is_equal)
                        last.then_inc(onehot_ready.sem, 1)
                        v.wait_ge(more_in[2 + b].sem, more_in[2 + b].after((h + 1) * 32))
                        v.wait_ge(pe_d.sem, pe_d.after(n - 1))
                        for u in range(QT):
                            v.tensor_scalar(tile_of(eq[b], u), tile_of(src_rows[b], u), srcT[:, bass.ds(n * QT + u, 1)], None,
                                            ALU.is_equal).then_inc(q_made.sem, 1)
                        v.tensor_scalar(delta[b], srcT[:, bass.ds(n * QT, QT)], trash, None, ALU.subtract)
                        for u in range(QT):
                            v.wait_ge(q_made.sem, q_made.after(n * QT + u + 1))
                            v.scalar_tensor_tensor(tile_of(seen, u), tile_of(eq[b], u), 1.0, lower[:, :], ALU.mult, ALU.mult,
                                                   accum_out=dups[b][:, u:u + 1]).then_inc(dups_made.sem, 1)
                        v.wait_ge(dups_made.sem, dups_made.after((n + 1) * QT))
                        v.scalar_tensor_tensor(picks[b], dups[b], 0.0, delta[b], ALU.is_equal, ALU.mult).then_inc(picked_rows.sem, 1)
                    if behind(n):
                        v.wait_ge(pe_d.sem, pe_d.after(n))
                        v.tensor_copy(msum[1 - b], bank(6)).then_inc(msum_ready.sem, 1)
                    if inside(n):
                        v.wait_ge(picked_rows.sem, picked_rows.after(n + 1))
                        if behind(n):
                            for u in range(QT):
                                v.wait_ge(scattered[u].sem, scattered[u].after((n - 1) * 16))
                        v.tensor_scalar(sidx[b], picks[b], trash, None, ALU.add).then_inc(sidx_ready.sem, 1)
                steps(v, step)
        for s in (pe_t, pe_m, pe_z, pe_d, ohT_ready, h1_ready, msg_ready, msum_ready, sidx_ready, picked_rows, onehot_ready,
                  idx_ready):
            s.passed(NQ)
        for s in (q_made, dups_made):
            s.passed(NQ * QT)
        for s in gathered[0:2 * QT]:
            s.passed(16 * (NQ // 2))
        for s in more_in[0:2]:
            s.passed(16 * QT * (NQ // 2))
        for s in more_in[2:4]:
            s.passed(32 * (NQ // 2))
        if stop <= 7: return

        load_weights([(W[0], t["L1_gnn_nW1"][0:D, :]), (W[1], t["L1_gnn_nW1"][D:2 * D, :]), (W[2], t["L1_gnn_nW2"]),
                      (bcol[:, 0:1], colv(t["L1_gnn_nb1"])), (brow[:, 0:D], row(t["L1_gnn_nb2"]))])
        place[0] = 0
        parts_in = [[in_f(GW) for a in range(AGG)] for b in range(2)]
        aT, uT = two(GW), two(GW)
        with nc.Block() as block:
            @block.sync
            def _(sp):
                with sp.Fori(0, NG // 2) as i:
                    for b in range(2):
                        q = i * 2 + b
                        sp.wait_ge(pe_t.sem, pe_t.after(q - 1))
                        for a in range(AGG):
                            sp.dma_start(group(parts_in[b][a]), rows_of(agg[a], q)).then_inc(more_in[b].sem, 16)

            @block.gpsimd
            def _(pool):
                with pool.Fori(0, NG) as q:
                    pool.wait_ge(pe_a.sem, pe_a.after(q))
                    pool.tensor_copy(stage, hs[:, bass.ds(q * GW, GW)]).then_inc(pool_a.sem, 1)

            @block.vector
            def _(v):
                with v.Fori(0, NG // 2) as i:
                    for b in range(2):
                        q = i * 2 + b
                        v.wait_ge(more_in[b].sem, more_in[b].after((i + 1) * (16 * AGG)))
                        total = parts_in[b][0]
                        for a in range(1, AGG):
                            v.tensor_tensor(total, total, parts_in[b][a], ALU.add).then_inc(dve_a.sem, 1)
                            v.wait_ge(dve_a.sem, dve_a.after(q * (AGG - 1) + a))
                        xg = xs[:, bass.ds(q * GW, GW)]
                        v.tensor_tensor(xg, xg, hs[:, bass.ds(q * GW, GW)], ALU.add).then_inc(dve_b.sem, 1)
                        v.wait_ge(pe_c.sem, pe_c.after(q + 1))
                        v.wait_ge(dve_b.sem, dve_b.after(q + 1))
                        v.tensor_tensor(xg, xg, psB[b], ALU.add).then_inc(dve_c.sem, 1)

            @block.tensor
            def _(pe):
                with pe.Fori(0, NG // 2) as i:
                    for b in range(2):
                        q = i * 2 + b
                        pe.wait_ge(pool_a.sem, pool_a.after(q + 1))
                        pe.wait_ge(act_b.sem, act_b.after(q - 1))
                        for j in range(GRP):
                            last = pe.transpose(tile_of(psA[b], j), tile_of(stage, j), ident[:, :])
                        last.then_inc(pe_a.sem, 1)
                        pe.wait_ge(dve_a.sem, dve_a.after((q + 1) * (AGG - 1)))
                        pe.wait_ge(dve_c.sem, dve_c.after(q - 1))
                        for j in range(GRP):
                            last = pe.transpose(tile_of(psB[b], j), tile_of(parts_in[b][0], j), ident[:, :])
                        last.then_inc(pe_t.sem, 1)
                        pe.wait_ge(act_a.sem, act_a.after(q * 2 + 2))
                        for a, z in ((0, 512), (512, GW)):
                            pe.matmul(psA[b][:, a:z], W[0], hT[b][:, a:z], start=True, stop=False)
                            last = pe.matmul(psA[b][:, a:z], W[1], aT[b][:, a:z], start=False, stop=True)
                        last.then_inc(pe_b.sem, 1)
                        pe.wait_ge(act_b.sem, act_b.after(q + 1))
                        for j in range(GRP):
                            pe.matmul(tile_of(psB[b], j), tile_of(uT[b], j), W[2], start=True, stop=False)
                            last = pe.matmul(tile_of(psB[b], j), ones[:, :], brow[:, 0:D], start=False, stop=True)
                        last.then_inc(pe_c.sem, 1)

            @block.scalar
            def _(act):
                with act.Fori(0, NG // 2) as i:
                    for b in range(2):
                        q = i * 2 + b
                        act.wait_ge(pe_b.sem, pe_b.after(q - 1))
                        act.wait_ge(pe_a.sem, pe_a.after(q + 1))
                        act.copy(hT[b], psA[b]).then_inc(act_a.sem, 1)
                        act.wait_ge(pe_t.sem, pe_t.after(q + 1))
                        act.copy(aT[b], psB[b]).then_inc(act_a.sem, 1)
                        act.wait_ge(pe_b.sem, pe_b.after(q + 1))
                        act.wait_ge(pe_c.sem, pe_c.after(q - 1))
                        act.activation(uT[b], psA[b], ACT.Silu, bias=bcol[:, 0:1]).then_inc(act_b.sem, 1)
        for s in (pe_a, pe_t, pe_b, pe_c, pool_a, dve_b, dve_c, act_b):
            s.passed(NG)
        act_a.passed(2 * NG)
        dve_a.passed((AGG - 1) * NG)
        for s in more_in[0:2]:
            s.passed(16 * AGG * (NG // 2))
        if stop <= 8: return

        def batch_norm():
            chunks = [(c, min(c + 512, N)) for c in range(0, N, 512)]
            bst = wk[:, 5 * GW:5 * GW + 6 * len(chunks)]
            mv, am, cm = bcol[:, 4:6], bcol[:, 6:7], bcol[:, 7:8]
            db2 = [wk[:, (2 + b) * GW:(3 + b) * GW] for b in range(2)]
            with nc.Block() as block:
                @block.sync
                def _(sp):
                    with sp.Fori(0, NG // 2) as i:
                        for b in range(2):
                            q = i * 2 + b
                            sp.wait_ge(dve_a.sem, dve_a.after(q - 1))
                            sp.dma_start(db2[b], row(dinv_d[bass.ds(q * GW, GW)]).broadcast_to([P, GW])).then_inc(more_in[b].sem, 16)

                @block.scalar
                def _(act):
                    with act.Fori(0, NG) as q:
                        act.wait_ge(dve_a.sem, dve_a.after(q + 1))
                        fg = F[:, bass.ds(q * GW, GW)]
                        act.activation(fg, fg, ACT.Identity, bias=bcol[:, 0:1]).then_inc(act_a.sem, 1)
                    act.wait_ge(dve_b.sem, dve_b.after(1))
                    act.activation(am, am, ACT.Sqrt).then_inc(act_b.sem, 1)
                    act.wait_ge(dve_b.sem, dve_b.after(2))
                    act.activation(F[:, 0:NP], F[:, 0:NP], ACT.Relu, bias=cm, scale=am)

                @block.vector
                def _(v):
                    link = linker(v)
                    with v.Fori(0, NG // 2) as i:
                        for b in range(2):
                            q = i * 2 + b
                            fg = F[:, bass.ds(q * GW, GW)]
                            v.wait_ge(more_in[b].sem, more_in[b].after((i + 1) * 16))
                            v.tensor_tensor(fg, fg, db2[b], ALU.mult).then_inc(dve_a.sem, 1)
                    v.wait_ge(act_a.sem, act_a.after(NG))
                    for n, (a, z) in enumerate(chunks):
                        last = v.bn_stats(bst[:, 6 * n:6 * n + 6], F[:, a:z])
                    link(last)
                    link(v.bn_aggr(mv, bst))
                    link(v.tensor_scalar(am, mv[:, 1:2], EPS, None, ALU.add))
                    v.nop().then_inc(dve_b.sem, 1)
                    v.wait_ge(act_b.sem, act_b.after(1))
                    link(v.reciprocal(am, am))
                    link(v.tensor_tensor(am, am, bcol[:, 1:2], ALU.mult))
                    link(v.tensor_tensor(cm, mv[:, 0:1], am, ALU.mult))
                    link(v.tensor_tensor(cm, bcol[:, 2:3], cm, ALU.subtract))
                    v.nop().then_inc(dve_b.sem, 1)
            act_a.passed(NG)
            act_b.passed(1)
            dve_a.passed(NG)
            dve_b.passed(2)
            for s in more_in[0:2]:
                s.passed(16 * (NG // 2))

        layer_norm(xs, hs, ACT.Relu)
        for n, from_f in (("1", False), ("2", True)):
            load_weights([(W[0], t["L2_gnn_W" + n])] +
                         [(bcol[:, m:m + 1], colv(t["L2_gnn_" + name + n])) for m, name in enumerate(("b", "g", "be"))])
            project(W[0], tab, from_f=from_f, scale=True, init_f=True)
            aggregate(tab)
            batch_norm()
        load_weights([(W[0], t["L2_gnn_Wf"]), (brow[:, 0:D], row(t["L2_gnn_bf"]))])
        with nc.Block() as block:
            @block.gpsimd
            def _(pool):
                bring(pool, F, hT, pe_a)

            @block.tensor
            def _(pe):
                with pe.Fori(0, NG // 2) as i:
                    for b in range(2):
                        q = i * 2 + b
                        pe.wait_ge(pool_a.sem, pool_a.after(q + 1))
                        pe.wait_ge(dve_a.sem, dve_a.after(q - 1))
                        for j in range(GRP):
                            pe.matmul(tile_of(psB[b], j), tile_of(hT[b], j), W[0], start=True, stop=False)
                            last = pe.matmul(tile_of(psB[b], j), ones[:, :], brow[:, 0:D], start=False, stop=True)
                        last.then_inc(pe_a.sem, 1)

            @block.vector
            def _(v):
                with v.Fori(0, NG // 2) as i:
                    for b in range(2):
                        q = i * 2 + b
                        v.wait_ge(pe_a.sem, pe_a.after(q + 1))
                        xg = xs[:, bass.ds(q * GW, GW)]
                        v.tensor_tensor(xg, xg, psB[b], ALU.add).then_inc(dve_a.sem, 1)
        for s in (pool_a, pe_a, dve_a):
            s.passed(NG)
        if stop <= 9: return

        layer_norm(xs, hs, ACT.Relu)
        layer_norm(hs, hs, ACT.Identity)
        load_weights([(W[0], t["L3_gnn_W_self"]), (W[1], t["L3_gnn_W_neigh"]), (brow[:, 0:D], row(t["L3_gnn_b"])),
                      (W[2], row(t["L3_gnn_gamma"]).broadcast_to([P, D])), (W[3], row(t["L3_gnn_beta"]).broadcast_to([P, D]))])
        every = lambda a: a.unsqueeze(1).broadcast_to([P, GRP, P])
        with nc.Block() as block:
            @block.vector
            def _(v):
                with v.Fori(0, NG) as q:
                    hg = group(hs[:, bass.ds(q * GW, GW)])
                    v.tensor_tensor(hg, hg, every(W[2]), ALU.mult).then_inc(dve_a.sem, 1)
                    v.wait_ge(dve_a.sem, dve_a.after(q + 1))
                    v.tensor_tensor(hg, hg, every(W[3]), ALU.add).then_inc(dve_b.sem, 1)

            @block.sync
            def _(sp):
                with sp.Fori(0, NG) as q:
                    sp.wait_ge(dve_b.sem, dve_b.after(q + 1))
                    sp.dma_start(rows_of(tab, q), group(hs[:, bass.ds(q * GW, GW)])).then_inc(stores.sem, 16)
                sp.wait_ge(stores.sem, stores.after(16 * NG))
        dve_a.passed(NG)
        dve_b.passed(NG)
        stores.passed(16 * NG)
        aggregate(tab, clear=True)

        fT = [wk[:, (4 + b) * GW:(5 + b) * GW] for b in range(2)]
        with nc.Block() as block:
            @block.gpsimd
            def _(pool):
                with pool.Fori(0, NG // 2) as i:
                    for b in range(2):
                        q = i * 2 + b
                        pool.wait_ge(pe_a.sem, pe_a.after(q - 1))
                        pool.tensor_copy(ost[b], hs[:, bass.ds(q * GW, GW)]).then_inc(pool_a.sem, 1)
                        pool.wait_ge(pe_b.sem, pe_b.after(q - 1))
                        pool.tensor_copy(fT[b], F[:, bass.ds(q * GW, GW)]).then_inc(pool_a.sem, 1)

            @block.tensor
            def _(pe):
                with pe.Fori(0, NG // 2) as i:
                    for b in range(2):
                        q = i * 2 + b
                        pe.wait_ge(pool_a.sem, pool_a.after(q * 2 + 1))
                        pe.wait_ge(dve_a.sem, dve_a.after(q - 1))
                        for j in range(GRP):
                            last = pe.transpose(tile_of(psA[b], j), tile_of(ost[b], j), ident[:, :])
                        last.then_inc(pe_a.sem, 1)
                        pe.wait_ge(act_a.sem, act_a.after(q + 1))
                        pe.wait_ge(pool_a.sem, pool_a.after(q * 2 + 2))
                        pe.wait_ge(dve_c.sem, dve_c.after(q - 1))
                        for j in range(GRP):
                            pe.matmul(tile_of(psB[b], j), tile_of(hT[b], j), W[0], start=True, stop=False)
                            pe.matmul(tile_of(psB[b], j), ones[:, :], brow[:, 0:D], start=False, stop=True)
                        for j in range(GRP):
                            last = pe.matmul(tile_of(psA[b], j), tile_of(fT[b], j), W[1], start=True, stop=True)
                        last.then_inc(pe_b.sem, 1)

            @block.scalar
            def _(act):
                with act.Fori(0, NG // 2) as i:
                    for b in range(2):
                        q = i * 2 + b
                        act.wait_ge(pe_a.sem, pe_a.after(q + 1))
                        act.wait_ge(pe_b.sem, pe_b.after(q - 1))
                        act.copy(hT[b], psA[b]).then_inc(act_a.sem, 1)

            @block.vector
            def _(v):
                with v.Fori(0, NG // 2) as i:
                    for b in range(2):
                        q = i * 2 + b
                        v.wait_ge(pe_b.sem, pe_b.after(q + 1))
                        r3 = rdeg[:, bass.ds(q * GRP, GRP)].unsqueeze(2).broadcast_to([P, GRP, P])
                        xg = xs[:, bass.ds(q * GW, GW)]
                        fg = F[:, bass.ds(q * GW, GW)]
                        v.tensor_tensor(group(fg), group(psA[b]), r3, ALU.mult).then_inc(dve_a.sem, 1)
                        v.tensor_tensor(xg, xg, psB[b], ALU.add).then_inc(dve_c.sem, 1)
                        v.wait_ge(dve_a.sem, dve_a.after(q + 1))
                        v.wait_ge(dve_c.sem, dve_c.after(q + 1))
                        v.tensor_tensor(xg, xg, fg, ALU.add).then_inc(dve_b.sem, 1)

            @block.sync
            def _(sp):
                with sp.Fori(0, NG - 1) as q:
                    sp.wait_ge(dve_b.sem, dve_b.after(q + 1))
                    sp.dma_start(rows_of(out, q), group(xs[:, bass.ds(q * GW, GW)])).then_inc(stores.sem, 16)
                sp.wait_ge(dve_b.sem, dve_b.after(NG))
                c = (NG - 1) * GW
                sp.dma_start(out[c:c + (GRP - 1) * P, :].rearrange("(i p) f -> p i f", p=P),
                             group(xs[:, c:c + (GRP - 1) * P])).then_inc(stores.sem, 16)
                sp.dma_start(out[(NT - 1) * P:N, :], xs[0:N - (NT - 1) * P, (NT - 1) * P:]).then_inc(stores.sem, 16)
                sp.wait_ge(stores.sem, stores.after(16 * (NG + 1)))


_FIELDS = ["x", "src", "dst", "edge_attr_16",
           "L0_gnn_W1", "L0_gnn_a_src1", "L0_gnn_a_dst1", "L0_gnn_b1", "L0_gnn_W2", "L0_gnn_a_src2", "L0_gnn_a_dst2",
           "L0_gnn_b2", "L1_gnn_eW1", "L1_gnn_eb1", "L1_gnn_eW2", "L1_gnn_eb2", "L1_gnn_nW1", "L1_gnn_nb1", "L1_gnn_nW2",
           "L1_gnn_nb2", "L2_gnn_W1", "L2_gnn_b1", "L2_gnn_g1", "L2_gnn_be1", "L2_gnn_W2", "L2_gnn_b2", "L2_gnn_g2",
           "L2_gnn_be2", "L2_gnn_Wf", "L2_gnn_bf", "L3_gnn_gamma", "L3_gnn_beta", "L3_gnn_W_self", "L3_gnn_W_neigh",
           "L3_gnn_b"]


def kernel(**inputs):
    import numpy as np
    import concourse.bacc as bacc
    from concourse.bass_utils import run_bass_kernel_spmd

    nc = bacc.Bacc("TRN2", target_bir_lowering=False, num_devices=1)
    arrays, t = {}, {}
    for name in _FIELDS:
        a = np.ascontiguousarray(inputs[name])
        arrays[f"in_{name}_dram"] = a
        t[name] = nc.dram_tensor(f"in_{name}_dram", a.shape, mybir.dt.from_np(a.dtype), kind="ExternalInput").ap()
    out = nc.dram_tensor("out_0_dram", (N, D), F32, kind="ExternalOutput").ap()
    build(nc, t, out)
    r = run_bass_kernel_spmd(nc, [arrays], core_ids=[0])
    return r.results[0]["out_0_dram"]
```

```python
from contextlib import ExitStack

import concourse.bass as bass
from concourse import mybir

F32 = mybir.dt.float32
I32 = mybir.dt.int32
ALU = mybir.AluOpType
ACT = mybir.ActivationFunctionType
AX_X = mybir.AxisListType.X

P = 128
N = 12500
E = 212500
D = 128
NT = (N + P - 1) // P
NP = NT * P
WIN = NP + P
ROW = 1664
G = ROW // P
K = G * P
EP = K * P
LAST = E - (P - 1) * ROW
GRP = 7
GW = GRP * P
NG = NT // GRP
HALF = 8
EI = K // (2 * HALF)
BT = 32
NBT = K // BT
HEADS = 4
HID = 32
SLOPE = 0.2
BIG = 1e30
EPS = 1e-5
LEAD = 16
AGG = 4


class Signal:

    def __init__(self, sem, at):
        self.sem, self.at = sem, at

    def after(self, n):
        return n + self.at

    def passed(self, n):
        self.at += n


def build(nc, t, out, stop=99):
    ctx = ExitStack()
    with ctx:
        ctx.enter_context(nc.allow_non_contiguous_dma(reason="columns of one element a row, all short"))
        def sb(name, shape, dt=F32):
            return ctx.enter_context(nc.sbuf_tensor(name, shape, dt))

        signals = []

        def sig(name, lead=LEAD):
            signals.append(Signal(ctx.enter_context(nc.semaphore(name)), lead))
            return signals[-1]

        def dram(name, shape, dt=F32):
            return nc.dram_tensor(name, shape, dt, kind="Internal").ap()

        tab = dram("tab", (NP, D))
        tab_b = dram("tab_b", (WIN, D))
        tab_g1 = dram("tab_g1", (NP, D + HEADS))
        tab_g2 = dram("tab_g2", (NP, D + 1))
        ald_e = dram("ald_e", (K * HEADS, P))
        ald_rows = dram("ald_rows", (NP, HEADS))
        ald_rows1 = dram("ald_rows1", (NP, 1))
        ex4 = dram("ex4", (EP, HEADS))
        ex1 = dram("ex1", (EP, 1))
        src_d = dram("src_d", (K, P), I32)
        loc_rows_d = dram("loc_rows_d", (K, P))
        dst_d = dram("dst_d", (K, P), I32)
        attr_d = dram("attr_d", (EP, 16))
        agg_all = [dram(f"agg{a}", (NP + 2 * K, D)) for a in range(AGG)]
        agg = [a[0:WIN, :] for a in agg_all]
        whole_rows = agg_all[0:2]
        eb_i_d = dram("eb_i_d", (G, P), I32)
        eb_f_d = dram("eb_f_d", (G, P))
        piece_d = dram("piece_d", (2 * K,), I32)
        keep_d = dram("keep_d", (2 * K,))
        loc_d = dram("loc_d", (P, K))
        start_d = dram("start_d", (NP + P,))
        dinv_d = dram("dinv_d", (NP,))
        same_d = dram("same_d", (P, ROW))

        xs = sb("xs", [P, NP])
        hs = sb("hs", [P, NP])
        F = sb("F", [P, WIN])
        srcT = sb("srcT", [P, K + BT], I32)
        locT = sb("locT", [P, K])
        ebi = sb("ebi", [1, K], I32)
        wk = sb("wk", [P, 6 * GW])
        wts = sb("wts", [P, 7 * P])
        ident = sb("ident", [P, P])
        iota_row = sb("iota_row", [P, P])
        lower = sb("lower", [P, P])
        pcol = sb("pcol", [P, 1])
        link_next = sb("link_next", [P, 1])
        same_ends = sb("same_ends", [P, 2 * G])
        piece_idx = sb("piece_idx", [P, 2 * G], I32)
        bcol = sb("bcol", [P, 8])
        idx = sb("idx", [P, 2 * HALF], I32)
        start_i = sb("start_i", [P, NT], I32)
        ald = sb("ald", [P, NT * HEADS])
        dinv = sb("dinv", [P, NT])
        rdeg = sb("rdeg", [P, NT])
        st6 = sb("st6", [P, 5 * P])
        rstd = sb("rstd", [P, NT])
        nmr = sb("nmr", [P, NT])
        sm = sb("sm", [P, 4 * NT])
        PS = ctx.enter_context(nc.psum_tensor("PS", [P, 8 * 512], F32))

        def bank(b, w=512):
            return PS[:, b * 512:b * 512 + w]

        def hslot(n):
            return hs[:, n * ROW:(n + 1) * ROW]

        def fslot(n):
            return F[:, n * ROW:(n + 1) * ROW]

        row = lambda ap: ap.rearrange("(a n) -> a n", a=1)
        colv = lambda ap: ap.rearrange("(n a) -> n a", a=1)
        gathered = [sig(f"gathered{j}", 0) for j in range(2 * HALF)]
        idx_ready = sig("idx_ready")
        onehot_ready = sig("onehot_ready")
        scaled = sig("scaled")
        summed = sig("summed")
        added = sig("added")
        chain = sig("chain")
        x_in = sig("x_in")
        tables_zero = sig("tables_zero")
        dve_s = sig("dve_s")
        achain = sig("achain")
        loads = sig("loads")
        loads2 = sig("loads2")
        stores = sig("stores")
        pe_a = sig("pe_a")
        pe_b = sig("pe_b")
        pe_c = sig("pe_c")
        act_a = sig("act_a")
        act_b = sig("act_b")
        act_c = sig("act_c")
        dve_a = sig("dve_a")
        dve_b = sig("dve_b")
        dve_c = sig("dve_c")
        brought = sig("brought")
        pe_t, pe_z, pe_m, pe_d = (sig(n) for n in ("pe_t", "pe_z", "pe_m", "pe_d"))
        attrT_ready, z2_ready, h1_ready, msg_ready, msum_ready, sidx_ready, picked_rows, q_made, dups_made = (
            sig(n) for n in ("attrT_ready", "z2_ready", "h1_ready", "msg_ready", "msum_ready", "sidx_ready", "picked_rows", "q_made",
                             "dups_made"))
        packed, turned, loc_rows, softmax_step, exped, w_turned, w_ready, ends_kept, pieces_kept, ald_in = (
            sig(n) for n in ("packed", "turned", "loc_rows", "softmax_step", "exped", "w_turned", "w_ready", "ends_kept",
                             "pieces_kept", "ald_in"))
        scattered = [sig(f"scattered{a}", 0) for a in range(AGG)]
        idx_taken = sig("idx_taken")
        spread = sig("spread", 0)
        picked = sig("picked", 0)
        half_in = [sig(f"half_in{b}", 0) for b in range(2)]
        half_out = [sig(f"half_out{b}") for b in range(2)]
        more_in = [sig(f"more_in{b}") for b in range(4)]

        def linker(eng, s=chain):
            def link(ins):
                s.at += 1
                ins.then_inc(s.sem, 1)
                eng.wait_ge(s.sem, s.at)
            return link

        with nc.Block() as block:
            @block.sync
            def _(sp):
                for s in signals:
                    if s.at:
                        sp.sem_inc(s.sem, LEAD)

        dstI, srcI = hslot(0).bitcast(I32), hslot(1).bitcast(I32)
        dstF, srcF, locF = hslot(2), hslot(3), hslot(4)
        ebB, junk = hslot(5), hslot(6)
        same = hslot(6)
        prevI = idx[:, 0:1]
        locA, loc_plain = wk[:, 0:K], wk[:, K:2 * K]
        small = lambda n: wk[:, 2 * K + 2 * n * G:2 * K + 2 * (n + 1) * G]
        ends_flat, piece_no, piece_to, piece_i = small(0), small(1), small(2), small(3).bitcast(I32)
        ends_dst = ends_flat.rearrange("p (g e) -> p g e", e=2)
        to_end, ends_up = (small(4)[:, n * G:(n + 1) * G].unsqueeze(2) for n in range(2))
        flat = lambda a: a.rearrange("(p j) -> p j", p=1)
        with nc.Block() as block:
            @block.gpsimd
            def _(pool):
                nc.gpsimd.iota(st6[:, 0:P].bitcast(I32), pattern=[[1, P]], base=0, channel_multiplier=0).then_inc(brought.sem, 1)
                nc.gpsimd.iota(sm[:, 0:NT].bitcast(I32), pattern=[[P, NT]], base=0, channel_multiplier=1).then_inc(brought.sem, 1)
                nc.gpsimd.iota(piece_i, pattern=[[1, 2 * G]], base=0, channel_multiplier=2 * G).then_inc(brought.sem, 1)

            @block.sync
            def _(sp):
                sp.wait_ge(dve_b.sem, dve_b.after(4))
                srcf, dstf = t["src"], t["dst"]
                for buf, ap in ((dstI, dstf), (srcI, srcf)):
                    sp.dma_start(buf[0:127, :], ap[0:127 * ROW].rearrange("(p j) -> p j", p=127)).then_inc(loads.sem, 16)
                    sp.dma_start(buf[127:128, 0:LAST], flat(ap[127 * ROW:E])).then_inc(loads.sem, 16)
                sp.dma_start(prevI[1:P, :], dstf[0:127 * ROW].rearrange("(p j) -> p j", j=ROW)[:, ROW - 1:ROW]).then_inc(loads.sem, 16)
                sp.dma_start(idx[0:P - 1, 1:2], dstf[LAST:E].rearrange("(p j) -> p j", j=ROW)[:, ROW - LAST:ROW - LAST + 1]).then_inc(loads.sem, 16)
                sp.dma_start(xs[:, 0:(NT - 1) * D].rearrange("p (i f) -> p i f", f=D),
                             t["x"][0:(NT - 1) * P, :].rearrange("(i p) f -> p i f", p=P)).then_inc(x_in.sem, 16)
                sp.dma_start(xs[0:N - (NT - 1) * P, (NT - 1) * D:NT * D], t["x"][(NT - 1) * P:N, :]).then_inc(x_in.sem, 16)
                sp.wait_ge(loads.sem, loads.after(16 * 6))
                sp.dma_start(src_d.rearrange("(p g) c -> p (g c)", p=P), srcI).then_inc(loads.sem, 16)
                sp.dma_start(dst_d.rearrange("(p g) c -> p (g c)", p=P), dstI).then_inc(loads.sem, 16)
                sp.wait_ge(loads.sem, loads.after(16 * 8))
                sp.wait_ge(dve_c.sem, dve_c.after(2))
                sp.dma_start(loc_rows_d.rearrange("(p g) c -> p (g c)", p=P), locF).then_inc(loads2.sem, 16)
                sp.dma_start(same_d, same).then_inc(tables_zero.sem, 16)
                sp.dma_start(keep_d.rearrange("(p n) -> p n", p=P), same_ends[:, :]).then_inc(loads2.sem, 16)
                sp.dma_start(piece_d.rearrange("(p n) -> p n", p=P), piece_i).then_inc(loads2.sem, 16)
                sp.dma_start(eb_i_d, st6[0:G, 4 * P:5 * P].bitcast(I32)).then_inc(loads2.sem, 16)
                sp.dma_start(eb_f_d, st6[0:G, 3 * P:4 * P]).then_inc(loads2.sem, 16)
                sp.wait_ge(loads2.sem, loads2.after(80))
                sp.dma_start(piece_idx[:, :].unsqueeze(2), piece_d.rearrange("(m c x) -> c m x", c=P, x=1)).then_inc(loads2.sem, 16)
                sp.dma_start(ebi[0:1, :], eb_i_d.rearrange("(a g) p -> a (g p)", a=1)).then_inc(loads2.sem, 16)
                sp.dma_start(ebB, eb_f_d.rearrange("(a g) p -> a (g p)", a=1).broadcast_to([P, K])).then_inc(loads2.sem, 16)
                sp.wait_ge(dve_b.sem, dve_b.after(4 + G))
                sp.dma_start(loc_d, loc_plain).then_inc(loads2.sem, 16)
                sp.wait_ge(loads2.sem, loads2.after(144))

            @block.vector
            def _(v):
                link = linker(v)
                v.memset(F[:, :], 0.0).then_inc(dve_a.sem, 1)
                v.memset(dstI[96:128, LAST:], N).then_inc(dve_b.sem, 1)
                v.memset(srcI[96:128, LAST:], N).then_inc(dve_b.sem, 1)
                v.memset(idx[:, 0:2], -1).then_inc(dve_b.sem, 1)
                v.memset(xs[:, (NT - 1) * D:], 0.0).then_inc(dve_b.sem, 1)
                v.memset(srcT[:, K:], 0)
                v.wait_ge(brought.sem, brought.after(3))
                v.tensor_copy(iota_row[:, :], st6[:, 0:P].bitcast(I32))
                link(v.tensor_copy(sm[:, NT:2 * NT], sm[:, 0:NT].bitcast(I32)))
                link(v.tensor_copy(pcol[:, :], sm[:, NT:NT + 1]))
                v.tensor_scalar(lower[:, :], iota_row[:, :], pcol[:, 0:1], None, ALU.is_lt)
                link(v.tensor_scalar(ident[:, :], iota_row[:, :], pcol[:, 0:1], None, ALU.is_equal))
                v.wait_ge(loads.sem, loads.after(16 * 6))
                v.tensor_copy(srcF, srcI)
                v.tensor_copy(st6[:, 2 * P:2 * P + 2], idx[:, 0:2])
                link(v.tensor_copy(dstF, dstI))
                v.tensor_tensor(link_next[:, :], dstF[:, ROW - 1:ROW], st6[:, 2 * P + 1:2 * P + 2], ALU.is_equal)
                v.tensor_tensor(same[:, 1:], dstF[:, 1:], dstF[:, :-1], ALU.is_equal)
                v.tensor_tensor(same[:, 0:1], dstF[:, 0:1], st6[:, 2 * P:2 * P + 1], ALU.is_equal)
                first = dstF.rearrange("p (g c) -> p g c", c=P)[:, :, 0:1]
                v.tensor_tensor(locF.rearrange("p (g c) -> p g c", c=P), dstF.rearrange("p (g c) -> p g c", c=P),
                                first.broadcast_to([P, G, P]), ALU.subtract)
                last = dstF.rearrange("p (g c) -> p g c", c=P)[:, :, P - 1:P]
                ends = same_ends[:, :].rearrange("p (g e) -> p g e", e=2)
                v.tensor_tensor(ends[:, :, 1:2], last, first, ALU.is_equal)
                v.tensor_copy(ends_dst[:, :, 0:1], first)
                v.tensor_copy(ends_dst[:, :, 1:2], last)
                link(v.tensor_copy(st6[:, P:P + G], first.rearrange("p g c -> p (g c)")))
                link(v.tensor_copy(ends[:, :, 0:1], same.rearrange("p (g c) -> p g c", c=P)[:, :, 0:1]))
                loc3, locA3 = (a.rearrange("p (g c) -> p g c", c=P) for a in (locF, locA))
                last_loc = loc3[:, :, P - 1:P]
                link(v.tensor_scalar(to_end, last_loc, 0.0, None, ALU.is_gt))
                link(v.scalar_tensor_tensor(ends_up, last_loc, float(1 - P), to_end, ALU.add, ALU.mult))
                link(v.tensor_tensor(locA3, loc3, last_loc.broadcast_to([P, G, P]), ALU.is_equal))
                link(v.tensor_tensor(locA3, locA3, ends_up.broadcast_to([P, G, P]), ALU.mult))
                link(v.tensor_tensor(locA3, loc3, locA3, ALU.subtract))
                link(v.tensor_copy(piece_no, piece_i))
                link(v.tensor_scalar(piece_no, piece_no, float(NP), None, ALU.add))
                link(v.tensor_tensor(piece_to, piece_no, ends_flat, ALU.subtract))
                link(v.tensor_tensor(piece_to[:, 0:2 * G - 1], piece_to[:, 0:2 * G - 1], same_ends[:, 1:], ALU.mult))
                link(v.tensor_tensor(piece_to[:, 2 * G - 1:], piece_to[:, 2 * G - 1:], link_next[:, :], ALU.mult))
                link(v.tensor_tensor(piece_to, piece_to, ends_flat, ALU.add))
                link(v.tensor_copy(piece_i, piece_to))
                v.nop().then_inc(dve_c.sem, 1)
                v.wait_ge(pe_a.sem, pe_a.after(1))
                v.tensor_copy(st6[0:G, 4 * P:5 * P].bitcast(I32), PS[0:G, 0:P])
                link(v.tensor_copy(st6[0:G, 3 * P:4 * P], PS[0:G, 0:P]))
                v.nop().then_inc(dve_c.sem, 1)
                for g in range(G):
                    b = 1 + g % 3
                    v.wait_ge(pe_b.sem, pe_b.after(g + 1))
                    v.tensor_copy(loc_plain[:, g * P:(g + 1) * P], PS[:, b * 1024:b * 1024 + P])
                    v.tensor_copy(locT[:, g * P:(g + 1) * P], PS[:, b * 1024 + P:b * 1024 + 2 * P])
                    link(v.tensor_copy(srcT[:, g * P:(g + 1) * P], PS[:, b * 1024 + 512:b * 1024 + 512 + P]))
                    v.nop().then_inc(dve_b.sem, 1)

            @block.tensor
            def _(pe):
                pe.wait_ge(dve_c.sem, dve_c.after(1))
                pe.transpose(PS[0:G, 0:P], st6[:, P:P + G], ident[:, :]).then_inc(pe_a.sem, 1)
                for g in range(G):
                    b = 1 + g % 3
                    if g >= 3:
                        pe.wait_ge(dve_b.sem, dve_b.after(4 + g - 2))
                    pe.transpose(PS[:, b * 1024:b * 1024 + P], locF[:, g * P:(g + 1) * P], ident[:, :])
                    pe.transpose(PS[:, b * 1024 + P:b * 1024 + 2 * P], locA[:, g * P:(g + 1) * P], ident[:, :])
                    pe.transpose(PS[:, b * 1024 + 512:b * 1024 + 512 + P], srcF[:, g * P:(g + 1) * P], ident[:, :]).then_inc(pe_b.sem, 1)
        brought.passed(3); dve_a.passed(1); dve_b.passed(4 + G); dve_c.passed(2); pe_a.passed(1); pe_b.passed(G)
        loads.passed(16 * 8); loads2.passed(144)
        if stop <= 0: return

        nodeid = sm[:, NT:2 * NT]
        cnt, cnt2 = sm[:, 2 * NT:3 * NT], sm[:, 3 * NT:4 * NT]
        rows = wk[:, 8 * P:8 * P + 2 * GRP * P].bitcast(I32)
        with nc.Block() as block:
            @block.vector
            def _(v):
                link = linker(v)
                with v.Fori(0, NG // 2) as i:
                    for b in range(2):
                        q = i * 2 + b
                        for j in range(GRP):
                            c = q * GRP + j
                            v.tensor_scalar(junk, ebB, nodeid[:, bass.ds(c, 1)], 0.0, ALU.is_lt, ALU.add,
                                            accum_out=cnt[:, bass.ds(c, 1)]).then_inc(dve_a.sem, 1)
                            v.wait_ge(dve_a.sem, dve_a.after(q * (GRP + 1) + j + 1))
                        of_group = cnt[:, bass.ds(q * GRP, GRP)]
                        v.tensor_scalar(of_group, of_group, -1.0, 0.0, ALU.add, ALU.max).then_inc(dve_a.sem, 1)
                        v.wait_ge(dve_a.sem, dve_a.after((q + 1) * (GRP + 1)))
                        v.wait_ge(half_in[b].sem, half_in[b].after(i * (16 * GRP)))
                        v.tensor_scalar(idx[:, b * HALF:b * HALF + GRP], of_group, 0.0, None, ALU.add).then_inc(idx_ready.sem, 1)
                    for b in range(2):
                        q = i * 2 + b
                        v.wait_ge(half_in[b].sem, half_in[b].after((i + 1) * (16 * GRP)))
                        for j in range(GRP):
                            c = q * GRP + j
                            v.tensor_scalar(junk[:, 0:P], rows[:, (b * GRP + j) * P:(b * GRP + j + 1) * P],
                                            nodeid[:, bass.ds(c, 1)], 0.0, ALU.is_lt, ALU.add,
                                            accum_out=cnt2[:, bass.ds(c, 1)]).then_inc(dve_b.sem, 1)
                            v.wait_ge(dve_b.sem, dve_b.after(c + 1))
                link(v.scalar_tensor_tensor(cnt2, cnt, float(P), cnt2, ALU.mult, ALU.add))
                v.memset(wk[:, 0:P], 0.0)
                link(v.tensor_copy(start_i[:, :], cnt2))
                v.nop().then_inc(dve_c.sem, 1)
                v.wait_ge(pe_a.sem, pe_a.after(1))
                startT = wk[0:NT, P:2 * P]
                link(v.tensor_copy(startT, PS[0:NT, 0:P]))
                v.nop().then_inc(dve_c.sem, 1)
                v.wait_ge(loads2.sem, loads2.after(16))
                degT = wk[0:NT, 3 * P:4 * P]
                link(v.tensor_tensor(degT, wk[0:NT, 2 * P:3 * P], startT, ALU.subtract))
                link(v.tensor_scalar(wk[0:NT, 4 * P:5 * P], degT, 0.0, 1.0, ALU.max, ALU.add))
                link(v.tensor_scalar(degT, degT, 1.0, None, ALU.max))
                v.nop().then_inc(dve_c.sem, 1)
                v.wait_ge(act_a.sem, act_a.after(1))
                v.reciprocal(wk[0:NT, 5 * P:6 * P], wk[0:NT, 4 * P:5 * P])
                link(v.reciprocal(degT, degT))
                v.nop().then_inc(dve_c.sem, 1)
                v.wait_ge(pe_a.sem, pe_a.after(2))
                v.tensor_copy(dinv[:, :], PS[:, 1024:1024 + NT])
                v.tensor_copy(rdeg[:, :], PS[:, 2048:2048 + NT])

            @block.scalar
            def _(act):
                act.dma_start(ex4.rearrange("(p j) h -> p (j h)", p=P), F[:, 0:ROW * HEADS]).then_inc(tables_zero.sem, 16)
                act.dma_start(ex1.rearrange("(p j) h -> p (j h)", p=P), F[:, 0:ROW]).then_inc(tables_zero.sem, 16)
                act.dma_start(attr_d[E:EP, :].rearrange("(a b) d -> a (b d)", a=4), F[0:4, 0:(EP - E) * 4]).then_inc(tables_zero.sem, 16)
                act.dma_start(tab_b[NP:WIN, :], F[:, 0:D]).then_inc(tables_zero.sem, 16)
                for n, a in enumerate((0, 2)):
                    act.wait_ge(dve_a.sem, dve_a.after((2 + 3 * n) * (GRP + 1)))
                    act.dma_start(agg[a].rearrange("(p i) d -> p (i d)", p=P), F[:, 0:WIN]).then_inc(tables_zero.sem, 16)
                act.wait_ge(dve_c.sem, dve_c.after(3))
                act.activation(wk[0:NT, 4 * P:5 * P], wk[0:NT, 4 * P:5 * P], ACT.Sqrt).then_inc(act_a.sem, 1)

            @block.tensor
            def _(pe):
                pe.wait_ge(dve_c.sem, dve_c.after(1))
                pe.transpose(PS[0:NT, 0:P], cnt2, ident[:, :]).then_inc(pe_a.sem, 1)
                pe.wait_ge(dve_c.sem, dve_c.after(4))
                pe.transpose(PS[:, 1024:1024 + NT], wk[0:NT, 5 * P:6 * P], ident[0:NT, 0:NT])
                pe.transpose(PS[:, 2048:2048 + NT], wk[0:NT, 3 * P:4 * P], ident[0:NT, 0:NT]).then_inc(pe_a.sem, 1)

            @block.sync
            def _(sp):
                sp.wait_ge(dve_c.sem, dve_c.after(2))
                sp.dma_start(start_d[0:NP].rearrange("(i p) -> i p", p=P), wk[0:NT, P:2 * P]).then_inc(loads.sem, 16)
                sp.dma_start(flat(start_d[NP:NP + P]), wk[0:1, 0:P]).then_inc(loads.sem, 16)
                sp.wait_ge(loads.sem, loads.after(32))
                sp.dma_start(wk[0:NT, 2 * P:3 * P], start_d[1:NP + 1].rearrange("(i p) -> i p", p=P)).then_inc(loads2.sem, 16)
                sp.wait_ge(dve_c.sem, dve_c.after(4))
                sp.dma_start(dinv_d.rearrange("(i p) -> i p", p=P), wk[0:NT, 5 * P:6 * P]).then_inc(stores.sem, 16)
                sp.wait_ge(stores.sem, stores.after(16))
                sp.wait_ge(x_in.sem, x_in.after(32))
                sp.wait_ge(tables_zero.sem, tables_zero.after(16 * 7))

            @block.gpsimd
            def _(pool):
                with pool.Fori(0, NG // 2) as i:
                    for b in range(2):
                        pool.wait_ge(idx_ready.sem, idx_ready.after(i * 2 + b + 1))
                        pool.wait_ge(dve_b.sem, dve_b.after(i * (2 * GRP)))
                        pool.sem_inc(idx_taken.sem, 1)
                        for j in range(GRP):
                            pool.indirect_dma_start(rows[:, (b * GRP + j) * P:(b * GRP + j + 1) * P], None, dst_d,
                                                    bass.IndirectOffsetOnAxis(idx[:, b * HALF + j:b * HALF + j + 1], 0))\
                                .then_inc(half_in[b].sem, 16)
        dve_a.passed(NG * (GRP + 1)); dve_b.passed(NT); dve_c.passed(4); act_a.passed(1); pe_a.passed(2)
        idx_ready.passed(NG); loads.passed(32); loads2.passed(16); stores.passed(16)
        for s in half_in: s.passed(16 * GRP * (NG // 2))
        if stop <= 1: return

        group = lambda a: a.rearrange("p (i f) -> p i f", f=P)

        def row_stats(v, src, q):
            for j in range(GRP):
                c = q * GRP + j
                v.bn_stats(st6[:, bass.ds(c * 6, 6)], src[:, bass.ds(c * D, D)]).then_inc(dve_s.sem, 1)

        def layer_norm(src, dst, func, have_stats=False):
            st = st6[:, 0:NT * 6].rearrange("p (i s) -> p i s", s=6)
            col = lambda n: st[:, :, n:n + 1].rearrange("p i s -> p (i s)")
            a, b = sm[:, 0:NT], sm[:, 2 * NT:3 * NT]
            with nc.Block() as block:
                @block.vector
                def _(v):
                    link = linker(v)
                    if not have_stats:
                        with v.Fori(0, NG) as i:
                            row_stats(v, src, i)
                    v.wait_ge(dve_s.sem, dve_s.after(NT))
                    v.tensor_tensor(a, col(1), col(4), ALU.add)
                    v.tensor_tensor(b, col(1), col(4), ALU.subtract)
                    link(v.tensor_tensor(rstd[:, :], col(2), col(5), ALU.add))
                    link(v.tensor_tensor(b, b, b, ALU.mult))
                    link(v.tensor_scalar(rstd[:, :], rstd[:, :], 1.0 / D, EPS, ALU.mult, ALU.add))
                    link(v.scalar_tensor_tensor(rstd[:, :], b, 0.25, rstd[:, :], ALU.mult, ALU.add))
                    v.nop().then_inc(dve_b.sem, 1)
                    v.wait_ge(act_a.sem, act_a.after(1))
                    link(v.reciprocal(rstd[:, :], rstd[:, :]))
                    link(v.scalar_tensor_tensor(nmr[:, :], a, -0.5, rstd[:, :], ALU.mult, ALU.mult))
                    with v.Fori(0, NG) as q:
                        sg, dg = (group(a[:, bass.ds(q * GW, GW)]) for a in (src, dst))
                        r3, n3 = (a[:, bass.ds(q * GRP, GRP)].unsqueeze(2).broadcast_to([P, GRP, D]) for a in (rstd, nmr))
                        v.tensor_tensor(dg, sg, r3, ALU.mult).then_inc(dve_c.sem, 1)
                        v.wait_ge(dve_c.sem, dve_c.after(q * 2 + 1))
                        v.tensor_tensor(dg, dg, n3, ALU.add).then_inc(dve_c.sem, 1)

                @block.scalar
                def _(act):
                    act.wait_ge(dve_b.sem, dve_b.after(1))
                    act.activation(rstd[:, :], rstd[:, :], ACT.Sqrt).then_inc(act_a.sem, 1)
                    if func != ACT.Identity:
                        with act.Fori(0, NG) as q:
                            act.wait_ge(dve_c.sem, dve_c.after(q * 2 + 2))
                            dg = dst[:, bass.ds(q * GW, GW)]
                            act.activation(dg, dg, func)
            dve_s.passed(NT); dve_b.passed(1); dve_c.passed(2 * NG); act_a.passed(1)

        hT = [wk[:, b * GW:(b + 1) * GW] for b in range(2)]
        ost = [wk[:, (2 + b) * GW:(3 + b) * GW] for b in range(2)]
        psA = [PS[:, b * 2048:b * 2048 + GW] for b in range(2)]
        psB = [PS[:, b * 2048 + 1024:b * 2048 + 1024 + GW] for b in range(2)]
        W = [wts[:, n * P:(n + 1) * P] for n in range(5)]
        bias_b = [wts[:, (5 + n) * P:(6 + n) * P] for n in range(2)]
        every = lambda a, n=GRP: a.unsqueeze(1).broadcast_to([P, n, P])

        def tile_of(buf, j, w=P):
            return buf[:, j * w:(j + 1) * w]

        def rows_of(table, q):
            return table[bass.ds(q * GW, GW), 0:D].rearrange("(i p) f -> p i f", p=P)

        def project(weight, table, from_f=False, bias=None, scale=False, init_f=False, al=None, heads=0,
                    ald_table=None, ex=None, act_f=None):
            with nc.Block() as block:
                @block.tensor
                def _(pe):
                    with pe.Fori(0, NG // 2) as i:
                        for b in range(2):
                            q = i * 2 + b
                            if not from_f:
                                pe.wait_ge(brought.sem, brought.after(q + 1))
                                pe.wait_ge(act_a.sem, act_a.after(q - 1))
                                if init_f:
                                    pe.wait_ge(dve_c.sem, dve_c.after(q - 1))
                                if al is not None:
                                    pe.wait_ge(dve_b.sem, dve_b.after(q - 1))
                                for j in range(GRP):
                                    last = pe.transpose(tile_of(psA[b], j), tile_of(stage, j), ident[:, :])
                                last.then_inc(pe_a.sem, 1)
                            pe.wait_ge(act_a.sem, act_a.after(q + 1))
                            pe.wait_ge(dve_a.sem, dve_a.after(q - 1))
                            for j in range(GRP):
                                last = pe.matmul(tile_of(psB[b], j), tile_of(hT[b], j), weight, start=True, stop=True)
                            last.then_inc(pe_b.sem, 1)
                            if al is not None:
                                pe.wait_ge(dve_b.sem, dve_b.after(q - 1))
                                for j in range(GRP):
                                    c = b * 2048 + j * 2 * heads
                                    last = pe.matmul(PS[:, c:c + 2 * heads], tile_of(hT[b], j), al, start=True, stop=True)
                                last.then_inc(pe_c.sem, 1)
                            if init_f:
                                pe.wait_ge(dve_c.sem, dve_c.after(q - 1))
                                for a, z in ((0, 512), (512, GW)):
                                    last = pe.matmul(psA[b][:, a:z], weight, hT[b][:, a:z], start=True, stop=True)
                                last.then_inc(pe_c.sem, 1)

                if al is not None:
                    @block.gpsimd
                    def _(pool):
                        for i in range(NT):
                            n = min(P, N + 1 - i * P)
                            if i % GRP == 0:
                                pool.wait_ge(dve_b.sem, dve_b.after(i // GRP + 1))
                            pool.indirect_dma_start(ex, bass.IndirectOffsetOnAxis(start_i[0:n, i:i + 1], 0),
                                                    ald[0:n, i * heads:(i + 1) * heads], None).then_inc(spread.sem, 16)
                        pool.wait_ge(spread.sem, spread.after(16 * NT))

                @block.scalar
                def _(act):
                    with act.Fori(0, NG // 2) as i:
                        for b in range(2):
                            q = i * 2 + b
                            if not from_f:
                                act.wait_ge(pe_a.sem, pe_a.after(q))
                                act.copy(stage, hs[:, bass.ds(q * GW, GW)]).then_inc(brought.sem, 1)
                                act.wait_ge(pe_a.sem, pe_a.after(q + 1))
                            act.wait_ge(pe_b.sem, pe_b.after(q - 1))
                            if init_f or al is not None:
                                act.wait_ge(pe_c.sem, pe_c.after(q - 1))
                            if not from_f:
                                act.copy(hT[b], psA[b]).then_inc(act_a.sem, 1)
                            elif act_f is None:
                                act.copy(hT[b], F[:, bass.ds(q * GW, GW)]).then_inc(act_a.sem, 1)
                            else:
                                act.activation(hT[b], F[:, bass.ds(q * GW, GW)], **act_f).then_inc(act_a.sem, 1)

                @block.vector
                def _(v):
                    with v.Fori(0, NG // 2) as i:
                        for b in range(2):
                            q = i * 2 + b
                            v.wait_ge(pe_b.sem, pe_b.after(q + 1))
                            v.wait_ge(half_out[b].sem, half_out[b].after(i * 16))
                            if scale:
                                d = dinv[:, bass.ds(q * GRP, GRP)].unsqueeze(2).broadcast_to([P, GRP, P])
                                v.tensor_tensor(group(ost[b]), group(psB[b]), d, ALU.mult).then_inc(dve_a.sem, 1)
                            elif bias is not None:
                                v.tensor_tensor(group(ost[b]), group(psB[b]), every(bias), ALU.add).then_inc(dve_a.sem, 1)
                            else:
                                v.tensor_copy(ost[b], psB[b]).then_inc(dve_a.sem, 1)
                            if al is not None:
                                v.wait_ge(pe_c.sem, pe_c.after(q + 1))
                                both = PS[:, b * 2048:b * 2048 + GRP * 2 * heads].rearrange("p (i h) -> p i h", h=2 * heads)
                                cols = bass.ds(q * GRP * heads, GRP * heads)
                                v.tensor_copy(als[:, cols].rearrange("p (i h) -> p i h", h=heads), both[:, :, 0:heads])
                                v.tensor_copy(ald[:, cols].rearrange("p (i h) -> p i h", h=heads), both[:, :, heads:])\
                                    .then_inc(dve_b.sem, 1)
                            if init_f:
                                v.wait_ge(pe_c.sem, pe_c.after(q + 1))
                                v.wait_ge(more_in[0].sem, more_in[0].after((q + 1) * 16))
                                v.tensor_tensor(F[:, bass.ds(q * GW, GW)], psA[b], dB, ALU.mult).then_inc(dve_c.sem, 1)

                @block.sync
                def _(sp):
                    with sp.Fori(0, NG // 2) as i:
                        for b in range(2):
                            q = i * 2 + b
                            if init_f:
                                sp.wait_ge(dve_c.sem, dve_c.after(q))
                                sp.dma_start(dB, row(dinv_d[bass.ds(q * GW, GW)]).broadcast_to([P, GW])).then_inc(more_in[0].sem, 16)
                            sp.wait_ge(dve_a.sem, dve_a.after(q + 1))
                            sp.dma_start(rows_of(table, q), group(ost[b])).then_inc(half_out[b].sem, 16)
                    for b in range(2):
                        sp.wait_ge(half_out[b].sem, half_out[b].after(16 * (NG // 2)))
                    if al is not None:
                        sp.wait_ge(dve_b.sem, dve_b.after(NG))
                        for tb, buf in ((table[:, D:], als), (ald_table, ald)):
                            sp.dma_start(tb.rearrange("(i p) h -> p i h", p=P),
                                         buf[:, 0:NT * heads].rearrange("p (i h) -> p i h", h=heads)).then_inc(stores.sem, 16)
                        sp.wait_ge(stores.sem, stores.after(32))
            act_a.passed(NG)
            if not from_f:
                brought.passed(NG)
                pe_a.passed(NG)
            pe_b.passed(NG)
            dve_a.passed(NG)
            for s in half_out:
                s.passed(16 * (NG // 2))
            if al is not None:
                spread.passed(16 * NT)
                pe_c.passed(NG)
                dve_b.passed(NG)
                stores.passed(32)
            if init_f:
                pe_c.passed(NG)
                dve_c.passed(NG)
                more_in[0].passed(16 * NG)

        def bring(act, table, to, free, ready=brought, **act_f):
            with act.Fori(0, NG // 2) as i:
                for b in range(2):
                    q = i * 2 + b
                    act.wait_ge(free.sem, free.after(q - 1))
                    cols = table[:, bass.ds(q * GW, GW)]
                    if act_f:
                        act.activation(to[b], cols, **act_f).then_inc(ready.sem, 1)
                    else:
                        act.copy(to[b], cols).then_inc(ready.sem, 1)

        als = st6
        dB = wk[:, 4 * GW:5 * GW]
        stage = wk[:, 5 * GW:6 * GW]
        gbuf = [wk[:, j * P:(j + 1) * P] for j in range(2 * HALF)]
        onehot = [wk[:, (2 * HALF + j) * P:(2 * HALF + j + 1) * P] for j in range(2 * HALF)]

        def aggregate(table, clear=False):
            with nc.Block() as block:
                @block.scalar
                def _(act):
                    with act.Fori(0, EI) as i:
                        for b in range(2):
                            k0 = i * (2 * HALF) + b * HALF
                            act.wait_ge(summed.sem, summed.after(k0 - HALF))
                            act.copy(idx[:, b * HALF:(b + 1) * HALF], srcT[:, bass.ds(k0, HALF)]).then_inc(idx_ready.sem, 1)

                @block.gpsimd
                def _(pool):
                    with pool.Fori(0, EI) as i:
                        for b in range(2):
                            pool.wait_ge(idx_ready.sem, idx_ready.after(i * 2 + b + 1))
                            pool.sem_inc(idx_taken.sem, 1)
                            for j in range(b * HALF, (b + 1) * HALF):
                                pool.indirect_dma_start(gbuf[j], None, table, bass.IndirectOffsetOnAxis(idx[:, j:j + 1], 0))\
                                    .then_inc(gathered[j].sem, 16)

                @block.tensor
                def _(pe):
                    with pe.Fori(0, EI) as i:
                        for j in range(2 * HALF):
                            k = i * (2 * HALF) + j
                            pe.wait_ge(gathered[j].sem, gathered[j].after((i + 1) * 16))
                            pe.wait_ge(onehot_ready.sem, onehot_ready.after(k + 1))
                            pe.wait_ge(added.sem, added.after(k - 7))
                            pe.matmul(bank(j % 8, P), gbuf[j], onehot[j], start=True, stop=True).then_inc(summed.sem, 1)

                @block.vector
                def _(v):
                    if clear:
                        linker(v)(v.memset(F[:, :], 0.0))
                    with v.Fori(0, EI) as i:
                        for b in range(2):
                            k0 = i * (2 * HALF) + b * HALF
                            v.wait_ge(summed.sem, summed.after(k0 - HALF))
                            for j in range(HALF):
                                v.tensor_scalar(onehot[b * HALF + j], iota_row[:, :], locT[:, bass.ds(k0 + j, 1)], None,
                                                ALU.is_equal).then_inc(onehot_ready.sem, 1)
                            _, first_dst = nc.values_load_multi_w_load_instructions(
                                ebi[0:1, bass.ds(k0, HALF)], engines=[mybir.EngineType.DVE], min_val=0, max_val=NP,
                                skip_runtime_bounds_check_because="dst holds node numbers")
                            for j in range(HALF):
                                cols = F[:, bass.ds(first_dst[j], P)]
                                v.wait_ge(summed.sem, summed.after(k0 + j + 1))
                                v.wait_ge(added.sem, added.after(k0 + j))
                                v.tensor_tensor(cols, cols, bank((b * HALF + j) % 8, P), ALU.add).then_inc(added.sem, 1)
            for s in gathered:
                s.passed(16 * EI)
            summed.passed(K)
            added.passed(K)
            onehot_ready.passed(K)
            idx_ready.passed(2 * EI)

        def attention(heads, table, ald_table, ex, whole_rows):
            R = heads * BT
            TW = D + heads
            raw = hs[:, 0:ROW * heads]
            held = [F[:, h * ROW:(h + 1) * ROW] for h in range(heads)]
            same = hs[:, ROW * HEADS:ROW * (HEADS + 1)]
            alh = wk[:, 0:heads]
            first_dst = wk[:, P:P + 1].bitcast(I32)
            gt = [hs[:, s * BT * TW:(s + 1) * BT * TW].rearrange("p (j f) -> p j f", f=TW) for s in range(2)]
            kept = hs[:, NP - 2 * K:]
            used = [2 * HALF * P]

            def in_wk(width):
                used[0] += width
                return wk[:, used[0] - width:used[0]]

            onehot = [wk[:, j * P:(j + 1) * P] for j in range(2 * HALF)]
            bidx = [in_wk(BT).bitcast(I32) for _ in range(2)]
            pack_al, pack_loc, loc_r, ald_r, z, t1, p_r, w_r, same_r = (in_wk(P) for _ in range(9))
            md, cut_r, w_c, ends = in_wk(2 * P), in_wk(P + 1), in_wk(P), in_wk(NBT * 4)
            m_r, d_r = md[:, 0:P], md[:, P:2 * P]
            heads_of = lambda a: a[:, 0:R].rearrange("p (h j) -> p h j", j=BT)

            with nc.Block() as block:
                @block.gpsimd
                def _(pool):
                    pool.wait_ge(loads.sem, loads.after(32))
                    pool.sem_inc(idx_taken.sem, 1)
                    pool.indirect_dma_start(alh, None, ald_table,
                                            bass.IndirectOffsetOnAxis(first_dst, 0)).then_inc(picked.sem, 16)

                @block.sync
                def _(sp):
                    sp.dma_start(same, same_d).then_inc(loads.sem, 16)
                    sp.dma_start(first_dst, dst_d.rearrange("(p g) c -> p (g c)", p=P)[:, 0:1]).then_inc(loads.sem, 16)
                    sp.dma_start(raw, ex.rearrange("(p j) h -> p (j h)", p=P)).then_inc(ald_in.sem, 16)
                    rows = ald_e[0:K * heads, :].rearrange("(g u h j) c -> u h j g c", u=P // BT, h=heads, j=BT)
                    for h in range(heads):
                        sp.wait_ge(dve_a.sem, dve_a.after(h + 1))
                        for u in range(P // BT):
                            sp.dma_start(rows[u, h], held[h][u * BT:(u + 1) * BT, :].rearrange("j (g c) -> j g c", c=P))\
                                .then_inc(stores.sem, 16)
                    sp.wait_ge(stores.sem, stores.after(16 * heads * (P // BT)))

                @block.vector
                def _(v):
                    v.wait_ge(picked.sem, picked.after(16))
                    v.wait_ge(ald_in.sem, ald_in.after(16))
                    for h in range(heads):
                        ad = raw.rearrange("p (j h) -> p j h", h=heads)[:, :, h]
                        v.tensor_tensor_scan(held[h], same, ad, alh[:, h:h + 1], ALU.mult, ALU.add).then_inc(dve_a.sem, 1)
            loads.passed(32)
            picked.passed(16)
            ald_in.passed(16)
            dve_a.passed(heads)
            stores.passed(16 * heads * (P // BT))

            MASKS, SUMMED_AL, LOGITS, MAX, SHIFTED, SUM, WEIGHTS, STEPS = 2, 3, 4, 6, 7, 9, 11, 11
            QH = BT // HALF
            NATTR, NZERO = 50, 48
            ATTR, ZERO = E // NATTR, WIN // NZERO
            with nc.Block() as block:
                @block.scalar
                def _(act):
                    act.copy(bidx[0], srcT[:, 0:BT]).then_inc(idx_ready.sem, 1)
                    with act.Fori(0, NBT // 2) as i:
                        for s in range(2):
                            n = i * 2 + s
                            act.wait_ge(half_in[1 - s].sem, half_in[1 - s].after((i + s) * (16 * BT)))
                            act.copy(bidx[1 - s], srcT[:, bass.ds((n + 1) * BT, BT)]).then_inc(idx_ready.sem, 1)
                            act.wait_ge(turned.sem, turned.after(n * 2))
                            act.copy(heads_of(pack_loc), locT[:, bass.ds(n * BT, BT)].unsqueeze(1).broadcast_to([P, heads, BT]))\
                                .then_inc(packed.sem, 1)
                            act.wait_ge(turned.sem, turned.after(n * 2 + 1))
                            act.wait_ge(softmax_step.sem, softmax_step.after((n - 1) * STEPS + MASKS))
                            act.copy(loc_r[0:R, :], bank(4, P)[0:R, :]).then_inc(loc_rows.sem, 1)
                            act.wait_ge(half_in[s].sem, half_in[s].after((i + 1) * (16 * BT)))
                            act.copy(heads_of(pack_al), gt[s][:, :, D:].rearrange("p j h -> p h j")).then_inc(packed.sem, 1)
                            act.wait_ge(softmax_step.sem, softmax_step.after(n * STEPS + SHIFTED))
                            act.activation(p_r[0:R, :], p_r[0:R, :], ACT.Exp).then_inc(exped.sem, 1)
                            act.wait_ge(softmax_step.sem, softmax_step.after(n * STEPS + SUM))
                            act.copy(ends[0:R, bass.ds(n * 4, 4)].rearrange("p (w e) -> p w e", e=2),
                                     md[0:R, :].rearrange("p (w c) -> p w c", c=P)[:, :, 0:P:P - 1]).then_inc(ends_kept.sem, 1)
                            act.wait_ge(w_turned.sem, w_turned.after(n + 1))
                            act.copy(w_c[:, 0:R], bank(6, R)).then_inc(w_ready.sem, 1)
                            for h in range(QH):
                                q = n * QH + h
                                act.wait_ge(summed.sem, summed.after(q + 1))
                                act.copy(kept.rearrange("p (e k) -> p k e", e=2)[:, bass.ds(q * HALF, HALF), :],
                                         PS[:, h % 2 * 1024:(h % 2 + 1) * 1024].rearrange("p (j c) -> p j c", c=P)[:, :, 0:P:P - 1])\
                                    .then_inc(pieces_kept.sem, 1)

                @block.gpsimd
                def _(pool):
                    with pool.Fori(0, NBT // 2) as i:
                        for s in range(2):
                            n = i * 2 + s
                            pool.wait_ge(idx_ready.sem, idx_ready.after(n + 1))
                            for h in range(QH):
                                pool.wait_ge(summed.sem, summed.after(n * QH + h - 2 * QH + 1))
                                pool.sem_inc(idx_taken.sem, 1)
                                for j in range(h * HALF, (h + 1) * HALF):
                                    pool.indirect_dma_start(gt[s][:, j, :], None, table,
                                                            bass.IndirectOffsetOnAxis(bidx[s][:, j:j + 1], 0))\
                                        .then_inc(half_in[s].sem, 16)

                @block.sync
                def _(sp):
                    def al_d(n):
                        sp.wait_ge(softmax_step.sem, softmax_step.after((n - 1) * STEPS + SUMMED_AL))
                        sp.dma_start(ald_r[0:R, :], ald_e[bass.ds(n * R, R), :]).then_inc(ald_in.sem, 16)

                    def attributes(n):
                        rows = bass.ds(n * ATTR, ATTR)
                        sp.dma_start(attr_d[rows, :].rearrange("(a b) d -> a (b d)", a=10),
                                     t["edge_attr_16"][rows, :].rearrange("(a b) d -> a (b d)", a=10)).then_inc(loads.sem, 16)

                    def zeros(n):
                        rows = bass.ds(n * ZERO, ZERO)
                        for a in (1, 3):
                            sp.dma_start(agg[a][rows, :].rearrange("(a b) d -> a (b d)", a=8),
                                         agg[2][rows, :].rearrange("(a b) d -> a (b d)", a=8)).then_inc(loads.sem, 16)

                    if heads > 1:
                        with sp.Fori(0, NZERO) as n:
                            al_d(n)
                            attributes(n)
                            zeros(n)
                        for n in range(NZERO, NBT):
                            al_d(n)
                            if n < NATTR:
                                attributes(n)
                    else:
                        with sp.Fori(0, NBT) as n:
                            al_d(n)
                    sp.wait_ge(ald_in.sem, ald_in.after(16 * NBT))
                    if heads > 1:
                        sp.wait_ge(loads.sem, loads.after(16 * (NATTR + 2 * NZERO)))

                @block.tensor
                def _(pe):
                    with pe.Fori(0, NBT // 2) as i:
                        for s in range(2):
                            n = i * 2 + s
                            pe.wait_ge(packed.sem, packed.after(2 * n + 1))
                            pe.wait_ge(loc_rows.sem, loc_rows.after(n))
                            pe.transpose(bank(4, P)[0:R, :], pack_loc[:, 0:R], ident[:, :]).then_inc(turned.sem, 1)
                            pe.wait_ge(packed.sem, packed.after(2 * n + 2))
                            pe.wait_ge(softmax_step.sem, softmax_step.after((n - 1) * STEPS + SUMMED_AL))
                            pe.transpose(bank(5, P)[0:R, :], pack_al[:, 0:R], ident[:, :]).then_inc(turned.sem, 1)
                            pe.wait_ge(softmax_step.sem, softmax_step.after(n * STEPS + WEIGHTS))
                            pe.wait_ge(w_ready.sem, w_ready.after(n))
                            pe.transpose(bank(6, P), w_r, ident[:, :]).then_inc(w_turned.sem, 1)
                            for h in range(QH):
                                b, q = h % 2, n * QH + h
                                pe.wait_ge(added.sem, added.after((q - 1) * HALF))
                                pe.wait_ge(pieces_kept.sem, pieces_kept.after(q - 1))
                                for j in range(HALF):
                                    if heads > 1:
                                        pe.wait_ge(scaled.sem, scaled.after(q * HALF + j + 1))
                                    pe.wait_ge(onehot_ready.sem, onehot_ready.after(q * HALF + j + 1))
                                    last = pe.matmul(PS[:, (b * HALF + j) * P:(b * HALF + j + 1) * P],
                                                     gt[s][:, h * HALF + j, 0:D], onehot[b * HALF + j], start=True, stop=True)
                                last.then_inc(summed.sem, 1)

                @block.vector
                def _(v):
                    v.memset(same_r[0:R, 0:1], 0.0)
                    v.memset(w_r, 0.0)
                    v.memset(cut_r[0:R, 0:1], -BIG)
                    v.memset(cut_r[0:R, P:P + 1], -BIG)
                    linker(v)(v.memset(F[:, :], 0.0))
                    with v.Fori(0, NBT // 2) as i:
                        for s in range(2):
                            n = i * 2 + s

                            def onehots(h):
                                v.wait_ge(summed.sem, summed.after(n * QH + h - 1))
                                for j in range(h * HALF, (h + 1) * HALF):
                                    w, op = (w_c[:, j:j + 1], ALU.mult) if heads == 1 else (None, ALU.bypass)
                                    v.tensor_scalar(onehot[j % (2 * HALF)], iota_row[:, :], locT[:, bass.ds(n * BT + j, 1)], w,
                                                    ALU.is_equal, op).then_inc(onehot_ready.sem, 1)

                            def scale(h):
                                for j in range(h * HALF, (h + 1) * HALF):
                                    g3 = gt[s][:, j, 0:D].rearrange("p (h d) -> p h d", h=heads)
                                    w3 = heads_of(w_c)[:, :, j:j + 1].broadcast_to([P, heads, D // heads])
                                    v.tensor_tensor(g3, g3, w3, ALU.mult).then_inc(scaled.sem, 1)

                            def add(h):
                                k0 = n * BT + h * HALF
                                _, first_dst = nc.values_load_multi_w_load_instructions(
                                    ebi[0:1, bass.ds(k0, HALF)], engines=[mybir.EngineType.DVE], min_val=0, max_val=NP,
                                    skip_runtime_bounds_check_because="dst holds node numbers")
                                v.wait_ge(pieces_kept.sem, pieces_kept.after(n * QH + h + 1))
                                for j in range(HALF):
                                    cols = F[:, bass.ds(first_dst[j] + 1, P - 2)]
                                    v.wait_ge(added.sem, added.after(k0 + j))
                                    c = (h % 2 * HALF + j) * P
                                    v.tensor_tensor(cols, cols, PS[:, c + 1:c + P - 1], ALU.add).then_inc(added.sem, 1)

                            steps = [0]

                            def step(ins):
                                steps[0] += 1
                                ins.then_inc(softmax_step.sem, 1)
                                v.wait_ge(softmax_step.sem, softmax_step.after(n * STEPS + steps[0]))

                            v.wait_ge(loc_rows.sem, loc_rows.after(n + 1))
                            step(v.tensor_tensor(same_r[0:R, 1:], loc_r[0:R, 1:], loc_r[0:R, :-1], ALU.is_equal))
                            step(v.tensor_scalar(cut_r[0:R, 1:P], same_r[0:R, 1:], -1.0, BIG, ALU.add, ALU.mult))
                            if heads > 1:
                                onehots(0)
                            v.wait_ge(turned.sem, turned.after(2 * n + 2))
                            v.wait_ge(ald_in.sem, ald_in.after((n + 1) * 16))
                            step(v.tensor_tensor(z[0:R, :], bank(5, P)[0:R, :], ald_r[0:R, :], ALU.add))
                            step(v.scalar_tensor_tensor(z[0:R, :], z[0:R, :], SLOPE, z[0:R, :], ALU.mult, ALU.max))
                            step(v.tensor_tensor_scan(t1[0:R, :], cut_r[0:R, 0:P], z[0:R, :], -BIG, ALU.add, ALU.max))
                            v.wait_ge(ends_kept.sem, ends_kept.after(n))
                            step(v.tensor_tensor_scan(m_r[0:R, ::-1], cut_r[0:R, 1:][:, ::-1], t1[0:R, ::-1], -BIG, ALU.add, ALU.max))
                            step(v.tensor_tensor(p_r[0:R, :], z[0:R, :], m_r[0:R, :], ALU.subtract))
                            if heads > 1:
                                onehots(1)
                            v.wait_ge(exped.sem, exped.after(n + 1))
                            step(v.tensor_tensor_scan(t1[0:R, :], same_r[0:R, :], p_r[0:R, :], 0.0, ALU.mult, ALU.add))
                            step(v.tensor_tensor_scan(d_r[0:R, ::-1], cut_r[0:R, 1:][:, ::-1], t1[0:R, ::-1], -BIG, ALU.add, ALU.max))
                            step(v.reciprocal(t1[0:R, :], d_r[0:R, :]))
                            v.wait_ge(w_turned.sem, w_turned.after(n))
                            step(v.tensor_tensor(w_r[0:R, :], p_r[0:R, :], t1[0:R, :], ALU.mult))
                            v.wait_ge(w_ready.sem, w_ready.after(n + 1))
                            if heads > 1:
                                scale(0)
                                scale(1)
                            else:
                                onehots(0)
                                onehots(1)
                            for h in range(2, QH):
                                add(h - 2)
                                onehots(h)
                                if heads > 1:
                                    scale(h)
                            add(QH - 2)
                            add(QH - 1)
            idx_ready.passed(NBT + 1)
            packed.passed(2 * NBT)
            turned.passed(2 * NBT)
            softmax_step.passed(STEPS * NBT)
            for one in (loc_rows, exped, ends_kept, w_turned, w_ready):
                one.passed(NBT)
            summed.passed(NBT * QH)
            pieces_kept.passed(NBT * QH)
            ald_in.passed(16 * NBT)
            if heads > 1:
                loads.passed(16 * (NATTR + 2 * NZERO))
            onehot_ready.passed(K)
            added.passed(K)
            if heads > 1:
                scaled.passed(K)
            for one in half_in:
                one.passed(16 * BT * (NBT // 2))

            WD = 2 * G
            used = [0]
            sq = in_wk(heads * NBT)
            pieces, runs, sums = in_wk(heads * WD), in_wk(heads * WD), in_wk(heads * WD)
            t1, cut, cut_next, carry, crow = (in_wk(w) for w in (WD, WD, WD, 4 * HEADS, 3 * P))
            crow = crow[0:HEADS, :]
            zh = [pieces[:, h * WD:(h + 1) * WD] for h in range(heads)]
            runh = [runs[:, h * WD:(h + 1) * WD] for h in range(heads)]
            in_tiles = lambda a: a.rearrange("p (h g e) -> p h g e", g=G, e=2)
            alone = same_ends[:, :].rearrange("p (g e) -> p g e", e=2)[:, :, 1]
            spread_c = in_wk(2 * K)
            coef = spread_c.rearrange("p (g e c) -> p g e c", e=2, c=P)
            run = spread_c
            weighed, keep_b = hs[:, 0:2 * K], hs[:, 2 * K:4 * K]
            piece_rows = weighed.rearrange("p (m f) -> p m f", f=D)
            whole = [hs[:, 2 * K + b * GW:2 * K + (b + 1) * GW] for b in range(2)]
            with nc.Block() as block:
                @block.sync
                def _(sp):
                    sp.dma_start(keep_b, row(keep_d).broadcast_to([P, 2 * K])).then_inc(loads.sem, 16)
                    for u in range(P // BT):
                        for h in range(heads):
                            sp.dma_start(sq[u * BT:(u + 1) * BT, h * NBT:(h + 1) * NBT].rearrange("j (g w) -> j g w", w=4),
                                         ends[h * BT:(h + 1) * BT, :].rearrange("j (g u w) -> j g u w", u=P // BT, w=4)[:, :, u])\
                                .then_inc(loads.sem, 16)
                    sp.wait_ge(loads.sem, loads.after(16 * (1 + heads * (P // BT))))

                @block.vector
                def _(v):
                    link = linker(v)
                    link(v.tensor_scalar(cut, same_ends[:, :], -1.0, BIG, ALU.add, ALU.mult))
                    link(v.tensor_copy(cut_next[:, 0:WD - 1], cut[:, 1:]))
                    link(v.tensor_scalar(cut_next[:, WD - 1:WD], link_next[:, :], -1.0, BIG, ALU.add, ALU.mult))
                    v.wait_ge(loads.sem, loads.after(16 * (1 + heads * (P // BT))))
                    for h in range(heads):
                        of_w = sq[:, h * NBT:(h + 1) * NBT].rearrange("p (g w e) -> p g w e", w=2, e=2)
                        v.tensor_copy(in_tiles(pieces)[:, h], of_w[:, :, 0])
                        link(v.tensor_copy(in_tiles(sums)[:, h], of_w[:, :, 1]))
                        link(v.tensor_scalar(t1[:, 0:G], alone, -1.0, -1.0, ALU.mult, ALU.subtract))
                        link(v.tensor_tensor(in_tiles(sums)[:, h, :, 1], in_tiles(sums)[:, h, :, 1], t1[:, 0:G], ALU.mult))
            loads.passed(16 * (1 + heads * (P // BT)))

            def carries(v, link, whole, backward, keep_op, keep, none):
                link(v.tensor_copy(carry[:, HEADS:HEADS + heads], whole.broadcast_to([P, heads])))
                v.nop().then_inc(dve_b.sem, 1)
                v.wait_ge(pe_b.sem, pe_b.after(keep["n"] + 1))
                link(v.memset(crow[0:heads, :], none))
                if keep_op == ALU.mult:
                    link(v.tensor_copy(crow[0:heads, 0:P], PS[0:heads, 512:512 + P]))
                else:
                    link(v.tensor_scalar(crow[0:heads, 0:P], PS[0:heads, 512:512 + P], -1.0, BIG, ALU.add, ALU.mult))
                op1 = ALU.add if keep_op == ALU.mult else ALU.max
                if backward:
                    link(v.tensor_tensor_scan(crow[0:heads, P:2 * P][:, ::-1], crow[0:heads, 0:P][:, ::-1],
                                              PS[0:heads, 0:P][:, ::-1], none, keep_op, op1))
                    into = crow[0:heads, P + 1:2 * P + 1]
                else:
                    link(v.tensor_tensor_scan(crow[0:heads, P + 1:2 * P + 1], crow[0:heads, 0:P], PS[0:heads, 0:P],
                                              none, keep_op, op1))
                    into = crow[0:heads, P:2 * P]
                v.nop().then_inc(dve_b.sem, 1)
                v.wait_ge(pe_b.sem, pe_b.after(keep["n"] + 2))
                keep["n"] += 2
                link(v.tensor_copy(carry[:, 0:heads], PS[:, 1024:1024 + heads]))

            def segment_total(kind):
                hold, op0, op1, none = {"max": (cut, ALU.add, ALU.max, -BIG), "sum": (same_ends[:, :], ALU.mult, ALU.add, 0.0)}[kind]
                with nc.Block() as block:
                    @block.tensor
                    def _(pe):
                        for r in range(2):
                            pe.wait_ge(dve_b.sem, dve_b.after(2 * r + 1))
                            for n in range(2):
                                last = pe.transpose(PS[0:heads, n * 512:n * 512 + P], carry[:, n * HEADS:n * HEADS + heads],
                                                    ident[:, :])
                            last.then_inc(pe_b.sem, 1)
                            pe.wait_ge(dve_b.sem, dve_b.after(2 * r + 2))
                            c = P + 1 if r else P
                            pe.transpose(PS[:, 1024:1024 + heads], crow[0:heads, c:c + P], ident[0:heads, 0:heads])\
                                .then_inc(pe_b.sem, 1)

                    @block.vector
                    def _(v):
                        link = linker(v)
                        keep = {"n": 0}
                        link(v.tensor_reduce(carry[:, 2 * HEADS:2 * HEADS + 1], same_ends[:, :], AX_X, ALU.min))
                        link(v.tensor_reduce(carry[:, 2 * HEADS + 1:2 * HEADS + 2], cut_next, AX_X, ALU.min))
                        link(v.tensor_scalar(carry[:, 2 * HEADS + 1:2 * HEADS + 2], carry[:, 2 * HEADS + 1:2 * HEADS + 2],
                                             0.0, None, ALU.is_ge))
                        for h in range(heads):
                            link(v.tensor_tensor_scan(t1, hold, zh[h], none, op0, op1))
                            link(v.tensor_copy(carry[:, h:h + 1], t1[:, WD - 1:WD]))
                        carries(v, link, carry[:, 2 * HEADS:2 * HEADS + 1], False, op0, keep, none)
                        for h in range(heads):
                            link(v.tensor_tensor_scan(runh[h], hold, zh[h], carry[:, h:h + 1], op0, op1))
                        for h in range(heads):
                            link(v.tensor_tensor_scan(t1[:, ::-1], cut_next[:, ::-1], runh[h][:, ::-1], -BIG, ALU.add, ALU.max))
                            link(v.tensor_copy(carry[:, h:h + 1], t1[:, 0:1]))
                        carries(v, link, carry[:, 2 * HEADS + 1:2 * HEADS + 2], True, ALU.add, keep, -BIG)
                        for h in range(heads):
                            link(v.tensor_tensor_scan(runh[h][:, ::-1], cut_next[:, ::-1], runh[h][:, ::-1],
                                                      carry[:, h:h + 1], ALU.add, ALU.max))
                            if kind == "max":
                                link(v.tensor_tensor(zh[h], zh[h], runh[h], ALU.subtract))
                            else:
                                link(v.tensor_scalar(runh[h], runh[h], 1e-16, None, ALU.add))
                                link(v.reciprocal(runh[h], runh[h]))
                                link(v.tensor_tensor(zh[h], zh[h], runh[h], ALU.mult))
                dve_b.passed(4)
                pe_b.passed(4)

            segment_total("max")
            with nc.Block() as block:
                @block.scalar
                def _(act):
                    act.activation(pieces, pieces, ACT.Exp).then_inc(act_a.sem, 1)

                @block.vector
                def _(v):
                    v.wait_ge(act_a.sem, act_a.after(1))
                    v.tensor_tensor(pieces, pieces, sums, ALU.mult)
            act_a.passed(1)
            segment_total("sum")

            with nc.Block() as block:
                @block.tensor
                def _(pe):
                    pe.wait_ge(dve_b.sem, dve_b.after(1))
                    for n in range(2 * G):
                        if n >= 8:
                            pe.wait_ge(dve_c.sem, dve_c.after(n - 7))
                        pe.transpose(bank(n % 8, P), coef[:, n // 2, n % 2], ident[:, :]).then_inc(pe_a.sem, 1)
                    pe.wait_ge(dve_b.sem, dve_b.after(2))
                    for n in range(2 * G):
                        pe.wait_ge(dve_c.sem, dve_c.after(2 * G + n - 7))
                        pe.transpose(bank(n % 8, P), run[:, n * P:(n + 1) * P], ident[:, :]).then_inc(pe_a.sem, 1)

                @block.vector
                def _(v):
                    link = linker(v)
                    for n in range(2 * G):
                        last = v.tensor_copy(coef[:, n // 2, n % 2].rearrange("p (h d) -> p h d", h=heads),
                                             in_tiles(pieces)[:, :, n // 2, n % 2].unsqueeze(2).broadcast_to([P, heads, D // heads]))
                    link(last)
                    v.nop().then_inc(dve_b.sem, 1)
                    for n in range(2 * G):
                        g, e = n // 2, n % 2
                        v.wait_ge(pe_a.sem, pe_a.after(n + 1))
                        v.tensor_tensor(weighed.rearrange("p (t n) -> p t n", n=2 * G)[:, :, n],
                                        kept[:, e * K + g * P:e * K + (g + 1) * P], bank(n % 8, P), ALU.mult).then_inc(dve_c.sem, 1)
                    v.wait_ge(dve_c.sem, dve_c.after(2 * G))
                    v.wait_ge(pe_a.sem, pe_a.after(2 * G))
                    link(v.tensor_tensor_scan(run, keep_b, weighed, 0.0, ALU.mult, ALU.add))
                    v.nop().then_inc(dve_b.sem, 1)
                    for n in range(2 * G):
                        v.wait_ge(pe_a.sem, pe_a.after(2 * G + n + 1))
                        v.tensor_copy(piece_rows[:, n], bank(n % 8, P)).then_inc(dve_c.sem, 1)

                @block.gpsimd
                def _(pool):
                    for n in range(2 * G):
                        pool.wait_ge(dve_c.sem, dve_c.after(2 * G + n + 1))
                        pool.indirect_dma_start(whole_rows, bass.IndirectOffsetOnAxis(piece_idx[:, n:n + 1], 0),
                                                piece_rows[:, n], None).then_inc(spread.sem, 16)
                    pool.wait_ge(spread.sem, spread.after(32 * G))
                    pool.sem_inc(idx_taken.sem, 1)
            dve_b.passed(2)
            dve_c.passed(4 * G)
            pe_a.passed(4 * G)
            spread.passed(32 * G)

            with nc.Block() as block:
                @block.sync
                def _(sp):
                    with sp.Fori(0, NG // 2) as i:
                        for b in range(2):
                            q = i * 2 + b
                            sp.wait_ge(pe_a.sem, pe_a.after(q - 1))
                            sp.dma_start(group(whole[b]), rows_of(whole_rows, q)).then_inc(more_in[b].sem, 16)

                @block.tensor
                def _(pe):
                    with pe.Fori(0, NG // 2) as i:
                        for b in range(2):
                            q = i * 2 + b
                            pe.wait_ge(more_in[b].sem, more_in[b].after(i * 16 + 16))
                            pe.wait_ge(dve_a.sem, dve_a.after(q - 1))
                            for j in range(GRP):
                                last = pe.transpose(tile_of(psA[b], j), tile_of(whole[b], j), ident[:, :])
                            last.then_inc(pe_a.sem, 1)

                @block.vector
                def _(v):
                    with v.Fori(0, NG // 2) as i:
                        for b in range(2):
                            q = i * 2 + b
                            cols = F[:, bass.ds(q * GW, GW)]
                            v.wait_ge(pe_a.sem, pe_a.after(q + 1))
                            v.tensor_tensor(cols, cols, psA[b], ALU.add).then_inc(dve_a.sem, 1)
            pe_a.passed(NG)
            dve_a.passed(NG)
            for b in range(2):
                more_in[b].passed(16 * (NG // 2))

        def load_weights(items, rows=()):
            with nc.Block() as block:
                @block.sync
                def _(sp):
                    for dst, s in items:
                        sp.dma_start(dst, s).then_inc(loads.sem, 16)
                    sp.wait_ge(loads.sem, loads.after(16 * len(items)))
            loads.passed(16 * len(items))

        def attention_columns(w_sb, wt_sb, a_sb, al_sb, heads):
            with nc.Block() as block:
                @block.tensor
                def _(pe):
                    pe.transpose(bank(0, P), w_sb, ident[:, :]).then_inc(pe_a.sem, 1)
                    pe.wait_ge(dve_a.sem, dve_a.after(1))
                    pe.matmul(bank(1, 2 * heads), wt_sb, a_sb, start=True, stop=True).then_inc(pe_a.sem, 1)

                @block.vector
                def _(v):
                    v.wait_ge(pe_a.sem, pe_a.after(1))
                    v.tensor_copy(wt_sb, bank(0, P)).then_inc(dve_a.sem, 1)
                    v.wait_ge(pe_a.sem, pe_a.after(2))
                    v.tensor_copy(al_sb, bank(1, 2 * heads))
            pe_a.passed(2)
            dve_a.passed(1)

        layer_norm(xs, hs, ACT.Relu)
        with nc.Block() as block:
            @block.vector
            def _(v):
                v.memset(W[2][:, 0:2 * HEADS], 0.0).then_inc(dve_a.sem, 1)

            @block.sync
            def _(sp):
                sp.dma_start(W[0], t["L0_gnn_W1"]).then_inc(loads.sem, 16)
                sp.wait_ge(dve_a.sem, dve_a.after(1))
                for n, name in enumerate(("L0_gnn_a_src1", "L0_gnn_a_dst1")):
                    for h in range(HEADS):
                        sp.dma_start(W[2][h * HID:(h + 1) * HID, n * HEADS + h:n * HEADS + h + 1], colv(t[name][h, :])).then_inc(loads.sem, 16)
                sp.wait_ge(loads.sem, loads.after(16 * (1 + 2 * HEADS)))
        dve_a.passed(1)
        loads.passed(16 * (1 + 2 * HEADS))
        attention_columns(W[0], W[1], W[2][:, 0:2 * HEADS], W[3][:, 0:2 * HEADS], HEADS)
        project(W[0], tab_g1, al=W[3][:, 0:2 * HEADS], heads=HEADS, ald_table=ald_rows, ex=ex4)
        if stop <= 2: return
        attention(HEADS, tab_g1, ald_rows, ex4, whole_rows[0])
        if stop <= 4: return
        load_weights([(W[0], t["L0_gnn_W2"]), (W[2][:, 0:1], colv(t["L0_gnn_a_src2"][0, :])),
                      (W[2][:, 1:2], colv(t["L0_gnn_a_dst2"][0, :])), (bcol[:, 0:1], colv(t["L0_gnn_b1"])),
                      (bias_b[0], row(t["L0_gnn_b2"]).broadcast_to([P, D]))])
        attention_columns(W[0], W[1], W[2][:, 0:2], W[3][:, 0:2], 1)
        project(W[0], tab_g2, from_f=True, al=W[3][:, 0:2], heads=1, ald_table=ald_rows1, ex=ex1,
                act_f=dict(func=ACT.Relu, bias=bcol[:, 0:1]))
        attention(1, tab_g2, ald_rows1, ex1, whole_rows[1])
        if stop <= 5: return

        tmp, ex_ = ost, [wk[:, (4 + b) * GW:(5 + b) * GW] for b in range(2)]
        with nc.Block() as block:
            @block.gpsimd
            def _(pool):
                with pool.Fori(0, NG // 2) as i:
                    for b in range(2):
                        q = i * 2 + b
                        pool.wait_ge(pe_a.sem, pe_a.after(q - 1))
                        pool.tensor_copy(hT[b], F[:, bass.ds(q * GW, GW)]).then_inc(brought.sem, 1)

            @block.sync
            def _(sp):
                sp.dma_start(locT[:, :], loc_d).then_inc(loads.sem, 16)
                for a in range(2):
                    sp.dma_start(agg[a].rearrange("(p i) d -> p (i d)", p=P), agg[2].rearrange("(p i) d -> p (i d)", p=P))\
                        .then_inc(loads.sem, 16)
                sp.wait_ge(loads.sem, loads.after(48))

            @block.tensor
            def _(pe):
                with pe.Fori(0, NG // 2) as i:
                    for b in range(2):
                        q = i * 2 + b
                        pe.wait_ge(brought.sem, brought.after(q + 1))
                        pe.wait_ge(dve_a.sem, dve_a.after(q - 1))
                        for j in range(GRP):
                            last = pe.transpose(tile_of(psB[b], j), tile_of(hT[b], j), ident[:, :])
                        last.then_inc(pe_a.sem, 1)

            @block.scalar
            def _(act):
                with act.Fori(0, NG // 2) as i:
                    for b in range(2):
                        q = i * 2 + b
                        act.wait_ge(dve_a.sem, dve_a.after(q + 1))
                        act.activation(ex_[b], tmp[b], ACT.Exp).then_inc(act_a.sem, 1)
                        act.wait_ge(dve_b.sem, dve_b.after(q + 1))
                        act.activation(sm[:, b * NT + GRP:b * NT + 2 * GRP], sm[:, b * NT + 2 * GRP:b * NT + 3 * GRP], ACT.Ln)\
                            .then_inc(act_b.sem, 1)

            @block.vector
            def _(v):
                link = linker(v)
                with v.Fori(0, NG // 2) as i:
                    for b in range(2):
                        q = i * 2 + b
                        mx, lns, ssum = (sm[:, b * NT + n * GRP:b * NT + (n + 1) * GRP] for n in range(3))
                        wide = lambda a: a.unsqueeze(2).broadcast_to([P, GRP, P])
                        v.wait_ge(pe_a.sem, pe_a.after(q + 1))
                        v.tensor_tensor(group(tmp[b]), group(psB[b]), every(bias_b[0]), ALU.add).then_inc(dve_c.sem, 1)
                        v.wait_ge(dve_c.sem, dve_c.after(q * 4 + 1))
                        v.tensor_reduce(mx, group(tmp[b]), AX_X, ALU.max).then_inc(dve_c.sem, 1)
                        v.wait_ge(dve_c.sem, dve_c.after(q * 4 + 2))
                        v.tensor_tensor(group(tmp[b]), group(tmp[b]), wide(mx), ALU.subtract).then_inc(dve_a.sem, 1)
                        if b == 1:
                            row_stats(v, xs, q - 1)
                        v.wait_ge(act_a.sem, act_a.after(q + 1))
                        v.tensor_reduce(ssum, group(ex_[b]), AX_X, ALU.add).then_inc(dve_b.sem, 1)
                        v.wait_ge(act_b.sem, act_b.after(q + 1))
                        v.wait_ge(dve_a.sem, dve_a.after(q + 1))
                        v.tensor_tensor(group(tmp[b]), group(tmp[b]), wide(lns), ALU.subtract).then_inc(dve_c.sem, 1)
                        v.wait_ge(dve_c.sem, dve_c.after(q * 4 + 3))
                        xg = xs[:, bass.ds(q * GW, GW)]
                        v.tensor_tensor(xg, xg, tmp[b], ALU.add).then_inc(dve_c.sem, 1)
                        v.wait_ge(dve_c.sem, dve_c.after(q * 4 + 4))
                        if b == 1:
                            row_stats(v, xs, q)
        for s in (dve_a, act_a, act_b, dve_b, pe_a, brought):
            s.passed(NG)
        dve_c.passed(4 * NG)
        loads.passed(48)
        if stop <= 6: return

        layer_norm(xs, hs, ACT.Relu, have_stats=True)
        QT = 4
        NQ = K // QT
        place = [0]

        def in_f(width, dt=F32):
            a = F[:, place[0]:place[0] + width]
            place[0] += width
            return a.bitcast(dt) if dt != F32 else a

        QW = QT * P
        two = lambda width, dt=F32: [in_f(width, dt) for _ in range(2)]
        a_rows, b_win, src_rows, loc_rows, attrs = two(QW), two(QW), two(QW, I32), two(QW), two(P)
        ohT, eq, attrT, h1, z2, msg, msum = two(QW), two(QW), two(P), two(QW), two(QW), two(QW), two(QW)
        seen, dups, delta, picks = in_f(QW), two(QT), two(QT), two(QT)
        wc = [in_f(P) for _ in range(QT)]
        sidx = two(QT, I32)
        trash = in_f(1)
        with nc.Block() as block:
            @block.vector
            def _(v):
                for w_ in wc + attrs:
                    last = v.memset(w_, 0.0)
                last.then_inc(dve_a.sem, 1)
                v.tensor_scalar(trash, pcol[:, :], float(NP), None, ALU.add)

            @block.sync
            def _(sp):
                for dst, s in ((W[0], t["L1_gnn_eW1"][0:D, :]), (W[1], t["L1_gnn_eW1"][D:2 * D, :]),
                               (W[2], t["L1_gnn_eW2"]), (bias_b[0], row(t["L1_gnn_eb1"]).broadcast_to([P, D])),
                               (bias_b[1], row(t["L1_gnn_eb2"]).broadcast_to([P, D]))):
                    sp.dma_start(dst, s).then_inc(loads.sem, 16)
                sp.wait_ge(dve_a.sem, dve_a.after(1))
                for u in range(QT):
                    sp.dma_start(wc[u][16 * u:16 * (u + 1), :], t["L1_gnn_eW1"][2 * D:, :]).then_inc(loads.sem, 16)
                sp.wait_ge(loads.sem, loads.after(16 * (5 + QT)))
        dve_a.passed(1)
        loads.passed(16 * (5 + QT))
        project(W[0], tab, bias=bias_b[0])
        project(W[1], tab_b)

        src_by_row, loc_by_row = (a.rearrange("(p g) c -> g p c", g=G) for a in (src_d, loc_rows_d))
        attr_by_row = attr_d.rearrange("(p g c) d -> g c p d", g=G, c=P)
        with nc.Block() as block:
            @block.sync
            def _(sp):
                with sp.Fori(0, G) as g:
                    with sp.Fori(0, P // (2 * QT)) as r:
                        i = g * (P // (2 * QT)) + r
                        _, first_dst = nc.values_load_multi_w_load_instructions(
                            ebi[0:1, bass.ds(i * (2 * QT), 2 * QT)], engines=[mybir.EngineType.SP], min_val=0, max_val=NP,
                            skip_runtime_bounds_check_because="dst holds node numbers")
                        for b in range(2):
                            n = i * 2 + b
                            p0 = r * (2 * QT) + b * QT
                            sp.wait_ge(q_made.sem, q_made.after((n - 1) * QT))
                            sp.dma_start(src_rows[b].rearrange("p (u c) -> p u c", u=QT),
                                         src_by_row[bass.ds(g, 1), bass.ds(p0, QT), :].broadcast_to([P, QT, P]))\
                                .then_inc(more_in[2 + b].sem, 16)
                            sp.wait_ge(onehot_ready.sem, onehot_ready.after(n - 1))
                            sp.dma_start(loc_rows[b].rearrange("p (u c) -> p u c", u=QT),
                                         loc_by_row[bass.ds(g, 1), bass.ds(p0, QT), :].broadcast_to([P, QT, P]))\
                                .then_inc(more_in[2 + b].sem, 16)
                            sp.wait_ge(pe_t.sem, pe_t.after(n - 1))
                            sp.dma_start(attrs[b][:, 0:QT * 16].rearrange("c (u d) -> c u d", u=QT),
                                         attr_by_row[bass.ds(g, 1), :, bass.ds(p0, QT), :].rearrange("g c p d -> (g c) p d"))\
                                .then_inc(more_in[2 + b].sem, 16)
                            sp.wait_ge(pe_z.sem, pe_z.after(n - 1))
                            for u in range(QT):
                                sp.dma_start(tile_of(b_win[b], u), tab_b[bass.ds(first_dst[b * QT + u], P), :])\
                                    .then_inc(more_in[b].sem, 16)

            @block.gpsimd
            def _(pool):
                def gather(n, b):
                    pool.wait_ge(idx_ready.sem, idx_ready.after(n + 1))
                    pool.sem_inc(idx_taken.sem, 1)
                    for u in range(QT):
                        pool.indirect_dma_start(tile_of(a_rows[b], u), None, tab,
                                                bass.IndirectOffsetOnAxis(idx[:, b * QT + u:b * QT + u + 1], 0))\
                            .then_inc(gathered[b * QT + u].sem, 16)

                def scatter(n, b):
                    pool.wait_ge(msum_ready.sem, msum_ready.after(n + 1))
                    pool.wait_ge(sidx_ready.sem, sidx_ready.after(n + 1))
                    for u in range(QT):
                        pool.wait_ge(scattered[u].sem, scattered[u].after(n * 16))
                        pool.sem_inc(idx_taken.sem, 1)
                        pool.indirect_dma_start(agg[u], bass.IndirectOffsetOnAxis(sidx[b][:, u:u + 1], 0),
                                                tile_of(msum[b], u), None, compute_op=ALU.add).then_inc(scattered[u].sem, 16)

                gather(0, 0)
                gather(1, 1)
                with pool.Fori(0, NQ // 2 - 1) as i:
                    for b in range(2):
                        gather(i * 2 + b + 2, b)
                        scatter(i * 2 + b, b)
                scatter(NQ - 2, 0)
                scatter(NQ - 1, 1)
                for u in range(QT):
                    pool.wait_ge(scattered[u].sem, scattered[u].after(NQ * 16))

            def steps(eng, step):
                step(0, 0, 0)
                with eng.Fori(0, NQ // 2 - 1) as i:
                    step(i * 2 + 1, 1, i)
                    step(i * 2 + 2, 0, i + 1)
                step(NQ - 1, 1, NQ // 2 - 1)
                step(NQ, 0, NQ // 2)

            inside = lambda n: not isinstance(n, int) or n < NQ
            behind = lambda n: not isinstance(n, int) or n > 0

            @block.tensor
            def _(pe):
                def step(n, b, h):
                    if inside(n):
                        pe.wait_ge(more_in[2 + b].sem, more_in[2 + b].after((h + 1) * 48))
                        pe.wait_ge(attrT_ready.sem, attrT_ready.after(n))
                        pe.transpose(bank(7, P), attrs[b], ident[:, :]).then_inc(pe_t.sem, 1)
                    if behind(n):
                        pe.wait_ge(h1_ready.sem, h1_ready.after(n))
                        pe.wait_ge(z2_ready.sem, z2_ready.after(n - 2))
                        for u in range(QT):
                            last = pe.matmul(tile_of(bank(5 - b), u), tile_of(h1[1 - b], u), W[2], start=True, stop=True)
                        last.then_inc(pe_m.sem, 1)
                    if inside(n):
                        pe.wait_ge(attrT_ready.sem, attrT_ready.after(n + 1))
                        pe.wait_ge(onehot_ready.sem, onehot_ready.after(n + 1))
                        pe.wait_ge(more_in[b].sem, more_in[b].after((h + 1) * (16 * QT)))
                        pe.wait_ge(h1_ready.sem, h1_ready.after(n - 1))
                        for u in range(QT):
                            pe.wait_ge(gathered[b * QT + u].sem, gathered[b * QT + u].after((h + 1) * 16))
                            z = tile_of(bank(2 + b), u)
                            pe.matmul(z, tile_of(a_rows[b], u), ident[:, :], start=True, stop=False)
                            pe.matmul(z, wc[u][0:QT * 16, :], attrT[b][0:QT * 16, :], start=False, stop=False)
                            last = pe.matmul(z, tile_of(b_win[b], u), tile_of(ohT[b], u), start=False, stop=True)
                        last.then_inc(pe_z.sem, 1)
                    if behind(n):
                        pe.wait_ge(msg_ready.sem, msg_ready.after(n))
                        pe.wait_ge(q_made.sem, q_made.after(n * QT))
                        pe.wait_ge(msum_ready.sem, msum_ready.after(n - 1))
                        for u in range(QT):
                            last = pe.matmul(tile_of(bank(6), u), tile_of(eq[1 - b], u), tile_of(msg[1 - b], u),
                                             start=True, stop=True)
                        last.then_inc(pe_d.sem, 1)
                steps(pe, step)

            @block.scalar
            def _(act):
                def take(n, b):
                    act.wait_ge(pe_z.sem, pe_z.after(n - 1))
                    act.copy(idx[:, b * QT:(b + 1) * QT], srcT[:, bass.ds(n * QT, QT)]).then_inc(idx_ready.sem, 1)

                def step(n, b, h):
                    if isinstance(n, int) and n == 0:
                        take(0, 0)
                        take(1, 1)
                    elif not isinstance(n, int):
                        take(n + 1, 1 - b)
                    if inside(n):
                        act.wait_ge(pe_t.sem, pe_t.after(n + 1))
                        act.wait_ge(pe_z.sem, pe_z.after(n - 1))
                        act.copy(attrT[b][0:QT * 16, :], PS[0:QT * 16, 7 * 512:7 * 512 + P]).then_inc(attrT_ready.sem, 1)
                    if behind(n):
                        act.wait_ge(z2_ready.sem, z2_ready.after(n))
                        act.wait_ge(pe_d.sem, pe_d.after(n - 2))
                        act.activation(msg[1 - b], z2[1 - b], ACT.Silu).then_inc(msg_ready.sem, 1)
                    if inside(n):
                        act.wait_ge(pe_z.sem, pe_z.after(n + 1))
                        act.wait_ge(pe_m.sem, pe_m.after(n - 1))
                        act.activation(h1[b], bank(2 + b), ACT.Silu).then_inc(h1_ready.sem, 1)
                steps(act, step)

            @block.vector
            def _(v):
                def step(n, b, h):
                    if inside(n):
                        v.wait_ge(more_in[2 + b].sem, more_in[2 + b].after((h + 1) * 48))
                        v.wait_ge(pe_z.sem, pe_z.after(n - 1))
                        v.tensor_scalar(ohT[b], loc_rows[b], pcol[:, 0:1], None, ALU.is_equal).then_inc(onehot_ready.sem, 1)
                    if behind(n):
                        v.wait_ge(pe_m.sem, pe_m.after(n))
                        v.wait_ge(msg_ready.sem, msg_ready.after(n - 2))
                        v.tensor_tensor(z2[1 - b].rearrange("p (u f) -> p u f", f=P), bank(5 - b).rearrange("p (u f) -> p u f", f=P),
                                        every(bias_b[1], QT), ALU.add).then_inc(z2_ready.sem, 1)
                    if inside(n):
                        v.wait_ge(pe_d.sem, pe_d.after(n - 1))
                        for u in range(QT):
                            v.tensor_scalar(tile_of(eq[b], u), tile_of(src_rows[b], u), srcT[:, bass.ds(n * QT + u, 1)], None,
                                            ALU.is_equal).then_inc(q_made.sem, 1)
                        v.tensor_scalar(delta[b], srcT[:, bass.ds(n * QT, QT)], trash, None, ALU.subtract)
                        for u in range(QT):
                            v.wait_ge(q_made.sem, q_made.after(n * QT + u + 1))
                            v.scalar_tensor_tensor(tile_of(seen, u), tile_of(eq[b], u), 1.0, lower[:, :], ALU.mult, ALU.mult,
                                                   accum_out=dups[b][:, u:u + 1]).then_inc(dups_made.sem, 1)
                        v.wait_ge(dups_made.sem, dups_made.after((n + 1) * QT))
                        v.scalar_tensor_tensor(picks[b], dups[b], 0.0, delta[b], ALU.is_equal, ALU.mult).then_inc(picked_rows.sem, 1)
                    if behind(n):
                        v.wait_ge(pe_d.sem, pe_d.after(n))
                        v.tensor_copy(msum[1 - b], bank(6)).then_inc(msum_ready.sem, 1)
                    if inside(n):
                        v.wait_ge(picked_rows.sem, picked_rows.after(n + 1))
                        if behind(n):
                            for u in range(QT):
                                v.wait_ge(scattered[u].sem, scattered[u].after((n - 1) * 16))
                        v.tensor_scalar(sidx[b], picks[b], trash, None, ALU.add).then_inc(sidx_ready.sem, 1)
                steps(v, step)
        for s in (pe_t, pe_m, pe_z, pe_d, attrT_ready, z2_ready, h1_ready, msg_ready, msum_ready, sidx_ready, picked_rows, onehot_ready,
                  idx_ready):
            s.passed(NQ)
        for s in (q_made, dups_made):
            s.passed(NQ * QT)
        for s in gathered[0:2 * QT]:
            s.passed(16 * (NQ // 2))
        for s in more_in[0:2]:
            s.passed(16 * QT * (NQ // 2))
        for s in more_in[2:4]:
            s.passed(48 * (NQ // 2))
        if stop <= 7: return

        load_weights([(W[0], t["L1_gnn_nW1"][0:D, :]), (W[1], t["L1_gnn_nW1"][D:2 * D, :]), (W[2], t["L1_gnn_nW2"]),
                      (bcol[:, 0:1], colv(t["L1_gnn_nb1"])), (bias_b[0], row(t["L1_gnn_nb2"]).broadcast_to([P, D]))])
        place[0] = 0
        parts_in = [[in_f(GW) for a in range(AGG)] for b in range(2)]
        aT, uT = two(GW), two(GW)
        with nc.Block() as block:
            @block.sync
            def _(sp):
                with sp.Fori(0, NG // 2) as i:
                    for b in range(2):
                        q = i * 2 + b
                        sp.wait_ge(pe_t.sem, pe_t.after(q - 1))
                        for a in range(AGG):
                            sp.dma_start(group(parts_in[b][a]), rows_of(agg[a], q)).then_inc(more_in[b].sem, 16)

            @block.gpsimd
            def _(pool):
                with pool.Fori(0, NG) as q:
                    pool.wait_ge(pe_a.sem, pe_a.after(q))
                    pool.tensor_copy(stage, hs[:, bass.ds(q * GW, GW)]).then_inc(brought.sem, 1)

            @block.vector
            def _(v):
                with v.Fori(0, NG // 2) as i:
                    for b in range(2):
                        q = i * 2 + b
                        v.wait_ge(more_in[b].sem, more_in[b].after((i + 1) * (16 * AGG)))
                        total = parts_in[b][0]
                        for a in range(1, AGG):
                            v.tensor_tensor(total, total, parts_in[b][a], ALU.add).then_inc(dve_a.sem, 1)
                            v.wait_ge(dve_a.sem, dve_a.after(q * (AGG - 1) + a))
                        xg = xs[:, bass.ds(q * GW, GW)]
                        v.tensor_tensor(xg, xg, hs[:, bass.ds(q * GW, GW)], ALU.add).then_inc(dve_b.sem, 1)
                        v.wait_ge(dve_b.sem, dve_b.after(q * 2 + 1))
                        v.tensor_tensor(group(xg), group(xg), every(bias_b[0]), ALU.add).then_inc(dve_b.sem, 1)
                        if b == 1:
                            row_stats(v, xs, q - 1)
                        v.wait_ge(pe_c.sem, pe_c.after(q + 1))
                        v.wait_ge(dve_b.sem, dve_b.after(q * 2 + 2))
                        v.tensor_tensor(xg, xg, psB[b], ALU.add).then_inc(dve_c.sem, 1)
                        v.wait_ge(dve_c.sem, dve_c.after(q + 1))
                        if b == 1:
                            row_stats(v, xs, q)

            @block.tensor
            def _(pe):
                with pe.Fori(0, NG // 2) as i:
                    for b in range(2):
                        q = i * 2 + b
                        pe.wait_ge(brought.sem, brought.after(q + 1))
                        pe.wait_ge(act_b.sem, act_b.after(q - 1))
                        for j in range(GRP):
                            last = pe.transpose(tile_of(psA[b], j), tile_of(stage, j), ident[:, :])
                        last.then_inc(pe_a.sem, 1)
                        pe.wait_ge(dve_a.sem, dve_a.after((q + 1) * (AGG - 1)))
                        pe.wait_ge(dve_c.sem, dve_c.after(q - 1))
                        for j in range(GRP):
                            last = pe.transpose(tile_of(psB[b], j), tile_of(parts_in[b][0], j), ident[:, :])
                        last.then_inc(pe_t.sem, 1)
                        pe.wait_ge(act_a.sem, act_a.after(q * 2 + 2))
                        for a, z in ((0, 512), (512, GW)):
                            pe.matmul(psA[b][:, a:z], W[0], hT[b][:, a:z], start=True, stop=False)
                            last = pe.matmul(psA[b][:, a:z], W[1], aT[b][:, a:z], start=False, stop=True)
                        last.then_inc(pe_b.sem, 1)
                        pe.wait_ge(act_b.sem, act_b.after(q + 1))
                        for j in range(GRP):
                            last = pe.matmul(tile_of(psB[b], j), tile_of(uT[b], j), W[2], start=True, stop=True)
                        last.then_inc(pe_c.sem, 1)

            @block.scalar
            def _(act):
                with act.Fori(0, NG // 2) as i:
                    for b in range(2):
                        q = i * 2 + b
                        act.wait_ge(pe_b.sem, pe_b.after(q - 1))
                        act.wait_ge(pe_a.sem, pe_a.after(q + 1))
                        act.copy(hT[b], psA[b]).then_inc(act_a.sem, 1)
                        act.wait_ge(pe_t.sem, pe_t.after(q + 1))
                        act.copy(aT[b], psB[b]).then_inc(act_a.sem, 1)
                        act.wait_ge(pe_b.sem, pe_b.after(q + 1))
                        act.wait_ge(pe_c.sem, pe_c.after(q - 1))
                        act.activation(uT[b], psA[b], ACT.Silu, bias=bcol[:, 0:1]).then_inc(act_b.sem, 1)
        for s in (pe_a, pe_t, pe_b, pe_c, brought, dve_c, act_b):
            s.passed(NG)
        dve_b.passed(2 * NG)
        act_a.passed(2 * NG)
        dve_a.passed((AGG - 1) * NG)
        for s in more_in[0:2]:
            s.passed(16 * AGG * (NG // 2))
        if stop <= 8: return

        def batch_norm():
            half = GW // 2
            tail = N - (2 * NG - 1) * half
            bst = wk[:, 5 * GW:5 * GW + 12 * NG]
            mv, am, cm = bcol[:, 4:6], bcol[:, 6:7], bcol[:, 7:8]
            db2 = [wk[:, (2 + b) * GW:(3 + b) * GW] for b in range(2)]
            with nc.Block() as block:
                @block.sync
                def _(sp):
                    with sp.Fori(0, NG // 2) as i:
                        for b in range(2):
                            q = i * 2 + b
                            sp.wait_ge(dve_a.sem, dve_a.after(q - 1))
                            sp.dma_start(db2[b], row(dinv_d[bass.ds(q * GW, GW)]).broadcast_to([P, GW])).then_inc(more_in[b].sem, 16)

                @block.scalar
                def _(act):
                    with act.Fori(0, NG) as q:
                        act.wait_ge(dve_a.sem, dve_a.after(q + 1))
                        fg = F[:, bass.ds(q * GW, GW)]
                        act.activation(fg, fg, ACT.Identity, bias=bcol[:, 0:1]).then_inc(act_a.sem, 1)
                    act.wait_ge(dve_b.sem, dve_b.after(1))
                    act.activation(am, am, ACT.Sqrt).then_inc(act_b.sem, 1)

                @block.vector
                def _(v):
                    link = linker(v)
                    with v.Fori(0, NG // 2) as i:
                        for b in range(2):
                            q = i * 2 + b
                            fg = F[:, bass.ds(q * GW, GW)]
                            v.wait_ge(more_in[b].sem, more_in[b].after((i + 1) * 16))
                            v.tensor_tensor(fg, fg, db2[b], ALU.mult).then_inc(dve_a.sem, 1)
                    for q in range(NG):
                        v.wait_ge(act_a.sem, act_a.after(q + 1))
                        for n in range(2 * q, 2 * q + 2):
                            w = half if n < 2 * NG - 1 else tail
                            last = v.bn_stats(bst[:, 6 * n:6 * n + 6], F[:, n * half:n * half + w])
                    link(last)
                    link(v.bn_aggr(mv, bst))
                    link(v.tensor_scalar(am, mv[:, 1:2], EPS, None, ALU.add))
                    v.nop().then_inc(dve_b.sem, 1)
                    v.wait_ge(act_b.sem, act_b.after(1))
                    link(v.reciprocal(am, am))
                    link(v.tensor_tensor(am, am, bcol[:, 1:2], ALU.mult))
                    link(v.tensor_tensor(cm, mv[:, 0:1], am, ALU.mult))
                    v.tensor_tensor(cm, bcol[:, 2:3], cm, ALU.subtract)
            act_a.passed(NG)
            act_b.passed(1)
            dve_a.passed(NG)
            dve_b.passed(1)
            for s in more_in[0:2]:
                s.passed(16 * (NG // 2))

        layer_norm(xs, hs, ACT.Relu, have_stats=True)
        for n, from_f in (("1", False), ("2", True)):
            load_weights([(W[0], t["L2_gnn_W" + n])] +
                         [(bcol[:, m:m + 1], colv(t["L2_gnn_" + name + n])) for m, name in enumerate(("b", "g", "be"))])
            project(W[0], tab, from_f=from_f, scale=True, init_f=True,
                    act_f=dict(func=ACT.Relu, bias=bcol[:, 7:8], scale=bcol[:, 6:7]) if from_f else None)
            aggregate(tab)
            batch_norm()
        load_weights([(W[0], t["L2_gnn_Wf"]), (bias_b[0], row(t["L2_gnn_bf"]).broadcast_to([P, D]))])
        with nc.Block() as block:
            @block.scalar
            def _(act):
                bring(act, F, hT, pe_a, func=ACT.Relu, bias=bcol[:, 7:8], scale=bcol[:, 6:7])

            @block.tensor
            def _(pe):
                with pe.Fori(0, NG // 2) as i:
                    for b in range(2):
                        q = i * 2 + b
                        pe.wait_ge(brought.sem, brought.after(q + 1))
                        pe.wait_ge(dve_a.sem, dve_a.after(q - 1))
                        for j in range(GRP):
                            last = pe.matmul(tile_of(psB[b], j), tile_of(hT[b], j), W[0], start=True, stop=True)
                        last.then_inc(pe_a.sem, 1)

            @block.vector
            def _(v):
                with v.Fori(0, NG // 2) as i:
                    for b in range(2):
                        q = i * 2 + b
                        if b == 1:
                            row_stats(v, xs, q - 1)
                        v.wait_ge(pe_a.sem, pe_a.after(q + 1))
                        xg = xs[:, bass.ds(q * GW, GW)]
                        v.tensor_tensor(xg, xg, psB[b], ALU.add).then_inc(dve_a.sem, 1)
                        v.wait_ge(dve_a.sem, dve_a.after(q + 1))
                        v.tensor_tensor(group(xg), group(xg), every(bias_b[0]), ALU.add).then_inc(dve_b.sem, 1)
                        v.wait_ge(dve_b.sem, dve_b.after(q + 1))
                        if b == 1:
                            row_stats(v, xs, q)
        for s in (brought, pe_a, dve_a, dve_b):
            s.passed(NG)
        if stop <= 9: return

        layer_norm(xs, hs, ACT.Relu, have_stats=True)
        layer_norm(hs, hs, ACT.Identity)
        load_weights([(W[0], t["L3_gnn_W_self"]), (W[1], t["L3_gnn_W_neigh"]), (bias_b[0], row(t["L3_gnn_b"]).broadcast_to([P, D])),
                      (W[2], row(t["L3_gnn_gamma"]).broadcast_to([P, D])), (W[3], row(t["L3_gnn_beta"]).broadcast_to([P, D]))])
        with nc.Block() as block:
            @block.vector
            def _(v):
                with v.Fori(0, NG) as q:
                    hg = group(hs[:, bass.ds(q * GW, GW)])
                    v.tensor_tensor(hg, hg, every(W[2]), ALU.mult).then_inc(dve_a.sem, 1)
                    v.wait_ge(dve_a.sem, dve_a.after(q + 1))
                    v.tensor_tensor(hg, hg, every(W[3]), ALU.add).then_inc(dve_b.sem, 1)

            @block.sync
            def _(sp):
                with sp.Fori(0, NG) as q:
                    sp.wait_ge(dve_b.sem, dve_b.after(q + 1))
                    sp.dma_start(rows_of(tab, q), group(hs[:, bass.ds(q * GW, GW)])).then_inc(stores.sem, 16)
                sp.wait_ge(stores.sem, stores.after(16 * NG))
        dve_a.passed(NG)
        dve_b.passed(NG)
        stores.passed(16 * NG)
        aggregate(tab, clear=True)

        fT = [wk[:, (4 + b) * GW:(5 + b) * GW] for b in range(2)]
        with nc.Block() as block:
            @block.tensor
            def _(pe):
                with pe.Fori(0, NG // 2) as i:
                    for b in range(2):
                        q = i * 2 + b
                        pe.wait_ge(brought.sem, brought.after(q * 2 + 1))
                        pe.wait_ge(dve_a.sem, dve_a.after(q - 1))
                        for j in range(GRP):
                            last = pe.transpose(tile_of(psA[b], j), tile_of(ost[b], j), ident[:, :])
                        last.then_inc(pe_a.sem, 1)
                        pe.wait_ge(act_a.sem, act_a.after(q + 1))
                        pe.wait_ge(brought.sem, brought.after(q * 2 + 2))
                        pe.wait_ge(dve_c.sem, dve_c.after(q - 1))
                        for j in range(GRP):
                            pe.matmul(tile_of(psB[b], j), tile_of(hT[b], j), W[0], start=True, stop=True)
                        for j in range(GRP):
                            last = pe.matmul(tile_of(psA[b], j), tile_of(fT[b], j), W[1], start=True, stop=True)
                        last.then_inc(pe_b.sem, 1)

            @block.scalar
            def _(act):
                with act.Fori(0, NG // 2) as i:
                    for b in range(2):
                        q = i * 2 + b
                        act.wait_ge(pe_a.sem, pe_a.after(q - 1))
                        act.copy(ost[b], hs[:, bass.ds(q * GW, GW)]).then_inc(brought.sem, 1)
                        act.wait_ge(pe_b.sem, pe_b.after(q - 1))
                        act.copy(fT[b], F[:, bass.ds(q * GW, GW)]).then_inc(brought.sem, 1)
                        act.wait_ge(pe_a.sem, pe_a.after(q + 1))
                        act.copy(hT[b], psA[b]).then_inc(act_a.sem, 1)

            @block.vector
            def _(v):
                with v.Fori(0, NG // 2) as i:
                    for b in range(2):
                        q = i * 2 + b
                        v.wait_ge(pe_b.sem, pe_b.after(q + 1))
                        r3 = rdeg[:, bass.ds(q * GRP, GRP)].unsqueeze(2).broadcast_to([P, GRP, P])
                        xg = xs[:, bass.ds(q * GW, GW)]
                        fg = F[:, bass.ds(q * GW, GW)]
                        v.tensor_tensor(group(fg), group(psA[b]), r3, ALU.mult).then_inc(dve_a.sem, 1)
                        v.tensor_tensor(xg, xg, psB[b], ALU.add).then_inc(dve_c.sem, 1)
                        v.wait_ge(dve_a.sem, dve_a.after(q + 1))
                        v.wait_ge(dve_c.sem, dve_c.after(q + 1))
                        v.tensor_tensor(xg, xg, fg, ALU.add).then_inc(dve_b.sem, 1)
                        v.wait_ge(dve_b.sem, dve_b.after(q * 2 + 1))
                        v.tensor_tensor(group(xg), group(xg), every(bias_b[0]), ALU.add).then_inc(dve_b.sem, 1)

            @block.sync
            def _(sp):
                with sp.Fori(0, NG - 1) as q:
                    sp.wait_ge(dve_b.sem, dve_b.after(q * 2 + 2))
                    sp.dma_start(rows_of(out, q), group(xs[:, bass.ds(q * GW, GW)])).then_inc(stores.sem, 16)
                sp.wait_ge(dve_b.sem, dve_b.after(2 * NG))
                c = (NG - 1) * GW
                sp.dma_start(out[c:c + (GRP - 1) * P, :].rearrange("(i p) f -> p i f", p=P),
                             group(xs[:, c:c + (GRP - 1) * P])).then_inc(stores.sem, 16)
                sp.dma_start(out[(NT - 1) * P:N, :], xs[0:N - (NT - 1) * P, (NT - 1) * P:]).then_inc(stores.sem, 16)
                sp.wait_ge(stores.sem, stores.after(16 * (NG + 1)))


_FIELDS = ["x", "src", "dst", "edge_attr_16",
           "L0_gnn_W1", "L0_gnn_a_src1", "L0_gnn_a_dst1", "L0_gnn_b1", "L0_gnn_W2", "L0_gnn_a_src2", "L0_gnn_a_dst2",
           "L0_gnn_b2", "L1_gnn_eW1", "L1_gnn_eb1", "L1_gnn_eW2", "L1_gnn_eb2", "L1_gnn_nW1", "L1_gnn_nb1", "L1_gnn_nW2",
           "L1_gnn_nb2", "L2_gnn_W1", "L2_gnn_b1", "L2_gnn_g1", "L2_gnn_be1", "L2_gnn_W2", "L2_gnn_b2", "L2_gnn_g2",
           "L2_gnn_be2", "L2_gnn_Wf", "L2_gnn_bf", "L3_gnn_gamma", "L3_gnn_beta", "L3_gnn_W_self", "L3_gnn_W_neigh",
           "L3_gnn_b"]


def kernel(**inputs):
    import numpy as np
    import concourse.bacc as bacc
    from concourse.bass_utils import run_bass_kernel_spmd

    nc = bacc.Bacc("TRN2", target_bir_lowering=False, num_devices=1)
    arrays, t = {}, {}
    for name in _FIELDS:
        a = np.ascontiguousarray(inputs[name])
        arrays[f"in_{name}_dram"] = a
        t[name] = nc.dram_tensor(f"in_{name}_dram", a.shape, mybir.dt.from_np(a.dtype), kind="ExternalInput").ap()
    out = nc.dram_tensor("out_0_dram", (N, D), F32, kind="ExternalOutput").ap()
    build(nc, t, out)
    r = run_bass_kernel_spmd(nc, [arrays], core_ids=[0])
    return r.results[0]["out_0_dram"]
```
